# Optimizing a Trainium2 kernel written in Bass

```python
import numpy as np
import jax
import jax.numpy as jnp

def _softmax(x, axis=-1):
    return jax.nn.softmax(x, axis=axis)

def _gelu(x):
    return jax.nn.gelu(x, approximate=True)

def _silu(x):
    return jax.nn.silu(x)

def _sigmoid(x):
    return jax.nn.sigmoid(x)

def _layernorm(x, axis=-1, eps=1e-05):
    m = jnp.mean(x, axis=axis, keepdims=True)
    v = jnp.var(x, axis=axis, keepdims=True)
    return (x - m) / jnp.sqrt(v + eps)

def _scatter_add(tgt, idx, src, axis=0):
    return tgt.at[idx].add(src)

def _segment_sum(src, seg, n):
    return jax.ops.segment_sum(src, seg, n)
kernel_name = 'mk_hybrid_d1_jaxref_r8_85cd35'

def setup_inputs(seed: int=0):
    np.random.seed(seed)
    _w = jnp.asarray

    def _L0_attn_a_setup():
        import jax, jax.numpy as jnp
        import numpy as np
        B, T, C = (4, 512, 128)
        H = 16
        D = C // H
        EPS = 1e-06

        def _phi(x):
            return jax.nn.elu(x) + 1.0
        key = jax.random.key(seed)
        k1, k2, k3 = jax.random.split(key, 3)
        x = jax.random.normal(k1, (B, T, C), dtype=jnp.float32)
        Wqkv = jax.random.normal(k2, (3 * C, C), dtype=jnp.float32) * (1.0 / np.sqrt(C))
        Wproj = jax.random.normal(k3, (C, C), dtype=jnp.float32) * (1.0 / np.sqrt(C))
        bproj = jnp.zeros((C,), dtype=jnp.float32)
        return {'x': x, 'Wqkv': Wqkv, 'Wproj': Wproj, 'bproj': bproj}
    _L0_attn_a_in = _L0_attn_a_setup()

    def _L0_attn_b_setup():
        import jax, jax.numpy as jnp
        import numpy as np
        B, L, D, H, K = (8, 256, 128, 16, 31)
        D_CONV = D // H
        EPS = 1e-06
        key = jax.random.key(seed)
        ks = jax.random.split(key, 5)
        return {'x': jax.random.normal(ks[0], (B, L, D), dtype=jnp.float32), 'W_pe': jax.random.normal(ks[1], (D_CONV, 2 * K), dtype=jnp.float32) * 0.1, 'b_pe': jnp.zeros((2 * K,), dtype=jnp.float32), 'stt_energy': jnp.ones((1, H, 1, K), dtype=jnp.float32) + 0.02 * jax.random.normal(ks[2], (1, H, 1, K), dtype=jnp.float32), 'W_fc': jax.random.normal(ks[3], (D, D), dtype=jnp.float32) / jnp.sqrt(jnp.float32(D)), 'gamma': jnp.ones((D,), dtype=jnp.float32), 'beta': jnp.zeros((D,), dtype=jnp.float32)}
    _L0_attn_b_in = _L0_attn_b_setup()

    def _L0_ffn_setup():
        import math
        import jax, jax.numpy as jnp
        import numpy as np
        D_MODEL = 128
        D_FF = 512
        E = 8
        K = 2
        CAP_FACTOR = 1.25
        CLAMP = 10000.0
        LN_EPS = 1e-05
        B, S = (2, 256)
        key = jax.random.key(seed)
        ks = jax.random.split(key, 6)
        b12 = math.sqrt(6.0 / (D_MODEL + 2 * D_FF))
        b3 = math.sqrt(6.0 / (D_FF + D_MODEL))
        br = 0.02 * math.sqrt(3.0)
        return {'x': jax.random.normal(ks[0], (B, S, D_MODEL), dtype=jnp.float32), 'ln_gamma': jnp.ones((D_MODEL,), jnp.float32), 'ln_beta': jnp.zeros((D_MODEL,), jnp.float32), 'router_w': jax.random.uniform(ks[1], (E, D_MODEL), jnp.float32, -br, br), 'w12': jax.random.uniform(ks[2], (E, 2 * D_FF, D_MODEL), jnp.float32, -b12, b12), 'w3': jax.random.uniform(ks[3], (E, D_MODEL, D_FF), jnp.float32, -b3, b3)}
    _L0_ffn_in = _L0_ffn_setup()
    _d = {'L0_attn_a_x': _L0_attn_a_in['x'], 'L0_attn_a_Wqkv': _L0_attn_a_in['Wqkv'], 'L0_attn_a_Wproj': _L0_attn_a_in['Wproj'], 'L0_attn_a_bproj': _L0_attn_a_in['bproj'], 'L0_attn_b_W_pe': _L0_attn_b_in['W_pe'], 'L0_attn_b_b_pe': _L0_attn_b_in['b_pe'], 'L0_attn_b_stt_energy': _L0_attn_b_in['stt_energy'], 'L0_attn_b_W_fc': _L0_attn_b_in['W_fc'], 'L0_attn_b_gamma': _L0_attn_b_in['gamma'], 'L0_attn_b_beta': _L0_attn_b_in['beta'], 'L0_ffn_ln_gamma': _L0_ffn_in['ln_gamma'], 'L0_ffn_ln_beta': _L0_ffn_in['ln_beta'], 'L0_ffn_router_w': _L0_ffn_in['router_w'], 'L0_ffn_w12': _L0_ffn_in['w12'], 'L0_ffn_w3': _L0_ffn_in['w3']}
    _x0 = _d['L0_attn_a_x']
    _d['L0_attn_a_x'] = jax.random.normal(jax.random.fold_in(jax.random.key(seed), 1), (2, 2048, 128), dtype=_x0.dtype)
    del _x0
    return _d

def reference(L0_attn_a_x, L0_attn_a_Wqkv, L0_attn_a_Wproj, L0_attn_a_bproj, L0_attn_b_W_pe, L0_attn_b_b_pe, L0_attn_b_stt_energy, L0_attn_b_W_fc, L0_attn_b_gamma, L0_attn_b_beta, L0_ffn_ln_gamma, L0_ffn_ln_beta, L0_ffn_router_w, L0_ffn_w12, L0_ffn_w3):

    def _L0_attn_a_ref(x, Wqkv, Wproj, bproj):
        import jax, jax.numpy as jnp
        import numpy as np
        B, T, C = (4, 512, 128)
        H = 16
        D = C // H
        EPS = 1e-06

        def _phi(x):
            return jax.nn.elu(x) + 1.0
        b, t, c = x.shape
        qkv = jnp.einsum('btc,ec->bte', x, Wqkv)
        qkv = qkv.reshape(b, t, 3, H, D)
        q, k, v = (qkv[:, :, 0], qkv[:, :, 1], qkv[:, :, 2])
        q = _phi(q)
        k = _phi(k)
        kv = jnp.einsum('bnhd,bnhm->bhdm', k, v)
        k_sum = k.sum(axis=1)
        out = jnp.einsum('bnhd,bhdm->bnhm', q, kv)
        normalizer = jnp.einsum('bnhd,bhd->bnh', q, k_sum) + EPS
        out = out / normalizer[..., None]
        out = out.reshape(b, t, c)
        out = jnp.einsum('btc,oc->bto', out, Wproj) + bproj
        return out

    def _L0_attn_b_ref(x, W_pe, b_pe, stt_energy, W_fc, gamma, beta):
        import jax, jax.numpy as jnp
        import numpy as np
        B, L, D, H, K = (8, 256, 128, 16, 31)
        D_CONV = D // H
        EPS = 1e-06
        b, l, d_model = x.shape
        d = d_model // H
        residual = x
        avg = jnp.cumsum(x, axis=1) / jnp.arange(1, l + 1, dtype=x.dtype)[None, :, None]
        ci = avg.reshape(b, l, H, d).transpose(0, 2, 1, 3).reshape(b * H, l, d)
        pc = ci @ W_pe + b_pe
        dyn, gate = (pc[..., :K], pc[..., K:])
        stt = jnp.broadcast_to(stt_energy, (b, H, 1, K)).reshape(b * H, 1, K)
        energy = stt + jax.nn.sigmoid(gate) * dyn
        w = jax.nn.softmax(energy, axis=-1)
        t_idx = jnp.arange(l)[:, None]
        k_idx = jnp.arange(K)[None, :]
        w = jnp.where(t_idx + k_idx - (K - 1) >= 0, w, jnp.zeros((), x.dtype))
        padded = jnp.pad(ci, ((0, 0), (K - 1, 0), (0, 0)))
        out = jnp.zeros((b * H, l, d), dtype=x.dtype)
        for kk in range(K):
            out = out + w[:, :, kk:kk + 1] * padded[:, kk:kk + l, :]
        conv_loc = out.reshape(b, H, l, d).transpose(0, 2, 1, 3).reshape(b, l, d_model)
        v = conv_loc @ W_fc.T + residual
        mu = jnp.mean(v, axis=-1, keepdims=True)
        var = jnp.var(v, axis=-1, keepdims=True)
        v = (v - mu) / jnp.sqrt(var + EPS) * gamma + beta
        return v

    def _L0_ffn_ref(x, ln_gamma, ln_beta, router_w, w12, w3):
        import math
        import jax, jax.numpy as jnp
        import numpy as np
        D_MODEL = 128
        D_FF = 512
        E = 8
        K = 2
        CAP_FACTOR = 1.25
        CLAMP = 10000.0
        LN_EPS = 1e-05
        B, S = (2, 256)
        Bq, Sq, D = x.shape
        T = Bq * Sq
        mu = jnp.mean(x, axis=-1, keepdims=True)
        var = jnp.mean(jnp.square(x - mu), axis=-1, keepdims=True)
        xn = (x - mu) * jax.lax.rsqrt(var + LN_EPS) * ln_gamma + ln_beta
        xf = xn.reshape(T, D)
        logits = jnp.clip(xf @ router_w.T, -CLAMP, CLAMP)
        top_v, top_i = jax.lax.top_k(logits, K)
        m = jnp.max(top_v, axis=-1, keepdims=True)
        ev = jnp.exp(top_v - m)
        top_p = ev / (jnp.sum(ev, axis=-1, keepdims=True) + 1e-12)
        Stot = T * K
        experts = top_i.reshape(-1)
        weights = top_p.reshape(-1)
        tokens = jnp.repeat(jnp.arange(T), K)
        oh = (experts[:, None] == jnp.arange(E)[None, :]).astype(jnp.int32)
        pos = jnp.take_along_axis(jnp.cumsum(oh, axis=0) - 1, experts[:, None], axis=1)[:, 0]
        C = max(1, math.ceil(T * K * CAP_FACTOR / E))
        kept = pos < C
        slot = jnp.where(kept, experts * C + pos, E * C)
        buf = jnp.zeros((E * C + 1, D), x.dtype).at[slot].set(xf[tokens])
        xb = buf[:E * C].reshape(E, C, D)
        gu = jnp.einsum('ecd,efd->ecf', xb, w12)
        g, u = jnp.split(gu, 2, axis=-1)
        h = jax.nn.silu(g) * u
        yb = jnp.einsum('ecf,edf->ecd', h, w3).reshape(E * C, D)
        ys = yb[jnp.minimum(slot, E * C - 1)] * (weights * kept.astype(weights.dtype))[:, None]
        out = jnp.zeros((T, D), x.dtype).at[tokens].add(ys)
        return out.reshape(Bq, Sq, D)
    x = L0_attn_a_x
    x = x + _L0_attn_a_ref(_layernorm(x, axis=-1), L0_attn_a_Wqkv, L0_attn_a_Wproj, L0_attn_a_bproj)
    x = x + _L0_ffn_ref(_layernorm(x, axis=-1), L0_ffn_ln_gamma, L0_ffn_ln_beta, L0_ffn_router_w, L0_ffn_w12, L0_ffn_w3)
    x = x + _L0_attn_b_ref(_layernorm(x, axis=-1), L0_attn_b_W_pe, L0_attn_b_b_pe, L0_attn_b_stt_energy, L0_attn_b_W_fc, L0_attn_b_gamma, L0_attn_b_beta)
    x = x + _L0_ffn_ref(_layernorm(x, axis=-1), L0_ffn_ln_gamma, L0_ffn_ln_beta, L0_ffn_router_w, L0_ffn_w12, L0_ffn_w3)
    return x

_drawn_inputs = setup_inputs


def setup_inputs(seed=0):
    import zlib

    import numpy as np

    out = dict(_drawn_inputs(seed))
    spreads = {'L0_attn_a_bproj': (0.0, 0.1),
     'L0_attn_b_b_pe': (0.0, 0.1),
     'L0_attn_b_gamma': (1.0, 0.2),
     'L0_attn_b_beta': (0.0, 0.1),
     'L0_ffn_ln_gamma': (1.0, 0.2),
     'L0_ffn_ln_beta': (0.0, 0.1)}
    factors = {}
    for name, (base, spread) in spreads.items():
        noise = np.random.default_rng([zlib.crc32(name.encode()), seed]).standard_normal(out[name].shape)
        drawn = base * np.exp(spread * noise) if base else spread * noise
        out[name] = jnp.asarray(drawn.astype(out[name].dtype))
    for name, factor in factors.items():
        out[name] = (out[name] * factor).astype(out[name].dtype)
    return out
```

```python
import concourse.bass as bass
from concourse import mybir
from contextlib import ExitStack

P = 128
SEED = 8


def hybrid_block(nc, x, wqkvT, wprojT, bproj, wpe, bpe, stt, wfcT, gammaB, betaB,
                 gammaF, betaF, routerT, w12T, w3T, out):
    fp32, bf16, u32 = mybir.dt.float32, mybir.dt.bfloat16, mybir.dt.uint32
    ALU = mybir.AluOpType
    ACT = mybir.ActivationFunctionType
    AX = mybir.AxisListType

    B, T, C = x.shape
    E = w12T.shape[0]
    F = w3T.shape[2] * P
    H, D = 16, 8
    K = 31
    KP = 32
    NT = B * T // P
    GT = 4
    GPB = T // (GT * P)
    NG = B * GPB
    GN = GT * P
    TOPK = 2
    CAP = -(-B * T * TOPK * 5 // (4 * E))
    SLOTS = E * CAP
    CT = CAP // P
    CH = 2
    NC = CT // CH
    FT = F // P
    HALO = K - 1
    PADROW = HALO + T + 2
    FAR = 65536.0
    LN_EPS, ATT_EPS, CONV_EPS, CLAMP = 1e-5, 1e-6, 1e-6, 10000.0

    slots_in = nc.dram_tensor("slots_in", (SLOTS, C), fp32, kind="Internal").ap()
    slots_out = nc.dram_tensor("slots_out", (SLOTS, C), fp32, kind="Internal").ap()
    ci_pad = nc.dram_tensor("ci_pad", (C, B, PADROW), fp32, kind="Internal").ap()

    x_v = x.rearrange("b (t p) c -> p (b t) c", p=P)
    out_v = out.rearrange("b (t p) c -> p (b t) c", p=P)
    slots_in_v = slots_in.rearrange("(e t p) c -> e p t c", p=P, e=E)
    slots_out_v = slots_out.rearrange("(e t p) c -> e p t c", p=P, e=E)

    with ExitStack() as ctx:
        def sb(name, shape, dt=fp32):
            return ctx.enter_context(nc.sbuf_tensor(name, shape, dt))

        def sem(name):
            return ctx.enter_context(nc.semaphore(name))

        def two(name, shape, dt=fp32):
            return [sb(f"{name}{n}", shape, dt) for n in range(2)]

        ident = sb("ident", [P, P])
        before = sb("before", [P, P], bf16)
        ones = sb("ones", [P, GN], bf16)
        ones_f = sb("ones_f", [P, GN])
        same_head = sb("same_head", [P, H])
        mod_head = sb("mod_head", [P, H])
        pick = sb("pick", [P, 2, 32])
        spread = sb("spread", [P, D, H])
        inv_count = sb("inv_count", [P, T])
        minus_half = sb("minus_half", [P, GT])
        iota_e = sb("iota_e", [P, E])
        wqkv_sb = sb("wqkv_sb", [P, 3 * C])
        wproj_sb = sb("wproj_sb", [P, C])
        bproj_sb = sb("bproj_sb", [P, C])
        wpe_sb = sb("wpe_sb", [P, 2 * K])
        gate_w = sb("gate_w", [P, KP, H])
        dyn_w = sb("dyn_w", [P, KP, H])
        bpe_sb = sb("bpe_sb", [P, 2, KP, H])
        bpe_hi = sb("bpe_hi", [P, 2, KP, H], bf16)
        bpe_parts = sb("bpe_parts", [P, 2, KP, H], bf16)
        stt_sb = sb("stt_sb", [P, KP, H])
        wfc_sb = sb("wfc_sb", [P, C])
        gammaB_sb, betaB_sb = sb("gammaB_sb", [P, C]), sb("betaB_sb", [P, C])
        gammaF_sb, betaF_sb = sb("gammaF_sb", [P, C]), sb("betaF_sb", [P, C])
        router_sb = sb("router_sb", [P, E])

        X = sb("X", [P, NT, C])
        gather_at = sb("gather_at", [P, NT, TOPK], u32)
        route_w = sb("route_w", [P, NT, TOPK])

        stats = sb("stats", [P, GT, 6])
        mv = sb("mv", [P, GT, 2])
        var_eps = two("var_eps", [P, GT])
        rstd = two("rstd", [P, GT])

        arena = sb("arena", [P, 10240])

        arena_w = sb("arena_w", [P, 4096])

        def carve(arena):
            at = [0]

            def take(name, shape):
                n = 1
                for size in shape[1:]:
                    n *= size
                part = arena[0:shape[0], at[0]:at[0] + n]
                at[0] += n
                if len(shape) == 3:
                    part = part.rearrange("p (a b) -> p a b", a=shape[1])
                if len(shape) == 4:
                    part = part.rearrange("p (a b c) -> p a b c", a=shape[1], b=shape[2])
                return part
            return take, lambda name, shape: [take(name, shape) for _ in range(2)]

        att_sb, att_two = carve(arena)
        conv_sb, conv_two = carve(arena)
        _, hid_two = carve(arena_w)
        _, prod_two = carve(arena_w)
        zeros = arena_w[:, 0:CT * C]
        xn = att_two("xn", [P, GT, C])
        xnT = att_two("xnT", [P, GN])
        q_neg, q_exp = att_sb("q_neg", [P, GN]), att_sb("q_exp", [P, GN])
        k_neg, k_exp = att_sb("k_neg", [P, GN]), att_sb("k_exp", [P, GN])
        q_phi = att_sb("q_phi", [P, GPB, GN])
        k_phi = att_two("k_phi", [P, GN])
        v_one = att_two("v_one", [P, GT, C + 1])
        kv_norm = att_sb("kv_norm", [P, 2, H, D])
        norm_r = att_sb("norm_r", [P, GN])
        attT = att_two("attT", [P, GN])

        x_hat = sb("x_hat", [P, GT, C])
        x_gam = two("x_gam", [P, GT, C])
        xf = two("xf", [P, GT, C])
        xfT = two("xfT", [P, GN])
        logits = sb("logits", [P, GT, E])
        top = sb("top", [P, GT, 8])
        top_i = sb("top_i", [P, GT, 8], u32)
        expert = sb("expert", [P, GT, TOPK])
        onehot = sb("onehot", [P, GT, TOPK, E])
        hits = two("hits", [P, GT, E], bf16)
        hit_sum = sb("hit_sum", [P, E])
        hits_before = two("hits_before", [P, E], bf16)
        gap = sb("gap", [P, GT])
        e_gap = sb("e_gap", [P, GT])
        masked = sb("masked", [P, GT, TOPK, E])
        pos = sb("pos", [P, GT, TOPK])
        kept = sb("kept", [P, GT, TOPK])
        far = sb("far", [P, GT, TOPK])
        slot = sb("slot", [P, GT, TOPK])
        scatter_at = two("scatter_at", [P, GT * TOPK], u32)
        den = sb("den", [P, GT])
        prob = sb("prob", [P, GT, TOPK])

        w12_sb = two("w12_sb", [P, 2 * F])
        w3_sb = two("w3_sb", [P, FT, C])
        xb = two("xb", [P, CT, C])
        xbT = hid_two("xbT", [P, CH * P])
        silu_g = hid_two("silu_g", [P, 2, CH * P])
        hid = hid_two("hid", [P, FT, CH * P])
        yb = two("yb", [P, CT, C])

        gather_idx = two("gather_idx", [P, GT * TOPK], u32)
        y_got = two("y_got", [P, GT * TOPK, C])
        w_got = sb("w_got", [P, GT, TOPK])

        z = two("z", [P, GT, C])
        cum = two("cum", [P, GN])
        ci = two("ci", [P, GN])
        taps = two("taps", [P, D, GN + 24])
        th = conv_two("th", [P, KP, H])
        gated = conv_two("gated", [P, KP, H])
        energy = conv_two("energy", [P, KP, H])
        e_max = two("e_max", [P, H])
        e_sub = conv_two("e_sub", [P, KP, H])
        eT = conv_two("eT", [P, 4, GN])
        prod = prod_two("prod", [P, 4, GN])
        z_inv = conv_sb("z_inv", [P, GN])
        convT = conv_sb("convT", [P, GN])
        v_sb = conv_sb("v_sb", [P, GT, C])
        v_hat = conv_sb("v_hat", [P, GT, C])

        bank = [ctx.enter_context(nc.psum_tensor(f"bank{n}", [P, 512], fp32)) for n in range(8)]

        s = {n: sem(n) for n in (
            "zero_rows", "x_in0", "x_in1", "w_in", "consts_pool", "consts", "chain",
            "var_a", "rstd_a", "xn_ready", "xnT_ready", "xnT_copied", "q_ready", "k_ready", "v_ready",
            "q_negs", "k_negs", "q_exps", "k_exps", "v_copied", "q_done", "k_done", "kv_added",
            "kv_ready", "on_ready", "att_ready", "proj_ready", "x_attended",
            "var_r", "rstd_r", "gam_ready", "xf_ready", "xfT_ready", "xfT_copied", "logits_ready",
            "hits_ready", "gap_ready", "gap_exp", "pos_ready", "scatter_ready", "routed",
            "xbT_ready", "xbT_copied", "g_ready", "u_ready", "silu_ready", "hid_ready",
            "y_ready", "y_copied",
            "idx_copied", "combined", "stored",
            "var_z", "rstd_z", "z_ready", "zT_ready", "ci_ready",
            "gate_ready", "dyn_ready", "tanh_ready", "gated_ready", "energy_ready", "max_ready",
            "sub_ready", "eT_ready", "exp_ready", "prod_ready", "prod_added", "norm_ready",
            "conv_ready", "v_out", "var_v", "rstd_v", "x_convolved")}
        scattered = [sem(f"scattered{n}") for n in range(2)]
        gathered = [sem(f"gathered{n}") for n in range(2)]
        w_loaded = [sem(f"w_loaded{n}") for n in range(2)]
        xb_loaded = [sem(f"xb_loaded{n}") for n in range(2)]
        yb_stored = [sem(f"yb_stored{n}") for n in range(2)]
        ci_stored = [sem(f"ci_stored{n}") for n in range(2)]
        taps_loaded = [sem(f"taps_loaded{n}") for n in range(2)]

        def wait_alone(eng, semaphore, value):
            value = eng.lower_val(value)
            eng.wait_ge(s["consts_pool"], 1)
            eng.wait_ge(semaphore, value)

        def wait(eng, semaphore, value):
            eng.wait_ge(semaphore, value)

        def seed(eng, *names):
            for n in names:
                eng.sem_inc(s[n], SEED)

        def grp(i, q, r=0):
            return i * GPB + (q + 1 + NG * r + SEED)

        def half(i, q, r, per, start=SEED):
            return i * (16 * per * GPB // 2) + 16 * per * (q // 2 + 1 + NG // 2 * r + start)

        def rows_moved(i, q, r):
            return half(i, q, r, GT * TOPK, 0)

        def tile(i, q, j):
            return i * (GPB * GT) + (GT * q + j + 1 + SEED)

        def eighth(i, q, o):
            return i * (GPB * 8) + (8 * q + o + 1 + SEED)

        def chunk(i, b, c, r):
            return i * (2 * NC) + (b * NC + c + 1 + E * NC * r + SEED)

        def unit(i, b, c, f, r):
            return i * (4 * NC) + (2 * (b * NC + c) + f + 1 + 2 * E * NC * r + SEED)

        def by_pair(i, r, per):
            return i * (16 * per) + 16 * per * (1 + E // 2 * r + SEED)

        def tiles_of(t, i, q):
            return t[:, bass.ds(i * (GPB * GT) + GT * q, GT)]

        def tile_of(t, i, q, j):
            return t[:, bass.ds(i * (GPB * GT) + (GT * q + j), 1)].squeeze(1)

        def over(t, axis, n):
            t = t.unsqueeze(axis)
            shape = list(t.shape)
            shape[axis] = n
            return t.to_broadcast(shape)

        block = ctx.enter_context(nc.Block())

        @block.sync
        def _(eng):
            for m in (yb_stored, w_loaded, xb_loaded, ci_stored, taps_loaded):
                for n in range(2):
                    eng.sem_inc(m[n], 16 * SEED * {id(w_loaded): 2, id(taps_loaded): 8}.get(id(m), 1))
            for b in range(B):
                eng.dma_start(X[:, b * NT // B:(b + 1) * NT // B, :],
                              x_v[:, b * NT // B:(b + 1) * NT // B, :]).then_inc(s[f"x_in{b}"], 16)
                if b == 0:
                    for dst, src in ((wqkv_sb, wqkvT), (wproj_sb, wprojT), (bproj_sb, bproj),
                                     (router_sb, routerT), (gammaF_sb, gammaF), (betaF_sb, betaF)):
                        eng.dma_start(dst[:, :], src).then_inc(s["w_in"], 16)
            for dst, src in ((wpe_sb, wpe), (wfc_sb, wfcT), (gammaB_sb, gammaB), (betaB_sb, betaB)):
                eng.dma_start(dst[:, :], src).then_inc(s["w_in"], 16)
            eng.wait_ge(s["consts_pool"], 1)
            for part in range(2):
                eng.dma_start(bpe_sb[:, part, 0:K, :].rearrange("p k h -> p (k h)"), bpe[:, part]).then_inc(s["w_in"], 16)
            eng.dma_start(stt_sb[:, 0:K, :].rearrange("p k h -> p (k h)"), stt).then_inc(s["w_in"], 16)
            for e in range(E):
                eng.dma_start(slots_in_v[e], zeros.rearrange("p (t c) -> p t c", c=C))\
                   .then_inc(s["zero_rows"], 16)
            for b in range(B):
                eng.dma_start(ci_pad[:, b, 0:HALO], zeros[:, 0:HALO]).then_inc(s["zero_rows"], 16)

            def expert_io(r):
                eng.wait_ge(s["zero_rows"], 16 * (E + B))
                for n in range(2):
                    eng.wait_ge(scattered[n], rows_moved(B - 1, GPB - 2 + n, r))
                with eng.Fori(0, E // 2) as i:
                    for b in range(2):
                        wait_alone(eng, s["y_ready"], chunk(i, b, NC - 1, r) - 2 * NC)
                        e = i * 2 + b
                        eng.dma_start(xb[b][:, :, :], slots_in_v[bass.ds(e, 1)].squeeze(0)).then_inc(xb_loaded[b], 16)
                        eng.dma_start(w12_sb[b][:, :], w12T[bass.ds(e, 1)].squeeze(0)).then_inc(w_loaded[b], 16)
                        eng.dma_start(w3_sb[b][:, :, :], w3T[bass.ds(e, 1)].squeeze(0)).then_inc(w_loaded[b], 16)
                        if b == 1:
                            store(i, 0, r)
                    store(i, 1, r)

            def store(i, b, r):
                wait_alone(eng, s["y_copied"], chunk(i, b, NC - 1, r))
                eng.dma_start(slots_out_v[bass.ds(i * 2 + b, 1)].squeeze(0), yb[b][:, :, :]).then_inc(yb_stored[b], 16)

            expert_io(0)

            with eng.Fori(0, B) as i:
                for q in range(GPB):
                    p = q % 2
                    wait_alone(eng, s["ci_ready"], grp(i, q))
                    eng.dma_start(ci_pad[:, bass.ds(i, 1), HALO + GN * q:HALO + GN * (q + 1)].squeeze(1), ci[p][:, :])\
                       .then_inc(ci_stored[p], 16)
                    wait_alone(eng, ci_stored[p], half(i, q, 0, 1))
                    eng.wait_ge(s["prod_ready"], eighth(i, q, 7) - 16)
                    for k in range(8):
                        n = GN + 24 - (k == 7)
                        src = ci_pad.rearrange("(h d) b t -> h d b t", d=D)
                        eng.dma_start(taps[p][H * k:H * (k + 1), :, 0:n],
                                      src[:, :, bass.ds(i, 1), GN * q + k:GN * q + k + n].squeeze(2))\
                           .then_inc(taps_loaded[p], 16)

            expert_io(1)
            with eng.Fori(0, B) as i:
                for q in range(GPB):
                    wait_alone(eng, s["combined"], grp(i, q, 1))
                    eng.dma_start(tiles_of(out_v, i, q), tiles_of(X, i, q)).then_inc(s["stored"], 16)
            eng.wait_ge(s["stored"], 16 * NG)

        @block.gpsimd
        def _(eng):
            seed(eng, "rstd_a", "rstd_r", "xf_ready", "idx_copied", "rstd_z", "energy_ready",
                 "sub_ready", "rstd_v")
            eng.memset(zeros, 0.0)
            eng.memset(bpe_sb[:, :, :, :], 0.0)
            eng.memset(stt_sb[:, :, :], -1e30).then_inc(s["consts_pool"], 1)
            eng.memset(ident[:, :], 0.0)
            eng.memset(before[:, :], 1.0)
            eng.memset(ones[:, :], 1.0)
            eng.memset(ones_f[:, :], 1.0)
            eng.memset(minus_half[:, :], -0.5)
            for n in range(2):
                eng.memset(v_one[n][:, :, C:C + 1], 1.0)
            eng.memset(hits_before[0][:, :], 0.0)
            eng.memset(bpe_parts[:, :, :, :], 0.0)
            eng.memset(gate_w[:, :, :], 0.0)
            eng.memset(dyn_w[:, :, :], 0.0)
            eng.memset(pick[:, :, :], 0.0)
            for n in range(2):
                eng.memset(taps[n][:, :, :], 0.0)
            eng.iota(inv_count[:, :], pattern=[[1, T]], base=1, channel_multiplier=0,
                     allow_small_or_imprecise_dtypes=True)
            eng.iota(iota_e[:, :], pattern=[[1, E]], base=0, channel_multiplier=0,
                     allow_small_or_imprecise_dtypes=True).then_inc(s["consts_pool"], 1)
            eng.wait_ge(s["consts_pool"], 2)
            eng.affine_select(out=ident[:, :], in_=ident[:, :], compare_op=ALU.not_equal, fill=1.0,
                              base=0, pattern=[[-1, P]], channel_multiplier=1)
            eng.affine_select(out=before[:, :], in_=before[:, :], compare_op=ALU.is_gt, fill=0.0,
                              base=0, pattern=[[1, P]], channel_multiplier=-1).then_inc(s["consts_pool"], 1)

            def rsqrt(var, to, v, q):
                eng.wait_ge(s[var], v)
                eng.tensor_tensor(rstd[q % 2][:, :], var_eps[q % 2][:, :], minus_half[:, :],
                                  ALU.pow).then_inc(s[to], 1)

            def route(i, q, r):
                p = q % 2
                rsqrt("var_r", "rstd_r", grp(i, q, r), q)
                eng.wait_ge(s["gam_ready"], grp(i, q, r))
                if q >= 2:
                    eng.wait_ge(scattered[p], rows_moved(i, q - 2, r))
                eng.wait_ge(s["xfT_ready"], grp(i, q, r) - 2)
                eng.tensor_tensor(xf[p][:, :, :], x_gam[p][:, :, :], over(betaF_sb[:, :], 1, GT),
                                  ALU.add).then_inc(s["xf_ready"], 1)
                if q == 0:
                    eng.wait_ge(s["zero_rows"], 16 * (E + B))
                wait_alone(eng, s["xf_ready"], grp(i, q, r))
                eng.wait_ge(s["scatter_ready"], grp(i, q, r))
                for n in range(GT * TOPK):
                    eng.indirect_dma_start(
                        slots_in, bass.IndirectOffsetOnAxis(scatter_at[p][:, n:n + 1], 0),
                        xf[p][:, n // TOPK, :], None, bounds_check=SLOTS - 1,
                        oob_is_err=False).then_inc(scattered[p], 16)

            def settle(i, r):
                for n in range(2):
                    eng.wait_ge(scattered[n], rows_moved(i, GPB - 2 + n, r))

            def gather(i, q, r):
                p = q % 2
                eng.wait_ge(s["combined"], grp(i, q, r) - 2)
                eng.wait_ge(s["routed"], grp(i, q, r))
                eng.tensor_copy(gather_idx[p][:, :].rearrange("p (j k) -> p j k", k=TOPK),
                                tiles_of(gather_at, i, q)).then_inc(s["idx_copied"], 1)
                wait_alone(eng, s["idx_copied"], grp(i, q, r))
                for n in range(GT * TOPK):
                    eng.indirect_dma_start(
                        y_got[p][:, n, :], None, slots_out,
                        bass.IndirectOffsetOnAxis(gather_idx[p][:, n:n + 1], 0)).then_inc(gathered[p], 16)

            with eng.Fori(0, B) as i:
                for q in range(GPB):
                    rsqrt("var_a", "rstd_a", grp(i, q), q)
                for q in range(GPB):
                    route(i, q, 0)
                settle(i, 0)

            for n in range(2):
                eng.wait_ge(yb_stored[n], by_pair(E // 2 - 1, 0, 1))

            def conv_norms(i, q):
                rsqrt("var_z", "rstd_z", grp(i, q), q)

            def softmax(i, q):
                def add(j):
                    eng.wait_ge(s["gated_ready"], tile(i, q, j))
                    eng.wait_ge(s["max_ready"], tile(i, q, j) - 2)
                    eng.tensor_tensor(energy[j % 2][:, :, :], gated[j % 2][:, :, :], stt_sb[:, :, :],
                                      ALU.add).then_inc(s["energy_ready"], 1)

                def sub(j):
                    eng.wait_ge(s["max_ready"], tile(i, q, j))
                    eng.wait_ge(s["eT_ready"], tile(i, q, j) - 2)
                    eng.tensor_tensor(e_sub[j % 2][:, :, :], energy[j % 2][:, :, :],
                                      over(e_max[j % 2][:, :], 1, KP), ALU.subtract).then_inc(s["sub_ready"], 1)
                add(0)
                for j in range(1, GT):
                    add(j)
                    sub(j - 1)
                sub(GT - 1)

            with eng.Fori(0, B) as i:
                for q in range(GPB):
                    gather(i, q, 0)
                    conv_norms(i, q)
                    softmax(i, q)
                    rsqrt("var_v", "rstd_v", grp(i, q), q)
                    route(i, q, 1)
                settle(i, 1)

            for n in range(2):
                eng.wait_ge(yb_stored[n], by_pair(E // 2 - 1, 1, 1))
            with eng.Fori(0, B) as i:
                for q in range(GPB):
                    gather(i, q, 1)

        @block.scalar
        def _(eng):
            seed(eng, "xnT_copied", "q_exps", "k_exps", "v_copied", "xfT_copied", "gap_exp",
                 "xbT_copied", "silu_ready", "tanh_ready", "exp_ready")

            def attention(i, q):
                p = q % 2
                eng.wait_ge(s["xnT_ready"], grp(i, q))
                eng.wait_ge(s["v_ready"], grp(i, q) - 2)
                eng.activation(xnT[p][:, :], bank[7][:, :], ACT.Copy).then_inc(s["xnT_copied"], 1)
                eng.wait_ge(s["q_negs"], grp(i, q))
                eng.wait_ge(s["q_done"], grp(i, q) - 1)
                eng.activation(q_exp[:, :], q_neg[:, :], ACT.Exp).then_inc(s["q_exps"], 1)
                eng.wait_ge(s["k_negs"], grp(i, q))
                eng.wait_ge(s["k_done"], grp(i, q) - 1)
                eng.activation(k_exp[:, :], k_neg[:, :], ACT.Exp).then_inc(s["k_exps"], 1)
                eng.wait_ge(s["v_ready"], grp(i, q))
                eng.wait_ge(s["kv_added"], grp(i, q) - 2)
                eng.activation(v_one[p][:, :, 0:C], bank[2][:, :].rearrange("p (j c) -> p j c", c=C),
                               ACT.Copy).then_inc(s["v_copied"], 1)

            def route(i, q, r):
                p, bk = q % 2, bank[3] if r == 0 else bank[6]
                eng.wait_ge(s["xfT_ready"], grp(i, q, r))
                eng.wait_ge(s["logits_ready"], grp(i, q, r) - 2)
                eng.activation(xfT[p][:, :], bk[:, :], ACT.Copy).then_inc(s["xfT_copied"], 1)
                eng.wait_ge(s["gap_ready"], grp(i, q, r))
                eng.wait_ge(s["routed"], grp(i, q, r) - 1)
                eng.activation(e_gap[:, :], gap[:, :], ACT.Exp).then_inc(s["gap_exp"], 1)

            def experts(r):
                with eng.Fori(0, E // 2) as i:
                    for b in range(2):
                        for c in range(NC):
                            q = (NC * b + c) % 2
                            eng.wait_ge(s["xbT_ready"], chunk(i, b, c, r))
                            eng.wait_ge(s["u_ready"], unit(i, b, c, 1, r) - 4)
                            eng.activation(xbT[q][:, :], bank[q][:, 0:CH * P], ACT.Copy)\
                               .then_inc(s["xbT_copied"], 1)
                            for f in range(2):
                                eng.wait_ge(s["g_ready"], unit(i, b, c, f, r))
                                eng.wait_ge(s["hid_ready"], unit(i, b, c, f, r) - 2)
                                eng.activation(silu_g[f][:, :, :], bank[2 + f][:, :].rearrange("p (a n) -> p a n", a=2),
                                               ACT.Silu).then_inc(s["silu_ready"], 1)

            eng.wait_ge(s["consts"], 1)
            with eng.Fori(0, B) as i:
                for q in range(GPB):
                    attention(i, q)
                for q in range(GPB):
                    route(i, q, 0)
            experts(0)

            def softmax(i, q):
                p = q % 2

                def tanh(j):
                    eng.wait_ge(s["gate_ready"], tile(i, q, j))
                    eng.wait_ge(s["gated_ready"], tile(i, q, j) - 2)
                    eng.activation(th[j % 2][:, :, :], bank[j % 2][:, :].rearrange("p (k h) -> p k h", h=H),
                                   ACT.Tanh, scale=0.5).then_inc(s["tanh_ready"], 1)

                def exp(j):
                    eng.wait_ge(s["eT_ready"], tile(i, q, j))
                    if j == 0:
                        eng.wait_ge(s["prod_ready"], eighth(i, q, 7) - 16)
                        eng.wait_ge(s["norm_ready"], grp(i, q) - 2)
                    eng.activation(eT[p][:, :, P * j:P * (j + 1)], bank[4][:, :].rearrange("p (g n) -> p g n", g=4),
                                   ACT.Exp).then_inc(s["exp_ready"], 1)
                tanh(0)
                tanh(1)
                for j in range(GT):
                    exp(j)
                    if j + 2 < GT:
                        tanh(j + 2)

            with eng.Fori(0, B) as i:
                for q in range(GPB):
                    softmax(i, q)
                    route(i, q, 1)
            experts(1)

        @block.vector
        def _(eng):
            seed(eng, "var_a", "xn_ready", "q_negs", "k_negs", "q_done", "k_done", "kv_ready", "att_ready",
                 "x_attended", "var_r", "gam_ready", "hits_ready", "gap_ready", "scatter_ready", "routed",
                 "hid_ready", "y_copied", "combined", "var_z", "z_ready", "ci_ready", "gated_ready",
                 "max_ready", "prod_ready", "conv_ready", "var_v", "x_convolved")

            class Chain:

                def __init__(self, base):
                    self.base, self.n = base, 0

                def __call__(self, ins, apart=False):
                    self.n += 1
                    ins.then_inc(s["chain"], 1)
                    (wait_alone if apart else wait)(eng, s["chain"], self.base + self.n)

            once = Chain(0)
            eng.wait_ge(s["consts_pool"], 3)
            once(eng.reciprocal(inv_count[:, :], inv_count[:, :]))
            eng.tensor_reduce(same_head[:, :], ident[:, :].rearrange("p (h d) -> p h d", d=D), AX.X, ALU.add)
            once(eng.tensor_reduce(mod_head[:, :], ident[:, :].rearrange("p (k h) -> p h k", h=H), AX.X, ALU.add))
            eng.tensor_copy(spread[:, :, :], over(mod_head[:, :], 1, D))
            for n in range(2):
                once(eng.tensor_copy(pick[:, n, H * n:H * (n + 1)], mod_head[:, :]))
            eng.wait_ge(s["w_in"], 16 * 13)
            eng.tensor_tensor(dyn_w[:, 0:K, :], over(wpe_sb[:, 0:K], 2, H), over(same_head[:, :], 1, K), ALU.mult)
            once(eng.tensor_tensor(gate_w[:, 0:K, :], over(wpe_sb[:, K:2 * K], 2, H), over(same_head[:, :], 1, K),
                                   ALU.mult))
            eng.tensor_scalar(dyn_w[:, :, :], dyn_w[:, :, :], 0.5, None, ALU.mult)
            once(eng.tensor_scalar(bpe_sb[:, 0, :, :], bpe_sb[:, 0, :, :], 0.5, None, ALU.mult))
            for n in range(3):
                once(eng.tensor_copy(bpe_hi[:, :, :, :], bpe_sb[:, :, :, :]))
                eng.tensor_copy(bpe_parts[32 * n:32 * n + 1, :, :, :], bpe_hi[32 * n:32 * n + 1, :, :, :])
                once(eng.tensor_tensor(bpe_sb[:, :, :, :], bpe_sb[:, :, :, :], bpe_hi[:, :, :, :], ALU.subtract))
            eng.tensor_copy(bpe_hi[:, 0, 0, 0:1], bpe_hi[:, 0, 0, 0:1]).then_inc(s["consts"], 1)
            eng.wait_ge(s["consts"], 1)

            def moments(chain, tile_at, scale, eps, var, q):
                for j in range(GT):
                    ins = eng.bn_stats(stats[:, j, :], tile_at(j))
                chain(ins, apart=True)
                for j in range(GT):
                    ins = eng.bn_aggr(mv[:, j, :], stats[:, j, :])
                chain(ins)
                eng.tensor_scalar(var_eps[q % 2][:, :], mv[:, :, 1], scale, eps, ALU.mult, ALU.add)\
                   .then_inc(s[var], 1)

            def center(to, tile_at, q):
                for j in range(GT):
                    ins = eng.tensor_scalar(to[:, j, :], tile_at(j), mv[:, j, 0:1], rstd[q % 2][:, j:j + 1],
                                            ALU.subtract, ALU.mult)
                return ins

            def keys(chain, i, q):
                p = q % 2
                at = lambda j: tile_of(X, i, q, j)
                moments(chain, at, 1.0, LN_EPS, "var_a", q)
                eng.wait_ge(s["rstd_a"], grp(i, q))
                eng.wait_ge(s["xnT_ready"], grp(i, q) - 2)
                center(xn[p], at, q).then_inc(s["xn_ready"], 1)
                eng.wait_ge(s["q_ready"], grp(i, q))
                eng.wait_ge(s["q_exps"], grp(i, q) - 1)
                eng.tensor_scalar(q_neg[:, :], bank[0][:, :], 0.0, None, ALU.min).then_inc(s["q_negs"], 1)
                eng.wait_ge(s["k_ready"], grp(i, q))
                eng.wait_ge(s["k_exps"], grp(i, q) - 1)
                eng.tensor_scalar(k_neg[:, :], bank[1][:, :], 0.0, None, ALU.min).then_inc(s["k_negs"], 1)
                eng.wait_ge(s["q_exps"], grp(i, q))
                eng.wait_ge(s["on_ready"], grp(i, q) - GPB)
                eng.scalar_tensor_tensor(q_phi[:, q, :], bank[0][:, :], 0.0, q_exp[:, :], ALU.max, ALU.add)\
                   .then_inc(s["q_done"], 1)
                eng.wait_ge(s["k_exps"], grp(i, q))
                eng.wait_ge(s["kv_added"], grp(i, q) - 2)
                eng.scalar_tensor_tensor(k_phi[p][:, :], bank[1][:, :], 0.0, k_exp[:, :], ALU.max, ALU.add)\
                   .then_inc(s["k_done"], 1)

            def states(i):
                eng.wait_ge(s["kv_added"], grp(i, GPB - 1))
                eng.wait_ge(s["on_ready"], grp(i, GPB - 1) - GPB)
                eng.tensor_tensor(kv_norm[:, 0, :, :], bank[3][:, 0:C].rearrange("p (h m) -> p h m", m=D),
                                  over(same_head[:, :], 2, D), ALU.mult)
                eng.tensor_scalar(kv_norm[:, 1, :, :], over(same_head[:, :], 2, D), bank[3][:, C:C + 1], None,
                                  ALU.mult).then_inc(s["kv_ready"], 1)

            def attend(chain, i, q):
                p = q % 2
                eng.wait_ge(s["on_ready"], grp(i, q))
                chain(eng.tensor_scalar(norm_r[:, :], bank[5][:, :], ATT_EPS, None, ALU.add))
                chain(eng.reciprocal(norm_r[:, :], norm_r[:, :]))
                eng.wait_ge(s["proj_ready"], grp(i, q) - 2)
                eng.tensor_tensor(attT[p][:, :], bank[4][:, :], norm_r[:, :], ALU.mult).then_inc(s["att_ready"], 1)
                eng.wait_ge(s["proj_ready"], grp(i, q))
                xg = tiles_of(X, i, q)
                chain(eng.tensor_tensor(xg, bank[6][:, :].rearrange("p (j c) -> p j c", c=C), xg, ALU.add))
                eng.tensor_tensor(xg, xg, over(bproj_sb[:, :], 1, GT), ALU.add).then_inc(s["x_attended"], 1)
                wait_alone(eng, s["x_attended"], grp(i, q))

            def route(chain, i, q, r):
                p, bk = q % 2, bank[3] if r == 0 else bank[6]
                at = lambda j: tile_of(X, i, q, j)
                moments(chain, at, 1.0 + LN_EPS, LN_EPS * LN_EPS, "var_r", q)
                eng.wait_ge(s["rstd_r"], grp(i, q, r))
                chain(center(x_hat, at, q))
                eng.wait_ge(s["xf_ready"], grp(i, q, r) - 2)
                eng.tensor_tensor(x_gam[p][:, :, :], x_hat[:, :, :], over(gammaF_sb[:, :], 1, GT), ALU.mult)\
                   .then_inc(s["gam_ready"], 1)
                eng.wait_ge(s["logits_ready"], grp(i, q, r))
                chain(eng.tensor_scalar(logits[:, :, :], bk[:, 0:GT * E].rearrange("p (j e) -> p j e", e=E),
                                        -CLAMP, CLAMP, ALU.max, ALU.min), apart=True)
                for j in range(GT):
                    ins = eng.max(top[:, j, :], logits[:, j, :])
                chain(ins, apart=True)
                for j in range(GT):
                    ins = eng.max_index(top_i[:, j, :], top[:, j, :], logits[:, j, :])
                eng.wait_ge(s["gap_exp"], grp(i, q, r) - 1)
                chain(ins)
                eng.tensor_tensor(gap[:, :], top[:, :, 1], top[:, :, 0], ALU.subtract).then_inc(s["gap_ready"], 1)
                chain(eng.tensor_copy(expert[:, :, :], top_i[:, :, 0:TOPK]))
                chain(eng.tensor_tensor(onehot[:, :, :, :].rearrange("p j k e -> p (j k) e"),
                                        over(iota_e[:, :], 1, GT * TOPK),
                                        over(expert[:, :, :].rearrange("p j k -> p (j k)"), 2, E), ALU.is_equal))
                eng.wait_ge(s["pos_ready"], grp(i, q, r) - 1)
                eng.tensor_tensor(hits[p][:, :, :], onehot[:, :, 0, :], onehot[:, :, 1, :], ALU.add)\
                   .then_inc(s["hits_ready"], 1)
                eng.wait_ge(s["hits_ready"], grp(i, q, r))
                chain(eng.tensor_reduce(hit_sum[:, :], hits[p][:, :, :].rearrange("p j e -> p e j"), AX.X, ALU.add))
                chain(eng.tensor_tensor(hits_before[1 - p][:, :], hits_before[p][:, :], hit_sum[:, :], ALU.add))
                eng.wait_ge(s["pos_ready"], grp(i, q, r))
                chain(eng.tensor_tensor(masked[:, :, :, :], onehot[:, :, :, :],
                                        over(bk[:, 0:GT * E].rearrange("p (j e) -> p j e", e=E), 2, TOPK), ALU.mult))
                chain(eng.tensor_reduce(pos[:, :, :], masked[:, :, :, :], AX.X, ALU.add))
                eng.tensor_scalar(kept[:, :, :], pos[:, :, :], float(CAP), None, ALU.is_lt)
                eng.tensor_scalar(far[:, :, :], pos[:, :, :], float(CAP), FAR, ALU.is_ge, ALU.mult)
                chain(eng.scalar_tensor_tensor(slot[:, :, :], expert[:, :, :], float(CAP), pos[:, :, :],
                                               ALU.mult, ALU.add))
                chain(eng.tensor_tensor(slot[:, :, :], slot[:, :, :], far[:, :, :], ALU.add))
                eng.tensor_copy(scatter_at[p][:, :].rearrange("p (j k) -> p j k", k=TOPK), slot[:, :, :])\
                   .then_inc(s["scatter_ready"], 1)
                chain(eng.tensor_scalar(tiles_of(gather_at, i, q), slot[:, :, :], float(SLOTS - 1), None, ALU.min))
                eng.wait_ge(s["gap_exp"], grp(i, q, r))
                chain(eng.tensor_scalar(den[:, :], e_gap[:, :], 1.0, 1e-12, ALU.add, ALU.add))
                chain(eng.reciprocal(prob[:, :, 0], den[:, :]))
                chain(eng.tensor_tensor(prob[:, :, 1], e_gap[:, :], prob[:, :, 0], ALU.mult))
                eng.tensor_tensor(tiles_of(route_w, i, q), prob[:, :, :], kept[:, :, :], ALU.mult)\
                   .then_inc(s["routed"], 1)

            def experts(r):
                with eng.Fori(0, E // 2) as i:
                    def copy_y(b, c):
                        eng.wait_ge(s["y_ready"], chunk(i, b, c, r))
                        if c == 0:
                            eng.wait_ge(yb_stored[b], by_pair(i, r, 1) - 16)
                        eng.tensor_copy(yb[b][:, CH * c:CH * (c + 1), :],
                                        bank[6 + (NC * b + c) % 2][:, 0:CH * C].rearrange("p (t c) -> p t c", c=C))\
                           .then_inc(s["y_copied"], 1)
                    for n in range(2 * NC):
                        b, c = n // NC, n % NC
                        for f in range(2):
                            eng.wait_ge(s["silu_ready"], unit(i, b, c, f, r))
                            eng.wait_ge(s["u_ready"], unit(i, b, c, f, r))
                            if f == 0:
                                eng.wait_ge(s["y_ready"], chunk(i, b, c, r) - 2)
                            eng.tensor_tensor(hid[n % 2][:, 2 * f:2 * f + 2, :], silu_g[f][:, :, :],
                                              bank[4 + f][:, :].rearrange("p (a n) -> p a n", a=2), ALU.mult)\
                               .then_inc(s["hid_ready"], 1)
                            if f == 0 and n:
                                copy_y((n - 1) // NC, (n - 1) % NC)
                    copy_y(1, NC - 1)

            def combine(chain, i, q, r):
                p = q % 2
                chain(eng.tensor_copy(w_got[:, :, :], tiles_of(route_w, i, q)))
                eng.wait_ge(gathered[p], rows_moved(i, q, r))
                for k in range(TOPK):
                    for j in range(GT):
                        xt = tile_of(X, i, q, j)
                        ins = eng.scalar_tensor_tensor(xt, y_got[p][:, TOPK * j + k, :], w_got[:, j, k:k + 1], xt,
                                                       ALU.mult, ALU.add)
                    if k == 0:
                        chain(ins)
                ins.then_inc(s["combined"], 1)
                wait_alone(eng, s["combined"], grp(i, q, r))

            for b in range(B):
                eng.wait_ge(s[f"x_in{b}"], 16)
            n0 = once.n
            ATT, CMB, CNV = GPB * (2 + 3 + 18), GPB * 2, GPB * (3 + 8 + 2 + 18)
            with eng.Fori(0, B) as i:
                chain = Chain(i * ATT + n0)
                for q in range(GPB):
                    keys(chain, i, q)
                states(i)
                for q in range(GPB):
                    attend(chain, i, q)
                    route(chain, i, q, 0)
                assert chain.n == ATT, chain.n
            n0 += B * ATT
            experts(0)

            def means(chain, i, q):
                p = q % 2
                at = lambda j: tile_of(X, i, q, j)
                moments(chain, at, 1.0, LN_EPS, "var_z", q)
                eng.wait_ge(s["rstd_z"], grp(i, q))
                eng.wait_ge(s["zT_ready"], grp(i, q) - 2)
                center(z[p], at, q).then_inc(s["z_ready"], 1)
                eng.wait_ge(s["zT_ready"], grp(i, q))
                chain(eng.tensor_tensor_scan(cum[p][:, :], ones_f[:, :], bank[7][:, :],
                                             0.0 if q == 0 else cum[1 - p][:, GN - 1:GN], ALU.mult, ALU.add))
                eng.wait_ge(s["dyn_ready"], tile(i, q, GT - 1) - 2 * GT)
                eng.wait_ge(ci_stored[p], half(i, q, 0, 1) - 16)
                eng.tensor_tensor(ci[p][:, :], cum[p][:, :], inv_count[:, GN * q:GN * (q + 1)], ALU.mult)\
                   .then_inc(s["ci_ready"], 1)

            def softmax(chain, i, q):
                def gate(j):
                    eng.wait_ge(s["tanh_ready"], tile(i, q, j))
                    eng.wait_ge(s["dyn_ready"], tile(i, q, j))
                    eng.wait_ge(s["energy_ready"], tile(i, q, j) - 2)
                    eng.scalar_tensor_tensor(gated[j % 2][:, :, :], th[j % 2][:, :, :], 1.0,
                                             bank[2 + j % 2][:, :].rearrange("p (k h) -> p k h", h=H),
                                             ALU.add, ALU.mult).then_inc(s["gated_ready"], 1)

                def biggest(j):
                    eng.wait_ge(s["energy_ready"], tile(i, q, j))
                    eng.wait_ge(s["sub_ready"], tile(i, q, j) - 2)
                    eng.tensor_reduce(e_max[j % 2][:, :], energy[j % 2][:, 0:K, :].rearrange("p k h -> p h k"),
                                      AX.X, ALU.max).then_inc(s["max_ready"], 1)
                gate(0)
                for j in range(1, GT):
                    gate(j)
                    biggest(j - 1)
                biggest(GT - 1)

            def convolve(chain, i, q):
                p = q % 2
                eng.wait_ge(taps_loaded[p], half(i, q, 0, 8))
                eng.wait_ge(s["exp_ready"], tile(i, q, GT - 1))
                for o in range(8):
                    g, odd = o // 2, o % 2
                    eng.wait_ge(s["prod_added"], eighth(i, q, o) - 2)
                    eng.tensor_tensor(prod[odd][:, :, :], taps[p][:, odd:D:2, 8 * g:8 * g + GN],
                                      over(eT[p][:, g, :], 1, 4), ALU.mult).then_inc(s["prod_ready"], 1)
                eng.wait_ge(s["norm_ready"], grp(i, q))
                chain(eng.reciprocal(z_inv[:, :], bank[6][:, :]))
                eng.wait_ge(s["prod_added"], eighth(i, q, 7))
                eng.wait_ge(s["v_out"], grp(i, q) - 1)
                eng.tensor_tensor(convT[:, :], bank[5][:, :], z_inv[:, :], ALU.mult).then_inc(s["conv_ready"], 1)
                eng.wait_ge(s["v_out"], grp(i, q))
                chain(eng.tensor_tensor(v_sb[:, :, :], bank[6][:, :].rearrange("p (j c) -> p j c", c=C),
                                        z[p][:, :, :], ALU.add), apart=True)
                moments(chain, lambda j: v_sb[:, j, :], 1.0, CONV_EPS, "var_v", q)
                eng.wait_ge(s["rstd_v"], grp(i, q))
                chain(center(v_hat, lambda j: v_sb[:, j, :], q))
                chain(eng.tensor_tensor(v_hat[:, :, :], v_hat[:, :, :], over(gammaB_sb[:, :], 1, GT), ALU.mult))
                chain(eng.tensor_tensor(v_hat[:, :, :], v_hat[:, :, :], over(betaB_sb[:, :], 1, GT), ALU.add))
                xg = tiles_of(X, i, q)
                chain(eng.tensor_tensor(xg, xg, v_hat[:, :, :], ALU.add), apart=True)

            n1 = Chain(n0)
            n1(eng.memset(hits_before[0][:, :], 0.0))
            n0 += 1
            with eng.Fori(0, B) as i:
                chain = Chain(i * CNV + n0)
                for q in range(GPB):
                    combine(chain, i, q, 0)
                    means(chain, i, q)
                    softmax(chain, i, q)
                    convolve(chain, i, q)
                    route(chain, i, q, 1)
                assert chain.n == CNV, chain.n
            n0 += B * CNV
            experts(1)
            with eng.Fori(0, B) as i:
                chain = Chain(i * CMB + n0)
                for q in range(GPB):
                    combine(chain, i, q, 1)
                assert chain.n == CMB, chain.n

        @block.tensor
        def _(eng):
            seed(eng, "xnT_ready", "q_ready", "k_ready", "v_ready", "kv_added", "on_ready", "proj_ready",
                 "xfT_ready", "logits_ready", "pos_ready", "xbT_ready", "g_ready", "u_ready", "y_ready",
                 "zT_ready", "gate_ready", "dyn_ready", "eT_ready", "prod_added", "norm_ready", "v_out")
            eng.wait_ge(s["consts"], 1)

            def keys(i, q):
                p = q % 2
                eng.wait_ge(s["xn_ready"], grp(i, q))
                eng.wait_ge(s["xnT_copied"], grp(i, q) - 1)
                for j in range(GT):
                    mm = eng.transpose(bank[7][:, P * j:P * (j + 1)], xn[p][:, j, :], ident[:, :])
                mm.then_inc(s["xnT_ready"], 1)
                eng.wait_ge(s["xnT_copied"], grp(i, q))
                eng.wait_ge(s["q_done"], grp(i, q) - 1)
                eng.matmul(bank[0][:, :], wqkv_sb[:, 0:C], xnT[p][:, :], start=True, stop=True)\
                   .then_inc(s["q_ready"], 1)
                eng.wait_ge(s["k_done"], grp(i, q) - 1)
                eng.wait_ge(s["v_copied"], grp(i, q) - 1)
                for n, name in ((1, "k_ready"), (2, "v_ready")):
                    for j in range(GT):
                        mm = eng.matmul(bank[n][:, C * j:C * (j + 1)], xnT[p][:, P * j:P * (j + 1)],
                                        wqkv_sb[:, C * n:C * (n + 1)], start=True, stop=True)
                    mm.then_inc(s[name], 1)

            def add_kv(i, q):
                p = q % 2
                eng.wait_ge(s["k_done"], grp(i, q))
                eng.wait_ge(s["v_copied"], grp(i, q))
                if q == 0:
                    eng.wait_ge(s["routed"], grp(i, 0) - 1)
                for j in range(GT):
                    mm = eng.matmul(bank[3][:, 0:C + 1], k_phi[p][:, P * j:P * (j + 1)], v_one[p][:, j, :],
                                    start=(q == 0 and j == 0), stop=(q == GPB - 1 and j == GT - 1))
                mm.then_inc(s["kv_added"], 1)

            def attend(i, q):
                p = q % 2
                if q == 0:
                    eng.wait_ge(s["kv_ready"], i + (1 + SEED))
                eng.wait_ge(s["att_ready"], grp(i, q) - 1)
                eng.matmul(bank[4][:, :], kv_norm[:, 0, :, :].rearrange("p h m -> p (h m)"), q_phi[:, q, :],
                           start=True, stop=True)
                eng.matmul(bank[5][:, :], kv_norm[:, 1, :, :].rearrange("p h m -> p (h m)"), q_phi[:, q, :],
                           start=True, stop=True).then_inc(s["on_ready"], 1)
                eng.wait_ge(s["att_ready"], grp(i, q))
                eng.wait_ge(s["x_attended"], grp(i, q) - 1)
                for j in range(GT):
                    mm = eng.matmul(bank[6][:, C * j:C * (j + 1)], attT[p][:, P * j:P * (j + 1)], wproj_sb[:, :],
                                    start=True, stop=True)
                mm.then_inc(s["proj_ready"], 1)

            def route(i, q, r):
                p, bk = q % 2, bank[3] if r == 0 else bank[6]
                eng.wait_ge(s["xf_ready"], grp(i, q, r))
                eng.wait_ge(s["routed"], grp(i, q, r) - 1)
                for j in range(GT):
                    mm = eng.transpose(bk[:, P * j:P * (j + 1)], xf[p][:, j, :], ident[:, :])
                mm.then_inc(s["xfT_ready"], 1)
                eng.wait_ge(s["xfT_copied"], grp(i, q, r))
                for j in range(GT):
                    mm = eng.matmul(bk[:, E * j:E * (j + 1)], xfT[p][:, P * j:P * (j + 1)], router_sb[:, :],
                                    start=True, stop=True)
                mm.then_inc(s["logits_ready"], 1)
                eng.wait_ge(s["hits_ready"], grp(i, q, r))
                rows = hits[p][:, :, :].rearrange("p j e -> p (j e)")
                eng.matmul(bk[:, 0:GT * E], before[:, :], rows, start=True, stop=False, skip_group_check=True)
                for n in range(1, GT):
                    eng.matmul(bk[:, n * E:GT * E], ones[:, 0:P], rows[:, 0:(GT - n) * E],
                               start=False, stop=False, skip_group_check=True)
                eng.matmul(bk[:, 0:GT * E].rearrange("p (j e) -> p j e", e=E), ones[:, 0:P],
                           over(hits_before[p][:, :], 1, GT), start=False, stop=True,
                           skip_group_check=True).then_inc(s["pos_ready"], 1)

            def experts(r):
                with eng.Fori(0, E // 2) as i:
                    def turn(n):
                        b, c, q = n // NC, n % NC, n % 2
                        if c == 0:
                            eng.wait_ge(xb_loaded[b], by_pair(i, r, 1))
                        eng.wait_ge(s["xbT_copied"], chunk(i, b, c, r) - 2)
                        for t in range(CH):
                            mm = eng.transpose(bank[q][:, P * t:P * (t + 1)], xb[b][:, CH * c + t, :], ident[:, :])
                        mm.then_inc(s["xbT_ready"], 1)

                    def up(n, f):
                        b, c, q = n // NC, n % NC, n % 2
                        if f == 0:
                            eng.wait_ge(s["xbT_copied"], chunk(i, b, c, r))
                            if c == 0:
                                eng.wait_ge(w_loaded[b], by_pair(i, r, 2))
                        eng.wait_ge(s["hid_ready"], unit(i, b, c, f, r) - 2)
                        for half_of, at, name in ((0, 2, "g_ready"), (1, 4, "u_ready")):
                            for a in range(2):
                                col = F * half_of + P * (2 * f + a)
                                mm = eng.matmul(bank[at + f][:, CH * P * a:CH * P * (a + 1)],
                                                w12_sb[b][:, col:col + P], xbT[q][:, :], start=True, stop=True)
                            mm.then_inc(s[name], 1)

                    def down(n):
                        b, c, q = n // NC, n % NC, n % 2
                        eng.wait_ge(s["hid_ready"], unit(i, b, c, 1, r))
                        eng.wait_ge(s["y_copied"], chunk(i, b, c, r) - 2)
                        for t in range(CH):
                            for a in range(FT):
                                mm = eng.matmul(bank[6 + q][:, C * t:C * (t + 1)], hid[q][:, a, P * t:P * (t + 1)],
                                                w3_sb[b][:, a, :], start=(a == 0), stop=(a == FT - 1))
                        mm.then_inc(s["y_ready"], 1)

                    turn(0)
                    for n in range(2 * NC):
                        up(n, 0)
                        if n:
                            down(n - 1)
                        up(n, 1)
                        if n + 1 < 2 * NC:
                            turn(n + 1)
                    down(2 * NC - 1)

            with eng.Fori(0, B) as i:
                for q in range(GPB):
                    keys(i, q)
                    add_kv(i, q)
                for q in range(GPB):
                    attend(i, q)
                    route(i, q, 0)
            experts(0)

            def softmax(i, q):
                p = q % 2

                def logit(j):
                    if j == 0:
                        eng.wait_ge(s["ci_ready"], grp(i, q))
                    eng.wait_ge(s["tanh_ready"], tile(i, q, j) - 2)
                    eng.wait_ge(s["gated_ready"], tile(i, q, j) - 2)
                    for at, w, part, name in ((0, gate_w, 1, "gate_ready"), (2, dyn_w, 0, "dyn_ready")):
                        bk = bank[at + j % 2][:, :]
                        eng.matmul(bk, ci[p][:, P * j:P * (j + 1)], w[:, :, :].rearrange("p k h -> p (k h)"),
                                   start=True, stop=False)
                        eng.matmul(bk, ones[:, 0:P], bpe_parts[:, part, :, :].rearrange("p k h -> p (k h)"),
                                   start=False, stop=True).then_inc(s[name], 1)

                def turn(j):
                    eng.wait_ge(s["sub_ready"], tile(i, q, j))
                    eng.wait_ge(s["exp_ready"], tile(i, q, j) - 1)
                    rows = e_sub[j % 2][:, :, :].rearrange("p k h -> p (k h)")
                    for g in range(4):
                        mm = eng.transpose(bank[4][:, P * g:P * (g + 1)], rows[:, P * g:P * (g + 1)], ident[:, :])
                    mm.then_inc(s["eT_ready"], 1)
                logit(0)
                logit(1)
                for j in range(GT):
                    if j + 2 < GT:
                        logit(j + 2)
                    turn(j)

            def convolve(i, q):
                p = q % 2
                eng.wait_ge(s["exp_ready"], tile(i, q, GT - 1))
                eng.wait_ge(s["routed"], grp(i, q, 1) - 1)
                for g in range(4):
                    mm = eng.matmul(bank[6][:, :], spread[:, :, :].rearrange("p d h -> p (d h)"), eT[p][:, g, :],
                                    start=(g == 0), stop=(g == 3))
                mm.then_inc(s["norm_ready"], 1)
                eng.wait_ge(s["conv_ready"], grp(i, q) - 1)
                for o in range(8):
                    eng.wait_ge(s["prod_ready"], eighth(i, q, o))
                    for n in range(4):
                        mm = eng.matmul(bank[5][32 * n:32 * (n + 1), :], pick[:, o % 2, :], prod[o % 2][:, n, :],
                                        start=(o == 0), stop=(o == 7))
                    mm.then_inc(s["prod_added"], 1)
                eng.wait_ge(s["conv_ready"], grp(i, q))
                for j in range(GT):
                    mm = eng.matmul(bank[6][:, C * j:C * (j + 1)], convT[:, P * j:P * (j + 1)], wfc_sb[:, :],
                                    start=True, stop=True)
                mm.then_inc(s["v_out"], 1)

            with eng.Fori(0, B) as i:
                for q in range(GPB):
                    eng.wait_ge(s["z_ready"], grp(i, q))
                    eng.wait_ge(s["ci_ready"], grp(i, q) - 1)
                    for j in range(GT):
                        mm = eng.transpose(bank[7][:, P * j:P * (j + 1)], z[q % 2][:, j, :], ident[:, :])
                    mm.then_inc(s["zT_ready"], 1)
                    softmax(i, q)
                    convolve(i, q)
                    route(i, q, 1)
            experts(1)


def kernel(**inputs):
    import numpy as np
    import concourse.bacc as bacc
    from concourse import mybir as mb
    from concourse.bass_utils import run_bass_kernel_spmd

    a = {n.removeprefix("L0_"): np.asarray(v) for n, v in inputs.items()}
    H, D, K = 16, 8, 31
    E, F2, C = a["ffn_w12"].shape
    rows = lambda v: np.broadcast_to(v.reshape(1, -1), (P, v.size))
    by_head = lambda v: np.repeat(v.reshape(-1, K)[:, :, None], H, axis=2).reshape(-1, K * H)
    bpe = by_head(a["attn_b_b_pe"])
    arrays = {
        "x": a["attn_a_x"],
        "wqkvT": a["attn_a_Wqkv"].T,
        "wprojT": a["attn_a_Wproj"].T,
        "bproj": rows(a["attn_a_bproj"]),
        "wpe": np.tile(a["attn_b_W_pe"], (H, 1)),
        "bpe": np.broadcast_to(bpe[None], (P, 2, K * H)),
        "stt": rows(a["attn_b_stt_energy"].reshape(H, K).T),
        "wfcT": a["attn_b_W_fc"].T.reshape(H, D, C).transpose(1, 0, 2).reshape(C, C),
        "gammaB": rows(a["attn_b_gamma"]),
        "betaB": rows(a["attn_b_beta"]),
        "gammaF": rows(a["ffn_ln_gamma"]),
        "betaF": rows(a["ffn_ln_beta"]),
        "routerT": a["ffn_router_w"].T,
        "w12T": a["ffn_w12"].transpose(0, 2, 1),
        "w3T": a["ffn_w3"].transpose(0, 2, 1).reshape(E, F2 // 2 // P, P, C).transpose(0, 2, 1, 3),
    }
    arrays = {n: np.ascontiguousarray(v) for n, v in arrays.items()}
    nc = bacc.Bacc("TRN2", target_bir_lowering=False, num_devices=1)
    args = [nc.dram_tensor(n, v.shape, mb.dt.from_np(v.dtype), kind="ExternalInput").ap() for n, v in arrays.items()]
    out = nc.dram_tensor("out", a["attn_a_x"].shape, mb.dt.from_np(np.dtype("float32")), kind="ExternalOutput").ap()
    hybrid_block(nc, *args, out)
    r = run_bass_kernel_spmd(nc, [arrays], core_ids=[0])
    return r.results[0]["out"]
```

```python
import concourse.bass as bass
from concourse import mybir
from contextlib import ExitStack

P = 128
SEED = 8


def hybrid_block(nc, x, wqkvT, wprojT, bproj, wpe, bpe, stt, wfcT, gammaB, betaB,
                 gammaF, betaF, routerT, w12T, w3T, out):
    fp32, fp32r, bf16, u32 = mybir.dt.float32, mybir.dt.float32r, mybir.dt.bfloat16, mybir.dt.uint32
    ALU = mybir.AluOpType
    ACT = mybir.ActivationFunctionType
    AX = mybir.AxisListType

    B, T, C = x.shape
    E = w12T.shape[0]
    F = w3T.shape[2] * P
    H, D = 16, 8
    K = 31
    KP = 32
    NT = B * T // P
    GT = 4
    GPB = T // (GT * P)
    NG = B * GPB
    GN = GT * P
    TOPK = 2
    CAP = -(-B * T * TOPK * 5 // (4 * E))
    SLOTS = E * CAP
    CT = CAP // P
    CH = 2
    NC = CT // CH
    FT = F // P
    HALO = K - 1
    PADROW = HALO + T + 2
    GROUPS = range(GPB)
    FAR = 65536.0
    LN_EPS, ATT_EPS, CONV_EPS, CLAMP = 1e-5, 1e-6, 1e-6, 10000.0

    slots_in = nc.dram_tensor("slots_in", (SLOTS, C), fp32, kind="Internal").ap()
    slots_out = nc.dram_tensor("slots_out", (SLOTS, C), fp32, kind="Internal").ap()
    ci_pad = nc.dram_tensor("ci_pad", (C, B, PADROW), fp32, kind="Internal").ap()

    x_v = x.rearrange("b (t p) c -> p (b t) c", p=P)
    out_v = out.rearrange("b (t p) c -> p (b t) c", p=P)
    slots_in_v = slots_in.rearrange("(e t p) c -> e p t c", p=P, e=E)
    slots_out_v = slots_out.rearrange("(e t p) c -> e p t c", p=P, e=E)

    with ExitStack() as ctx:
        def sb(name, shape, dt=fp32):
            return ctx.enter_context(nc.sbuf_tensor(name, shape, dt))

        def sem(name):
            return ctx.enter_context(nc.semaphore(name))

        def two(name, shape, dt=fp32):
            return [sb(f"{name}{n}", shape, dt) for n in range(2)]

        ident = sb("ident", [P, P])
        before = sb("before", [P, P], bf16)
        ones = sb("ones", [P, GN], bf16)
        ones_f = sb("ones_f", [P, GN])
        same_head = sb("same_head", [P, H])
        mod_head = sb("mod_head", [P, H])
        pick = sb("pick", [P, 2, 32])
        inv_count = sb("inv_count", [P, T])
        minus_half = sb("minus_half", [P, GT])
        iota_e = sb("iota_e", [P, E])
        wqkv_sb = sb("wqkv_sb", [P, 3 * C])
        wproj_sb = sb("wproj_sb", [P, C])
        bproj_sb = sb("bproj_sb", [P, C])
        wpe_sb = sb("wpe_sb", [P, 2 * K])
        gate_w = sb("gate_w", [P, KP, H])
        dyn_w = sb("dyn_w", [P, KP, H])
        bpe_sb = sb("bpe_sb", [P, 2, KP, H])
        bpe_hi = sb("bpe_hi", [P, 2, KP, H], bf16)
        bpe_parts = sb("bpe_parts", [P, 2, KP, H], bf16)
        stt_sb = sb("stt_sb", [P, KP, H])
        wfc_sb = sb("wfc_sb", [P, C])
        gammaB_sb, betaB_sb = sb("gammaB_sb", [P, C]), sb("betaB_sb", [P, C])
        gammaF_sb, betaF_sb = sb("gammaF_sb", [P, 1]), sb("betaF_sb", [P, 1])
        router_sb = sb("router_sb", [P, E])

        X = sb("X", [P, NT, C])
        gather_at = sb("gather_at", [P, NT, TOPK], u32)
        route_w = sb("route_w", [P, NT, TOPK])

        stats, mv, var_eps, rstd = ({n: sb(f"{name}_{n}", [P, GT, *size]) for n in "arzv"} for name, size in (
            ("stats", [6]), ("mv", [2]), ("var_eps", []), ("rstd", [])))

        phase = ExitStack()
        arena = phase.enter_context(nc.sbuf_tensor("arena", [P, 10816], fp32))
        taps = [phase.enter_context(nc.sbuf_tensor(f"taps{n}", [P, D, GN + 24], fp32)) for n in range(2)]
        phase.close()
        w12_parts, xbT_parts = (
            [[sb(f"{name}_{part}{n}", size, fp32r) for part in ("hi", "lo")] for n in range(2)] for name, size in (
                ("w12", [P, 2 * F]), ("xbT", [P, CH * P])))
        xbT = two("xbT", [P, CH * P])
        silu_g = two("silu_g", [P, 2, CH * P])
        hid = two("hid", [P, FT, CH * P])
        rest = sb("rest", [P, 10816 + 2 * D * (GN + 24) - 2 * (4 * F + 5 * CH * P + FT * CH * P)])

        arena_w = sb("arena_w", [P, 4096])

        def carve(arena):
            at = [0]

            def take(name, shape):
                n = 1
                for size in shape[1:]:
                    n *= size
                part = arena[0:shape[0], at[0]:at[0] + n]
                at[0] += n
                if len(shape) == 3:
                    part = part.rearrange("p (a b) -> p a b", a=shape[1])
                if len(shape) == 4:
                    part = part.rearrange("p (a b c) -> p a b c", a=shape[1], b=shape[2])
                return part
            return take, lambda name, shape: [take(name, shape) for _ in range(2)]

        att_sb, att_two = carve(arena)
        conv_sb, conv_two = carve(arena)
        _, prod_two = carve(arena_w)
        zeros = arena_w[:, 0:CT * C]
        xn = att_two("xn", [P, GT, C])
        xnT = att_two("xnT", [P, GN])
        q_neg, q_exp = att_sb("q_neg", [P, GN]), att_sb("q_exp", [P, GN])
        k_neg, k_exp = att_sb("k_neg", [P, GN]), att_sb("k_exp", [P, GN])
        q_phi = att_sb("q_phi", [P, GPB, GN])
        k_phi = att_two("k_phi", [P, GN])
        v_one = att_two("v_one", [P, GT, C + 1])
        kv = att_sb("kv", [P, H, D])
        k_sum = att_sb("k_sum", [P, H])
        norm_r = att_sb("norm_r", [P, GT, H])
        att = xn
        attT = att_two("attT", [P, GN])

        xf = two("xf", [P, GT, C])
        xfT = two("xfT", [P, GN])
        logits = sb("logits", [P, GT, E])
        top = sb("top", [P, GT, 8])
        top_i = sb("top_i", [P, GT, 8], u32)
        expert = sb("expert", [P, GT, TOPK])
        onehot = sb("onehot", [P, GT, TOPK, E])
        hits = two("hits", [P, GT, E], bf16)
        hit_sum = sb("hit_sum", [P, E])
        hits_before = two("hits_before", [P, E], bf16)
        gap = sb("gap", [P, GT])
        e_gap = sb("e_gap", [P, GT])
        masked = sb("masked", [P, GT, TOPK, E])
        pos = sb("pos", [P, GT, TOPK])
        kept = sb("kept", [P, GT, TOPK])
        far = sb("far", [P, GT, TOPK])
        slot = sb("slot", [P, GT, TOPK])
        scatter_at = two("scatter_at", [P, GT * TOPK], u32)
        den = sb("den", [P, GT])
        prob = sb("prob", [P, GT, TOPK])

        w12_sb = two("w12_sb", [P, 2 * F])
        w3_sb = two("w3_sb", [P, FT, C])
        xb = two("xb", [P, CT, C])
        yb = two("yb", [P, CT, C])

        gather_idx = two("gather_idx", [P, GT * TOPK], u32)
        y_got = two("y_got", [P, GT * TOPK, C])
        w_got = sb("w_got", [P, GT, TOPK])

        z = two("z", [P, GT, C])
        cum = two("cum", [P, GN])
        ci = two("ci", [P, GN])
        th = conv_two("th", [P, KP, H])
        gated = conv_two("gated", [P, KP, H])
        energy = conv_two("energy", [P, KP, H])
        e_max = two("e_max", [P, H])
        e_sub = conv_two("e_sub", [P, KP, H])
        eT = conv_two("eT", [P, 4, GN])
        prod = prod_two("prod", [P, 4, GN])
        w_inv = conv_sb("w_inv", [P, GT, H])
        inv_wide = conv_sb("inv_wide", [P, GT, D, H])
        z_inv = conv_sb("z_inv", [P, GN])
        convT = conv_sb("convT", [P, GN])
        v_sb = conv_sb("v_sb", [P, GT, C])
        v_hat = conv_sb("v_hat", [P, GT, C])

        bank = [ctx.enter_context(nc.psum_tensor(f"bank{n}", [P, 512], fp32)) for n in range(8)]

        s = {n: sem(n) for n in (
            "zero_rows", "x_in", "w_att", "w_conv", "consts_pool", "consts", "chain",
            "var_a", "rstd_a", "xn_ready", "xnT_ready", "xnT_copied", "q_ready", "k_ready", "v_ready",
            "q_negs", "k_negs", "q_exps", "k_exps", "v_copied", "q_done", "k_done", "kv_added",
            "kv_ready", "on_ready", "att_ready", "attT_ready", "attT_copied", "proj_ready", "x_attended",
            "var_r", "rstd_r", "xf_ready", "xfT_ready", "xfT_copied", "logits_ready",
            "hits_ready", "gap_ready", "gap_exp", "pos_ready", "scatter_ready", "routed",
            "w_high", "w_split", "xbT_ready", "xbT_copied", "xbT_high", "xbT_low", "g_ready", "u_ready", "silu_ready", "hid_ready",
            "y_ready", "y_copied",
            "idx_copied", "combined", "stored",
            "var_z", "rstd_z", "z_ready", "zT_ready", "ci_ready",
            "gate_ready", "dyn_ready", "tanh_ready", "gated_ready", "energy_ready", "max_ready",
            "sub_ready", "eT_ready", "exp_ready", "prod_ready", "prod_added", "norm_ready",
            "inv_ready", "inv_widened", "inv_spread", "inv_copied", "conv_ready", "v_out", "var_v", "rstd_v", "x_convolved")}
        scattered = [sem(f"scattered{n}") for n in range(2)]
        gathered = [sem(f"gathered{n}") for n in range(2)]
        w_loaded = [sem(f"w_loaded{n}") for n in range(2)]
        xb_loaded = [sem(f"xb_loaded{n}") for n in range(2)]
        yb_stored = [sem(f"yb_stored{n}") for n in range(2)]
        ci_stored = [sem(f"ci_stored{n}") for n in range(2)]
        taps_loaded = [sem(f"taps_loaded{n}") for n in range(2)]

        def wait_alone(eng, semaphore, value):
            value = eng.lower_val(value)
            eng.wait_ge(s["consts_pool"], 1)
            eng.wait_ge(semaphore, value)

        def wait(eng, semaphore, value):
            eng.wait_ge(semaphore, value)

        def seed(eng, *names):
            for n in names:
                eng.sem_inc(s[n], SEED)

        def grp(i, q, r=0):
            return i * GPB + (q + 1 + NG * r + SEED)

        def half(i, q, r, per, start=SEED):
            return i * (16 * per * GPB // 2) + 16 * per * (q // 2 + 1 + NG // 2 * r + start)

        def rows_moved(i, q, r):
            return half(i, q, r, GT * TOPK, 0)

        def tile(i, q, j):
            return i * (GPB * GT) + (GT * q + j + 1 + SEED)

        def eighth(i, q, o):
            return i * (GPB * 8) + (8 * q + o + 1 + SEED)

        def chunk(i, b, c, r):
            return i * (2 * NC) + (b * NC + c + 1 + E * NC * r + SEED)

        def unit(i, b, c, f, r):
            return i * (4 * NC) + (2 * (b * NC + c) + f + 1 + 2 * E * NC * r + SEED)

        def split(i, b, r):
            return i * 2 + (b + 1 + E * r + SEED)

        def by_pair(i, r, per):
            return i * (16 * per) + 16 * per * (1 + E // 2 * r + SEED)

        def route_bank(r):
            return bank[3] if r == 0 else bank[6]

        def tiles_of(t, i, q):
            return t[:, bass.ds(i * (GPB * GT) + GT * q, GT)]

        def tile_of(t, i, q, j):
            return t[:, bass.ds(i * (GPB * GT) + (GT * q + j), 1)].squeeze(1)

        def over(t, axis, n):
            t = t.unsqueeze(axis)
            shape = list(t.shape)
            shape[axis] = n
            return t.to_broadcast(shape)

        block = ctx.enter_context(nc.Block())

        @block.sync
        def _(eng):
            for m in (yb_stored, w_loaded, xb_loaded, ci_stored, taps_loaded):
                for n in range(2):
                    eng.sem_inc(m[n], 16 * SEED * {id(w_loaded): 2, id(taps_loaded): 8}.get(id(m), 1))
            row = NT // B
            eng.dma_start(X[:, 0:row, :], x_v[:, 0:row, :]).then_inc(s["x_in"], 16)
            for dst, src in ((wqkv_sb, wqkvT), (wproj_sb, wprojT), (bproj_sb, bproj),
                             (router_sb, routerT), (gammaF_sb, gammaF), (betaF_sb, betaF)):
                eng.dma_start(dst[:, :], src).then_inc(s["w_att"], 16)
            for b in range(1, B):
                eng.wait_ge(s["x_in"], 16 * b)
                eng.dma_start(X[:, b * row:(b + 1) * row, :], x_v[:, b * row:(b + 1) * row, :])\
                   .then_inc(s["x_in"], 16)
            eng.wait_ge(s["consts_pool"], 3)
            for e in range(E):
                eng.dma_start(slots_in_v[e], zeros.rearrange("p (t c) -> p t c", c=C))\
                   .then_inc(s["zero_rows"], 16)
            for b in range(B):
                eng.dma_start(ci_pad[:, b, 0:HALO], zeros[:, 0:HALO]).then_inc(s["zero_rows"], 16)
            for dst, src in ((wpe_sb, wpe), (wfc_sb, wfcT), (gammaB_sb, gammaB), (betaB_sb, betaB)):
                eng.dma_start(dst[:, :], src).then_inc(s["w_conv"], 16)
            for part in range(2):
                eng.dma_start(bpe_sb[:, part, 0:K, :].rearrange("p k h -> p (k h)"), bpe[:, part])\
                   .then_inc(s["w_conv"], 16)
            eng.dma_start(stt_sb[:, 0:K, :].rearrange("p k h -> p (k h)"), stt).then_inc(s["w_conv"], 16)
            eng.wait_ge(s["consts_pool"], 4)

            def expert_io(r):
                if r:
                    eng.wait_ge(s["y_copied"], chunk(E // 2 - 1, 1, NC - 1, 0))
                for b in range(2):
                    load_weights(0, b)
                eng.wait_ge(s["zero_rows"], 16 * (E + B))
                for n in range(2):
                    eng.wait_ge(scattered[n], rows_moved(B - 1, GPB - 2 + n, r))
                for b in range(2):
                    load_rows(0, b)
                with eng.Fori(0, E // 2 - 1) as i:
                    for b in range(2):
                        store(i, b, r)
                        wait_alone(eng, s["w_split"], split(i, b, r))
                        load_weights(i + 1, b)
                        load_rows(i + 1, b)
                for b in range(2):
                    store(E // 2 - 1, b, r)

            def load_weights(i, b):
                e = i * 2 + b
                eng.dma_start(w12_sb[b][:, :], w12T[bass.ds(e, 1)].squeeze(0)).then_inc(w_loaded[b], 16)
                eng.dma_start(w3_sb[b][:, :, :], w3T[bass.ds(e, 1)].squeeze(0)).then_inc(w_loaded[b], 16)

            def load_rows(i, b):
                eng.dma_start(xb[b][:, :, :], slots_in_v[bass.ds(i * 2 + b, 1)].squeeze(0)).then_inc(xb_loaded[b], 16)

            def store(i, b, r):
                wait_alone(eng, s["y_copied"], chunk(i, b, NC - 1, r))
                eng.dma_start(slots_out_v[bass.ds(i * 2 + b, 1)].squeeze(0), yb[b][:, :, :]).then_inc(yb_stored[b], 16)

            expert_io(0)
            eng.wait_ge(s["consts_pool"], 5)

            with eng.Fori(0, B) as i:
                for q in range(GPB):
                    p = q % 2
                    wait_alone(eng, s["ci_ready"], grp(i, q))
                    eng.dma_start(ci_pad[:, bass.ds(i, 1), HALO + GN * q:HALO + GN * (q + 1)].squeeze(1), ci[p][:, :])\
                       .then_inc(ci_stored[p], 16)
                    wait_alone(eng, ci_stored[p], half(i, q, 0, 1))
                    eng.wait_ge(s["prod_ready"], eighth(i, q, 7) - 16)
                    for k in range(8):
                        n = GN + 24 - (k == 7)
                        src = ci_pad.rearrange("(h d) b t -> h d b t", d=D)
                        eng.dma_start(taps[p][H * k:H * (k + 1), :, 0:n],
                                      src[:, :, bass.ds(i, 1), GN * q + k:GN * q + k + n].squeeze(2))\
                           .then_inc(taps_loaded[p], 16)

            expert_io(1)
            with eng.Fori(0, B) as i:
                for q in range(GPB):
                    wait_alone(eng, s["combined"], grp(i, q, 1))
                    eng.dma_start(tiles_of(out_v, i, q), tiles_of(X, i, q)).then_inc(s["stored"], 16)
            eng.wait_ge(s["stored"], 16 * NG)

        @block.gpsimd
        def _(eng):
            seed(eng, "rstd_a", "rstd_r", "w_high", "w_split", "idx_copied", "rstd_z", "energy_ready",
                 "sub_ready", "rstd_v")
            eng.memset(ident[:, :], 0.0)
            eng.memset(before[:, :], 1.0).then_inc(s["consts_pool"], 1)
            eng.wait_ge(s["consts_pool"], 1)
            eng.affine_select(out=ident[:, :], in_=ident[:, :], compare_op=ALU.not_equal, fill=1.0,
                              base=0, pattern=[[-1, P]], channel_multiplier=1)
            eng.affine_select(out=before[:, :], in_=before[:, :], compare_op=ALU.is_gt, fill=0.0,
                              base=0, pattern=[[1, P]], channel_multiplier=-1)
            eng.memset(ones[:, :], 1.0)
            eng.memset(ones_f[:, :], 1.0)
            eng.memset(minus_half[:, :], -0.5)
            for n in range(2):
                eng.memset(v_one[n][:, :, C:C + 1], 1.0)
            eng.memset(hits_before[0][:, :], 0.0)
            eng.iota(iota_e[:, :], pattern=[[1, E]], base=0, channel_multiplier=0,
                     allow_small_or_imprecise_dtypes=True).then_inc(s["consts_pool"], 1)
            eng.memset(zeros, 0.0).then_inc(s["consts_pool"], 1)
            eng.memset(bpe_sb[:, :, K:KP, :], 0.0)
            eng.memset(stt_sb[:, K:KP, :], -1e30)
            eng.memset(gate_w[:, K:KP, :], 0.0)
            eng.memset(dyn_w[:, K:KP, :], 0.0)
            eng.memset(pick[:, :, :], 0.0)
            eng.memset(bpe_parts[:, :, :, :], 0.0)
            eng.iota(inv_count[:, :], pattern=[[1, T]], base=1, channel_multiplier=0,
                     allow_small_or_imprecise_dtypes=True).then_inc(s["consts_pool"], 1)

            def rsqrt(norm, v):
                eng.wait_ge(s[f"var_{norm}"], v)
                eng.tensor_tensor(rstd[norm][:, :], var_eps[norm][:, :], minus_half[:, :],
                                  ALU.pow).then_inc(s[f"rstd_{norm}"], 1)

            def scatter(i, q, r, steps=range(GT * TOPK)):
                p = q % 2
                if steps[0] == 0:
                    if q == 0:
                        eng.wait_ge(s["zero_rows"], 16 * (E + B))
                    wait_alone(eng, s["scatter_ready"], grp(i, q, r))
                for n in steps:
                    eng.indirect_dma_start(
                        slots_in, bass.IndirectOffsetOnAxis(scatter_at[p][:, n:n + 1], 0),
                        xf[p][:, n // TOPK, :], None, bounds_check=SLOTS - 1,
                        oob_is_err=False).then_inc(scattered[p], 16)

            def settle(i, r):
                for n in range(2):
                    eng.wait_ge(scattered[n], rows_moved(i, GPB - 2 + n, r))

            def gather(i, q, r, steps=range(GT * TOPK)):
                p = q % 2
                if steps[0] == 0:
                    eng.wait_ge(s["combined"], grp(i, q, r) - 2)
                    eng.wait_ge(s["routed"], grp(i, q, r))
                    eng.tensor_copy(gather_idx[p][:, :].rearrange("p (j k) -> p j k", k=TOPK),
                                    tiles_of(gather_at, i, q)).then_inc(s["idx_copied"], 1)
                    wait_alone(eng, s["idx_copied"], grp(i, q, r))
                for n in steps:
                    eng.indirect_dma_start(
                        y_got[p][:, n, :], None, slots_out,
                        bass.IndirectOffsetOnAxis(gather_idx[p][:, n:n + 1], 0)).then_inc(gathered[p], 16)

            def split_weights(r):
                with eng.Fori(0, E // 2) as i:
                    for b in range(2):
                        wait_alone(eng, s["y_ready"], chunk(i, b, NC - 1, r) - 2 * NC)
                        wait_alone(eng, w_loaded[b], by_pair(i, r, 2))
                        eng.tensor_copy(w12_parts[b][0][:, :], w12_sb[b][:, :]).then_inc(s["w_high"], 1)
                        eng.wait_ge(s["w_high"], split(i, b, r))
                        eng.tensor_tensor(w12_parts[b][1][:, :], w12_sb[b][:, :], w12_parts[b][0][:, :],
                                          ALU.subtract).then_inc(s["w_split"], 1)

            with eng.Fori(0, B) as i:
                for q in range(GPB):
                    rsqrt("a", grp(i, q))
                rsqrt("r", grp(i, 0, 0))
                for q in GROUPS:
                    if q + 1 < GPB:
                        rsqrt("r", grp(i, q + 1, 0))
                    scatter(i, q, 0)
                settle(i, 0)

            split_weights(0)

            for n in range(2):
                eng.wait_ge(yb_stored[n], by_pair(E // 2 - 1, 0, 1))
            for n in range(2):
                ins = eng.memset(taps[n][:, :, GN + 23:GN + 24], 0.0)
            ins.then_inc(s["consts_pool"], 1)

            def add(i, q, j):
                eng.wait_ge(s["gated_ready"], tile(i, q, j))
                eng.wait_ge(s["max_ready"], tile(i, q, j) - 2)
                eng.tensor_tensor(energy[j % 2][:, :, :], gated[j % 2][:, :, :], stt_sb[:, :, :],
                                  ALU.add).then_inc(s["energy_ready"], 1)

            def sub(i, q, j):
                eng.wait_ge(s["max_ready"], tile(i, q, j))
                eng.wait_ge(s["eT_ready"], tile(i, q, j) - 2)
                eng.tensor_tensor(e_sub[j % 2][:, :, :], energy[j % 2][:, :, :],
                                  over(e_max[j % 2][:, :], 1, KP), ALU.subtract).then_inc(s["sub_ready"], 1)

            with eng.Fori(0, B) as i:
                for q in range(-2, GPB + 2):
                    early, late, ahead, next_ = q - 2 in GROUPS, q - 1 in GROUPS, q + 2 in GROUPS, q + 1 in GROUPS
                    if early:
                        scatter(i, q - 2, 1, range(0, 5))
                    if next_:
                        rsqrt("z", grp(i, q + 1))
                    if early:
                        scatter(i, q - 2, 1, range(5, 8))
                    if late:
                        rsqrt("v", grp(i, q - 1))
                    if ahead:
                        gather(i, q + 2, 0, range(0, 6))
                    if late:
                        rsqrt("r", grp(i, q - 1, 1))
                    for j in range(GT):
                        if ahead and j < 2:
                            gather(i, q + 2, 0, range(6 + j, 7 + j))
                        if next_:
                            add(i, q + 1, j)
                            if j:
                                sub(i, q + 1, j - 1)
                    if next_:
                        sub(i, q + 1, GT - 1)
                settle(i, 1)

            split_weights(1)
            for n in range(2):
                eng.wait_ge(yb_stored[n], by_pair(E // 2 - 1, 1, 1))
            with eng.Fori(0, B) as i:
                for q in range(GPB):
                    gather(i, q, 1)

        @block.scalar
        def _(eng):
            seed(eng, "xnT_copied", "q_exps", "k_exps", "v_copied", "xfT_copied", "gap_exp",
                 "xbT_copied", "silu_ready", "tanh_ready", "exp_ready",
                 "xbT_high", "attT_copied", "inv_widened", "inv_copied")

            def copy_rows(i, q):
                eng.wait_ge(s["xnT_ready"], grp(i, q))
                eng.wait_ge(s["v_ready"], grp(i, q) - 2)
                eng.activation(xnT[q % 2][:, :], bank[7][:, :], ACT.Copy).then_inc(s["xnT_copied"], 1)

            def copy_v(i, q):
                eng.wait_ge(s["v_ready"], grp(i, q))
                eng.wait_ge(s["kv_added"], grp(i, q) - 2)
                eng.activation(v_one[q % 2][:, :, 0:C], bank[2 + 4 * (q % 2)][:, :].rearrange("p (j c) -> p j c", c=C),
                               ACT.Copy).then_inc(s["v_copied"], 1)

            def exps(i, q):
                eng.wait_ge(s["q_negs"], grp(i, q))
                eng.wait_ge(s["q_done"], grp(i, q) - 1)
                eng.activation(q_exp[:, :], q_neg[:, :], ACT.Exp).then_inc(s["q_exps"], 1)
                eng.wait_ge(s["k_negs"], grp(i, q))
                eng.wait_ge(s["k_done"], grp(i, q) - 1)
                eng.activation(k_exp[:, :], k_neg[:, :], ACT.Exp).then_inc(s["k_exps"], 1)

            def copy_att(i, q):
                eng.wait_ge(s["attT_ready"], grp(i, q))
                eng.wait_ge(s["proj_ready"], grp(i, q) - 2)
                eng.activation(attT[q % 2][:, :], bank[5 - 4 * (q % 2)][:, :], ACT.Copy).then_inc(s["attT_copied"], 1)

            def turned(i, q, r):
                p, bk = q % 2, route_bank(r)
                eng.wait_ge(s["xfT_ready"], grp(i, q, r))
                eng.wait_ge(s["logits_ready"], grp(i, q, r) - 2)
                eng.activation(xfT[p][:, :], bk[:, :], ACT.Identity, scale=gammaF_sb[:, 0:1],
                               bias=betaF_sb[:, 0:1]).then_inc(s["xfT_copied"], 1)

            def gap_exp(i, q, r):
                eng.wait_ge(s["gap_ready"], grp(i, q, r))
                eng.wait_ge(s["routed"], grp(i, q, r) - 1)
                eng.activation(e_gap[:, :], gap[:, :], ACT.Exp).then_inc(s["gap_exp"], 1)

            def experts(r):
                def copy_rows(i, n):
                    q = n % 2
                    b, c = n // NC, n % NC
                    eng.wait_ge(s["xbT_ready"], chunk(i, b, c, r))
                    eng.wait_ge(s["xbT_low"], chunk(i, b, c, r) - 2)
                    eng.wait_ge(s["u_ready"], unit(i, b, c, 1, r) - 4)
                    eng.activation(xbT[q][:, :], bank[q][:, 0:CH * P], ACT.Identity,
                                   scale=gammaF_sb[:, 0:1], bias=betaF_sb[:, 0:1]).then_inc(s["xbT_copied"], 1)
                    eng.wait_ge(s["xbT_copied"], chunk(i, b, c, r))
                    eng.activation(xbT_parts[q][0][:, :], xbT[q][:, :], ACT.Copy).then_inc(s["xbT_high"], 1)

                def silu(i, n, f):
                    eng.wait_ge(s["g_ready"], unit(i, n // NC, n % NC, f, r))
                    eng.wait_ge(s["hid_ready"], unit(i, n // NC, n % NC, f, r) - 2)
                    eng.activation(silu_g[f][:, :, :], bank[2 + f][:, :].rearrange("p (a n) -> p a n", a=2),
                                   ACT.Silu).then_inc(s["silu_ready"], 1)

                def pair(i, last=False):
                    for n in range(2 * NC):
                        silu(i, n, 0)
                        if n + 1 < 2 * NC:
                            copy_rows(i, n + 1)
                        elif not last:
                            copy_rows(i + 1, 0)
                        silu(i, n, 1)
                copy_rows(0, 0)
                with eng.Fori(0, E // 2 - 1) as i:
                    pair(i)
                pair(E // 2 - 1, last=True)

            eng.wait_ge(s["w_att"], 16 * 6)
            with eng.Fori(0, B) as i:
                copy_rows(i, 0)
                for q in GROUPS:
                    copy_v(i, q)
                    if q + 1 < GPB:
                        copy_rows(i, q + 1)
                    exps(i, q)
                copy_att(i, 0)
                for q in GROUPS:
                    if q + 1 < GPB:
                        copy_att(i, q + 1)
                    turned(i, q, 0)
                    gap_exp(i, q, 0)
            experts(0)

            def tanh(i, q, j):
                eng.wait_ge(s["gate_ready"], tile(i, q, j))
                eng.wait_ge(s["gated_ready"], tile(i, q, j) - 2)
                eng.activation(th[j % 2][:, :, :], bank[j % 2][:, :].rearrange("p (k h) -> p k h", h=H),
                               ACT.Tanh, scale=0.5).then_inc(s["tanh_ready"], 1)

            def exp(i, q, j):
                eng.wait_ge(s["eT_ready"], tile(i, q, j))
                if j == 0:
                    eng.wait_ge(s["prod_ready"], eighth(i, q, 7) - 16)
                    eng.wait_ge(s["norm_ready"], grp(i, q) - 2)
                eng.activation(eT[q % 2][:, :, P * j:P * (j + 1)], bank[4][:, :].rearrange("p (g n) -> p g n", g=4),
                               ACT.Exp).then_inc(s["exp_ready"], 1)

            def widen_inverse(i, q):
                eng.wait_ge(s["inv_ready"], grp(i, q))
                eng.activation(inv_wide[:, :, :, :], over(w_inv[:, :, :], 2, D), ACT.Copy).then_inc(s["inv_widened"], 1)

            def copy_inverse(i, q):
                eng.wait_ge(s["inv_spread"], grp(i, q))
                eng.activation(z_inv[:, :], bank[7][:, :], ACT.Copy).then_inc(s["inv_copied"], 1)

            with eng.Fori(0, B) as i:
                for q in range(-1, GPB + 1):
                    late, now, next_ = q - 1 in GROUPS, q in GROUPS, q + 1 in GROUPS
                    if next_:
                        tanh(i, q + 1, 0)
                        tanh(i, q + 1, 1)
                    if late:
                        turned(i, q - 1, 1)
                    if now:
                        widen_inverse(i, q)
                        copy_inverse(i, q)
                    if next_:
                        exp(i, q + 1, 0)
                        tanh(i, q + 1, 2)
                        exp(i, q + 1, 1)
                        tanh(i, q + 1, 3)
                        exp(i, q + 1, 2)
                    if late:
                        gap_exp(i, q - 1, 1)
                    if next_:
                        exp(i, q + 1, 3)
            experts(1)

        @block.vector
        def _(eng):
            seed(eng, "var_a", "xn_ready", "q_negs", "k_negs", "q_done", "k_done", "kv_ready", "att_ready",
                 "x_attended", "var_r", "xf_ready", "hits_ready", "gap_ready", "scatter_ready", "routed",
                 "xbT_low", "hid_ready", "y_copied", "combined", "var_z", "z_ready", "ci_ready", "gated_ready",
                 "max_ready", "prod_ready", "inv_ready", "conv_ready", "var_v", "x_convolved")

            class Chain:

                def __init__(self, base):
                    self.base, self.n = base, 0

                def __call__(self, ins, apart=False):
                    self.n += 1
                    ins.then_inc(s["chain"], 1)
                    (wait_alone if apart else wait)(eng, s["chain"], self.base + self.n)

            def conv_consts(once):
                once(eng.reciprocal(inv_count[:, :], inv_count[:, :]))
                once(eng.tensor_reduce(mod_head[:, :], ident[:, :].rearrange("p (k h) -> p h k", h=H), AX.X, ALU.add))
                for n in range(2):
                    once(eng.tensor_copy(pick[:, n, H * n:H * (n + 1)], mod_head[:, :]))
                eng.wait_ge(s["w_conv"], 16 * 7)
                eng.tensor_tensor(dyn_w[:, 0:K, :], over(wpe_sb[:, 0:K], 2, H), over(same_head[:, :], 1, K), ALU.mult)
                once(eng.tensor_tensor(gate_w[:, 0:K, :], over(wpe_sb[:, K:2 * K], 2, H),
                                       over(same_head[:, :], 1, K), ALU.mult))
                eng.tensor_scalar(dyn_w[:, :, :], dyn_w[:, :, :], 0.5, None, ALU.mult)
                once(eng.tensor_scalar(bpe_sb[:, 0, :, :], bpe_sb[:, 0, :, :], 0.5, None, ALU.mult))
                for n in range(3):
                    once(eng.tensor_copy(bpe_hi[:, :, :, :], bpe_sb[:, :, :, :]))
                    eng.tensor_copy(bpe_parts[32 * n:32 * n + 1, :, :, :], bpe_hi[32 * n:32 * n + 1, :, :, :])
                    once(eng.tensor_tensor(bpe_sb[:, :, :, :], bpe_sb[:, :, :, :], bpe_hi[:, :, :, :], ALU.subtract))
                eng.memset(hits_before[0][:, :], 0.0).then_inc(s["consts"], 1)
                eng.wait_ge(s["consts"], 1)

            def moments(chain, norm, tile_at, scale, eps):
                for j in range(GT):
                    ins = eng.bn_stats(stats[norm][:, j, :], tile_at(j))
                chain(ins, apart=True)
                for j in range(GT):
                    ins = eng.bn_aggr(mv[norm][:, j, :], stats[norm][:, j, :])
                chain(ins)
                eng.tensor_scalar(var_eps[norm][:, :], mv[norm][:, :, 1], scale, eps, ALU.mult, ALU.add)\
                   .then_inc(s[f"var_{norm}"], 1)

            def center(norm, to, tile_at):
                for j in range(GT):
                    ins = eng.tensor_scalar(to[:, j, :], tile_at(j), mv[norm][:, j, 0:1], rstd[norm][:, j:j + 1],
                                            ALU.subtract, ALU.mult)
                return ins

            def key_moments(chain, i, q):
                if q == 0:
                    wait_alone(eng, s["x_in"], i * 16 + 16)
                moments(chain, "a", lambda j: tile_of(X, i, q, j), 1.0, LN_EPS)

            def key_rows(i, q):
                eng.wait_ge(s["rstd_a"], grp(i, q))
                eng.wait_ge(s["xnT_ready"], grp(i, q) - 2)
                center("a", xn[q % 2], lambda j: tile_of(X, i, q, j)).then_inc(s["xn_ready"], 1)

            def negatives(i, q):
                at = 4 * (q % 2)
                eng.wait_ge(s["q_ready"], grp(i, q))
                eng.wait_ge(s["q_exps"], grp(i, q) - 1)
                eng.tensor_scalar(q_neg[:, :], bank[at][:, :], 0.0, None, ALU.min).then_inc(s["q_negs"], 1)
                eng.wait_ge(s["k_ready"], grp(i, q))
                eng.wait_ge(s["k_exps"], grp(i, q) - 1)
                eng.tensor_scalar(k_neg[:, :], bank[at + 1][:, :], 0.0, None, ALU.min).then_inc(s["k_negs"], 1)

            def phis(i, q):
                at = 4 * (q % 2)
                eng.wait_ge(s["q_exps"], grp(i, q))
                eng.wait_ge(s["on_ready"], grp(i, q) - GPB)
                eng.scalar_tensor_tensor(q_phi[:, q, :], bank[at][:, :], 0.0, q_exp[:, :], ALU.max, ALU.add)\
                   .then_inc(s["q_done"], 1)
                eng.wait_ge(s["k_exps"], grp(i, q))
                eng.wait_ge(s["kv_added"], grp(i, q) - 2)
                eng.scalar_tensor_tensor(k_phi[q % 2][:, :], bank[at + 1][:, :], 0.0, k_exp[:, :], ALU.max, ALU.add)\
                   .then_inc(s["k_done"], 1)

            def states(i):
                eng.wait_ge(s["kv_added"], grp(i, GPB - 1))
                eng.wait_ge(s["on_ready"], grp(i, GPB - 1) - GPB)
                eng.tensor_tensor(kv[:, :, :], bank[3][:, 0:C].rearrange("p (h m) -> p h m", m=D),
                                  over(same_head[:, :], 2, D), ALU.mult)
                eng.tensor_scalar(k_sum[:, :], same_head[:, :], bank[3][:, C:C + 1], None,
                                  ALU.mult).then_inc(s["kv_ready"], 1)

            def normalize(chain, i, q):
                p = q % 2
                eng.wait_ge(s["on_ready"], grp(i, q))
                chain(eng.tensor_scalar(norm_r[:, :, :],
                                        bank[5 - 4 * p][:, 0:GT * H].rearrange("p (j h) -> p j h", h=H),
                                        ATT_EPS, None, ALU.add))
                chain(eng.reciprocal(norm_r[:, :, :], norm_r[:, :, :]))
                eng.wait_ge(s["attT_ready"], grp(i, q) - 2)
                eng.tensor_tensor(att[p][:, :, :].rearrange("p j (h m) -> p (j h) m", m=D),
                                  bank[4 - 4 * p][:, :].rearrange("p (a m) -> p a m", m=D),
                                  over(norm_r[:, :, :].rearrange("p j h -> p (j h)"), 2, D),
                                  ALU.mult).then_inc(s["att_ready"], 1)

            def attend(i, q):
                eng.wait_ge(s["proj_ready"], grp(i, q))
                xg = tiles_of(X, i, q)
                eng.tensor_tensor(xg, bank[6 - 4 * (q % 2)][:, :].rearrange("p (j c) -> p j c", c=C), xg,
                                  ALU.add).then_inc(s["x_attended"], 1)
                wait_alone(eng, s["x_attended"], grp(i, q))

            def route_moments(chain, i, q, r):
                moments(chain, "r", lambda j: tile_of(X, i, q, j), 1.0 + LN_EPS, LN_EPS * LN_EPS)

            def route_rows(i, q, r):
                p = q % 2
                eng.wait_ge(s["rstd_r"], grp(i, q, r))
                if q >= 2:
                    eng.wait_ge(scattered[p], rows_moved(i, q - 2, r))
                eng.wait_ge(s["xfT_ready"], grp(i, q, r) - 2)
                center("r", xf[p], lambda j: tile_of(X, i, q, j)).then_inc(s["xf_ready"], 1)

            def choose(chain, i, q, r):
                p, bk = q % 2, route_bank(r)
                eng.wait_ge(s["logits_ready"], grp(i, q, r))
                chain(eng.tensor_scalar(logits[:, :, :], bk[:, 0:GT * E].rearrange("p (j e) -> p j e", e=E),
                                        -CLAMP, CLAMP, ALU.max, ALU.min), apart=True)
                for j in range(GT):
                    ins = eng.max(top[:, j, :], logits[:, j, :])
                chain(ins, apart=True)
                for j in range(GT):
                    ins = eng.max_index(top_i[:, j, :], top[:, j, :], logits[:, j, :])
                eng.wait_ge(s["gap_exp"], grp(i, q, r) - 1)
                chain(ins)
                eng.tensor_tensor(gap[:, :], top[:, :, 1], top[:, :, 0], ALU.subtract).then_inc(s["gap_ready"], 1)
                chain(eng.tensor_copy(expert[:, :, :], top_i[:, :, 0:TOPK]))
                chain(eng.tensor_tensor(onehot[:, :, :, :].rearrange("p j k e -> p (j k) e"),
                                        over(iota_e[:, :], 1, GT * TOPK),
                                        over(expert[:, :, :].rearrange("p j k -> p (j k)"), 2, E), ALU.is_equal))
                eng.wait_ge(s["pos_ready"], grp(i, q, r) - 1)
                eng.tensor_tensor(hits[p][:, :, :], onehot[:, :, 0, :], onehot[:, :, 1, :], ALU.add)\
                   .then_inc(s["hits_ready"], 1)
                eng.wait_ge(s["hits_ready"], grp(i, q, r))
                chain(eng.tensor_reduce(hit_sum[:, :], hits[p][:, :, :].rearrange("p j e -> p e j"), AX.X, ALU.add))
                chain(eng.tensor_tensor(hits_before[1 - p][:, :], hits_before[p][:, :], hit_sum[:, :], ALU.add))

            def place(chain, i, q, r):
                p, bk = q % 2, route_bank(r)
                eng.wait_ge(s["pos_ready"], grp(i, q, r))
                chain(eng.tensor_tensor(masked[:, :, :, :], onehot[:, :, :, :],
                                        over(bk[:, 0:GT * E].rearrange("p (j e) -> p j e", e=E), 2, TOPK), ALU.mult))
                chain(eng.tensor_reduce(pos[:, :, :], masked[:, :, :, :], AX.X, ALU.add))
                eng.tensor_scalar(kept[:, :, :], pos[:, :, :], float(CAP), None, ALU.is_lt)
                eng.tensor_scalar(far[:, :, :], pos[:, :, :], float(CAP), FAR, ALU.is_ge, ALU.mult)
                chain(eng.scalar_tensor_tensor(slot[:, :, :], expert[:, :, :], float(CAP), pos[:, :, :],
                                               ALU.mult, ALU.add))
                chain(eng.tensor_tensor(slot[:, :, :], slot[:, :, :], far[:, :, :], ALU.add))
                eng.tensor_copy(scatter_at[p][:, :].rearrange("p (j k) -> p j k", k=TOPK), slot[:, :, :])\
                   .then_inc(s["scatter_ready"], 1)
                chain(eng.tensor_scalar(tiles_of(gather_at, i, q), slot[:, :, :], float(SLOTS - 1), None, ALU.min))
                eng.wait_ge(s["gap_exp"], grp(i, q, r))
                chain(eng.tensor_scalar(den[:, :], e_gap[:, :], 1.0, 1e-12, ALU.add, ALU.add))
                chain(eng.reciprocal(prob[:, :, 0], den[:, :]))
                chain(eng.tensor_tensor(prob[:, :, 1], e_gap[:, :], prob[:, :, 0], ALU.mult))
                eng.tensor_tensor(tiles_of(route_w, i, q), prob[:, :, :], kept[:, :, :], ALU.mult)\
                   .then_inc(s["routed"], 1)

            def experts(r):
                def low_rows(i, n):
                    b, c, q = n // NC, n % NC, n % 2
                    eng.wait_ge(s["xbT_high"], chunk(i, b, c, r))
                    eng.wait_ge(s["u_ready"], unit(i, b, c, 1, r) - 4)
                    eng.tensor_tensor(xbT_parts[q][1][:, :], xbT[q][:, :], xbT_parts[q][0][:, :], ALU.subtract)\
                       .then_inc(s["xbT_low"], 1)

                def features(i, n, f):
                    b, c = n // NC, n % NC
                    eng.wait_ge(s["silu_ready"], unit(i, b, c, f, r))
                    eng.wait_ge(s["u_ready"], unit(i, b, c, f, r))
                    if f == 0:
                        eng.wait_ge(s["y_ready"], chunk(i, b, c, r) - 2)
                    eng.tensor_tensor(hid[n % 2][:, 2 * f:2 * f + 2, :], silu_g[f][:, :, :],
                                      bank[4 + f][:, :].rearrange("p (a n) -> p a n", a=2), ALU.mult)\
                       .then_inc(s["hid_ready"], 1)

                def copy_y(i, n):
                    b, c = n // NC, n % NC
                    eng.wait_ge(s["y_ready"], chunk(i, b, c, r))
                    if c == 0:
                        eng.wait_ge(yb_stored[b], by_pair(i, r, 1) - 16)
                    eng.tensor_copy(yb[b][:, CH * c:CH * (c + 1), :],
                                    bank[6 + n % 2][:, 0:CH * C].rearrange("p (t c) -> p t c", c=C))\
                       .then_inc(s["y_copied"], 1)

                def pair(i, first=False, last=False):
                    for n in range(2 * NC):
                        features(i, n, 0)
                        if n + 1 < 2 * NC:
                            low_rows(i, n + 1)
                        elif not last:
                            low_rows(i + 1, 0)
                        features(i, n, 1)
                        if n:
                            copy_y(i, n - 1)
                        elif not first:
                            copy_y(i - 1, 2 * NC - 1)
                low_rows(0, 0)
                pair(0, first=True)
                with eng.Fori(1, E // 2 - 1) as i:
                    pair(i)
                pair(E // 2 - 1, last=True)
                copy_y(E // 2 - 1, 2 * NC - 1)

            def combine(chain, i, q, r):
                p = q % 2
                chain(eng.tensor_copy(w_got[:, :, :], tiles_of(route_w, i, q)))
                eng.wait_ge(gathered[p], rows_moved(i, q, r))
                for k in range(TOPK):
                    for j in range(GT):
                        xt = tile_of(X, i, q, j)
                        ins = eng.scalar_tensor_tensor(xt, y_got[p][:, TOPK * j + k, :], w_got[:, j, k:k + 1], xt,
                                                       ALU.mult, ALU.add)
                    if k == 0:
                        chain(ins)
                ins.then_inc(s["combined"], 1)
                wait_alone(eng, s["combined"], grp(i, q, r))

            once = Chain(0)
            eng.wait_ge(s["consts_pool"], 2)
            once(eng.tensor_reduce(same_head[:, :], ident[:, :].rearrange("p (h d) -> p h d", d=D), AX.X, ALU.add))
            n0 = once.n
            ATT, CMB, CNV = GPB * (2 + 2 + 17), GPB * 2, GPB * (3 + 7 + 2 + 17)
            with eng.Fori(0, B) as i:
                chain = Chain(i * ATT + n0)
                key_moments(chain, i, 0)
                key_rows(i, 0)
                key_moments(chain, i, 1)
                for q in GROUPS:
                    if q + 1 < GPB:
                        key_rows(i, q + 1)
                    negatives(i, q)
                    if q + 2 < GPB:
                        key_moments(chain, i, q + 2)
                    phis(i, q)
                states(i)
                normalize(chain, i, 0)
                attend(i, 0)
                route_moments(chain, i, 0, 0)
                for q in GROUPS:
                    more = q + 1 < GPB
                    if more:
                        normalize(chain, i, q + 1)
                    route_rows(i, q, 0)
                    if more:
                        attend(i, q + 1)
                        route_moments(chain, i, q + 1, 0)
                    choose(chain, i, q, 0)
                    place(chain, i, q, 0)
                assert chain.n == ATT, chain.n
            n0 += B * ATT
            once = Chain(n0)
            conv_consts(once)
            n0 += once.n
            experts(0)

            def z_rows(i, q):
                p = q % 2
                eng.wait_ge(s["rstd_z"], grp(i, q))
                eng.wait_ge(s["zT_ready"], grp(i, q) - 2)
                center("z", z[p], lambda j: tile_of(X, i, q, j)).then_inc(s["z_ready"], 1)

            def means(chain, i, q):
                p = q % 2
                eng.wait_ge(s["zT_ready"], grp(i, q))
                chain(eng.tensor_tensor_scan(cum[p][:, :], ones_f[:, :], bank[7][:, :],
                                             0.0 if q == 0 else cum[1 - p][:, GN - 1:GN], ALU.mult, ALU.add))
                eng.wait_ge(s["dyn_ready"], tile(i, q, GT - 1) - 2 * GT)
                eng.wait_ge(ci_stored[p], half(i, q, 0, 1) - 16)
                eng.tensor_tensor(ci[p][:, :], cum[p][:, :], inv_count[:, GN * q:GN * (q + 1)], ALU.mult)\
                   .then_inc(s["ci_ready"], 1)

            def gate(i, q, j):
                eng.wait_ge(s["tanh_ready"], tile(i, q, j))
                eng.wait_ge(s["dyn_ready"], tile(i, q, j))
                eng.wait_ge(s["energy_ready"], tile(i, q, j) - 2)
                eng.scalar_tensor_tensor(gated[j % 2][:, :, :], th[j % 2][:, :, :], 1.0,
                                         bank[2 + j % 2][:, :].rearrange("p (k h) -> p k h", h=H),
                                         ALU.add, ALU.mult).then_inc(s["gated_ready"], 1)

            def biggest(i, q, j):
                eng.wait_ge(s["energy_ready"], tile(i, q, j))
                eng.wait_ge(s["sub_ready"], tile(i, q, j) - 2)
                eng.tensor_reduce(e_max[j % 2][:, :], energy[j % 2][:, 0:K, :].rearrange("p k h -> p h k"),
                                  AX.X, ALU.max).then_inc(s["max_ready"], 1)

            def product(i, q, o):
                p, g, odd = q % 2, o // 2, o % 2
                if o == 0:
                    eng.wait_ge(taps_loaded[p], half(i, q, 0, 8))
                    eng.wait_ge(s["exp_ready"], tile(i, q, GT - 1))
                eng.wait_ge(s["prod_added"], eighth(i, q, o) - 2)
                eng.tensor_tensor(prod[odd][:, :, :], taps[p][:, odd:D:2, 8 * g:8 * g + GN],
                                  over(eT[p][:, g, :], 1, 4), ALU.mult).then_inc(s["prod_ready"], 1)

            def invert(i, q):
                eng.wait_ge(s["norm_ready"], grp(i, q))
                eng.reciprocal(w_inv[:, :, :], bank[7][:, 0:GT * H].rearrange("p (j h) -> p j h", h=H))\
                   .then_inc(s["inv_ready"], 1)

            def divide(i, q):
                eng.wait_ge(s["prod_added"], eighth(i, q, 7))
                eng.wait_ge(s["inv_copied"], grp(i, q))
                eng.wait_ge(s["v_out"], grp(i, q) - 1)
                eng.tensor_tensor(convT[:, :], bank[5][:, :], z_inv[:, :], ALU.mult).then_inc(s["conv_ready"], 1)

            def v_moments(chain, i, q):
                eng.wait_ge(s["v_out"], grp(i, q))
                chain(eng.tensor_tensor(v_sb[:, :, :], bank[6][:, :].rearrange("p (j c) -> p j c", c=C),
                                        z[q % 2][:, :, :], ALU.add), apart=True)
                moments(chain, "v", lambda j: v_sb[:, j, :], 1.0, CONV_EPS)

            def v_rows(chain, i, q):
                eng.wait_ge(s["rstd_v"], grp(i, q))
                chain(center("v", v_hat, lambda j: v_sb[:, j, :]))
                chain(eng.tensor_tensor(v_hat[:, :, :], v_hat[:, :, :], over(gammaB_sb[:, :], 1, GT), ALU.mult))
                chain(eng.tensor_tensor(v_hat[:, :, :], v_hat[:, :, :], over(betaB_sb[:, :], 1, GT), ALU.add))
                xg = tiles_of(X, i, q)
                chain(eng.tensor_tensor(xg, xg, v_hat[:, :, :], ALU.add), apart=True)

            with eng.Fori(0, B) as i:
                chain = Chain(i * CNV + n0)
                for q in range(-1, GPB + 1):
                    late, now, next_ = q - 1 in GROUPS, q in GROUPS, q + 1 in GROUPS
                    if now:
                        product(i, q, 0)
                    if late:
                        divide(i, q - 1)
                    if next_:
                        combine(chain, i, q + 1, 0)
                        moments(chain, "z", lambda j: tile_of(X, i, q + 1, j), 1.0, LN_EPS)
                    if now:
                        product(i, q, 1)
                    if late:
                        v_moments(chain, i, q - 1)
                    if next_:
                        z_rows(i, q + 1)
                    if now:
                        product(i, q, 2)
                    if next_:
                        means(chain, i, q + 1)
                    if late:
                        v_rows(chain, i, q - 1)
                        route_moments(chain, i, q - 1, 1)
                    if now:
                        product(i, q, 3)
                    if next_:
                        gate(i, q + 1, 0)
                    if late:
                        route_rows(i, q - 1, 1)
                    if now:
                        product(i, q, 4)
                    if next_:
                        gate(i, q + 1, 1)
                        biggest(i, q + 1, 0)
                    if now:
                        invert(i, q)
                        product(i, q, 5)
                    if next_:
                        gate(i, q + 1, 2)
                        biggest(i, q + 1, 1)
                    if now:
                        product(i, q, 6)
                    if next_:
                        gate(i, q + 1, 3)
                        biggest(i, q + 1, 2)
                    if late:
                        choose(chain, i, q - 1, 1)
                    if now:
                        product(i, q, 7)
                    if next_:
                        biggest(i, q + 1, 3)
                    if late:
                        place(chain, i, q - 1, 1)
                assert chain.n == CNV, chain.n
            n0 += B * CNV
            experts(1)
            with eng.Fori(0, B) as i:
                chain = Chain(i * CMB + n0)
                for q in range(GPB):
                    combine(chain, i, q, 1)
                assert chain.n == CMB, chain.n

        @block.tensor
        def _(eng):
            seed(eng, "xnT_ready", "q_ready", "k_ready", "v_ready", "kv_added", "on_ready", "proj_ready",
                 "xfT_ready", "logits_ready", "pos_ready", "xbT_ready", "g_ready", "u_ready", "y_ready",
                 "zT_ready", "gate_ready", "dyn_ready", "eT_ready", "prod_added", "norm_ready", "v_out",
                 "attT_ready", "inv_spread")
            eng.wait_ge(s["consts_pool"], 2)
            eng.wait_ge(s["w_att"], 16 * 6)

            def turn_x(i, q):
                eng.wait_ge(s["xn_ready"], grp(i, q))
                eng.wait_ge(s["xnT_copied"], grp(i, q) - 1)
                for j in range(GT):
                    mm = eng.transpose(bank[7][:, P * j:P * (j + 1)], xn[q % 2][:, j, :], ident[:, :])
                mm.then_inc(s["xnT_ready"], 1)

            def keys(i, q):
                p, at = q % 2, 4 * (q % 2)
                if q < 2:
                    eng.wait_ge(s["x_attended"], grp(i, 0) - 1)
                eng.wait_ge(s["xnT_copied"], grp(i, q))
                eng.wait_ge(s["q_done"], grp(i, q) - 2)
                eng.matmul(bank[at][:, :], wqkv_sb[:, 0:C], xnT[p][:, :], start=True, stop=True)\
                   .then_inc(s["q_ready"], 1)
                eng.wait_ge(s["k_done"], grp(i, q) - 2)
                eng.wait_ge(s["v_copied"], grp(i, q) - 2)
                for n, name in ((1, "k_ready"), (2, "v_ready")):
                    for j in range(GT):
                        mm = eng.matmul(bank[at + n][:, C * j:C * (j + 1)], xnT[p][:, P * j:P * (j + 1)],
                                        wqkv_sb[:, C * n:C * (n + 1)], start=True, stop=True)
                    mm.then_inc(s[name], 1)

            def add_kv(i, q):
                p = q % 2
                eng.wait_ge(s["k_done"], grp(i, q))
                eng.wait_ge(s["v_copied"], grp(i, q))
                if q == 0:
                    eng.wait_ge(s["routed"], grp(i, 0) - 1)
                for j in range(GT):
                    mm = eng.matmul(bank[3][:, 0:C + 1], k_phi[p][:, P * j:P * (j + 1)], v_one[p][:, j, :],
                                    start=(q == 0 and j == 0), stop=(q == GPB - 1 and j == GT - 1))
                mm.then_inc(s["kv_added"], 1)

            def query(i, q):
                p = q % 2
                if q == 0:
                    eng.wait_ge(s["kv_ready"], i + (1 + SEED))
                eng.wait_ge(s["att_ready"], grp(i, q) - 2)
                eng.wait_ge(s["attT_copied"], grp(i, q) - 2)
                for j in range(GT):
                    rows = q_phi[:, q, P * j:P * (j + 1)]
                    eng.matmul(bank[4 - 4 * p][:, C * j:C * (j + 1)], rows, kv[:, :, :].rearrange("p h m -> p (h m)"),
                               start=True, stop=True)
                    mm = eng.matmul(bank[5 - 4 * p][:, H * j:H * (j + 1)], rows, k_sum[:, :], start=True, stop=True)
                mm.then_inc(s["on_ready"], 1)

            def turn_att(i, q):
                p = q % 2
                eng.wait_ge(s["att_ready"], grp(i, q))
                for j in range(GT):
                    mm = eng.transpose(bank[5 - 4 * p][:, P * j:P * (j + 1)], att[p][:, j, :], ident[:, :])
                mm.then_inc(s["attT_ready"], 1)

            def project_att(i, q):
                p = q % 2
                eng.wait_ge(s["attT_copied"], grp(i, q))
                eng.wait_ge(s["x_attended"], grp(i, q) - 2)
                for j in range(GT):
                    to = bank[6 - 4 * p][:, C * j:C * (j + 1)]
                    eng.matmul(to, attT[p][:, P * j:P * (j + 1)], wproj_sb[:, :], start=True, stop=False)
                    mm = eng.matmul(to, ones_f[0:1, 0:P], bproj_sb[0:1, :], start=False, stop=True)
                mm.then_inc(s["proj_ready"], 1)

            def turn_rows(i, q, r):
                p, bk = q % 2, route_bank(r)
                eng.wait_ge(s["xf_ready"], grp(i, q, r))
                eng.wait_ge(s["routed"], grp(i, q, r) - 1)
                for j in range(GT):
                    mm = eng.transpose(bk[:, P * j:P * (j + 1)], xf[p][:, j, :], ident[:, :])
                mm.then_inc(s["xfT_ready"], 1)

            def router(i, q, r):
                p, bk = q % 2, route_bank(r)
                eng.wait_ge(s["xfT_copied"], grp(i, q, r))
                for j in range(GT):
                    mm = eng.matmul(bk[:, E * j:E * (j + 1)], xfT[p][:, P * j:P * (j + 1)], router_sb[:, :],
                                    start=True, stop=True)
                mm.then_inc(s["logits_ready"], 1)

            def count(i, q, r):
                p, bk = q % 2, route_bank(r)
                eng.wait_ge(s["hits_ready"], grp(i, q, r))
                rows = hits[p][:, :, :].rearrange("p j e -> p (j e)")
                eng.matmul(bk[:, 0:GT * E], before[:, :], rows, start=True, stop=False, skip_group_check=True)
                for n in range(1, GT):
                    eng.matmul(bk[:, n * E:GT * E], ones[:, 0:P], rows[:, 0:(GT - n) * E],
                               start=False, stop=False, skip_group_check=True)
                eng.matmul(bk[:, 0:GT * E].rearrange("p (j e) -> p j e", e=E), ones[:, 0:P],
                           over(hits_before[p][:, :], 1, GT), start=False, stop=True,
                           skip_group_check=True).then_inc(s["pos_ready"], 1)

            def experts(r):
                def turn(i, n):
                    b, c, q = n // NC, n % NC, n % 2
                    if c == 0:
                        eng.wait_ge(xb_loaded[b], by_pair(i, r, 1))
                    eng.wait_ge(s["xbT_copied"], chunk(i, b, c, r) - 2)
                    for t in range(CH):
                        mm = eng.transpose(bank[q][:, P * t:P * (t + 1)], xb[b][:, CH * c + t, :], ident[:, :])
                    mm.then_inc(s["xbT_ready"], 1)

                def product(to, ws, xs):
                    eng.matmul(to, ws[1], xs[0], start=True, stop=False)
                    eng.matmul(to, ws[0], xs[1], start=False, stop=False)
                    return eng.matmul(to, ws[0], xs[0], start=False, stop=True)

                def up(i, n, f):
                    b, c, q = n // NC, n % NC, n % 2
                    if f == 0:
                        eng.wait_ge(s["xbT_low"], chunk(i, b, c, r))
                        if c == 0:
                            eng.wait_ge(s["w_split"], split(i, b, r))
                    eng.wait_ge(s["hid_ready"], unit(i, b, c, f, r) - 2)
                    for half_of, at, name in ((0, 2, "g_ready"), (1, 4, "u_ready")):
                        for a in range(2):
                            col = F * half_of + P * (2 * f + a)
                            mm = product(bank[at + f][:, CH * P * a:CH * P * (a + 1)],
                                         [t[:, col:col + P] for t in w12_parts[b]], [t[:, :] for t in xbT_parts[q]])
                        mm.then_inc(s[name], 1)

                def down(i, n):
                    b, c, q = n // NC, n % NC, n % 2
                    eng.wait_ge(s["hid_ready"], unit(i, b, c, 1, r))
                    eng.wait_ge(s["y_copied"], chunk(i, b, c, r) - 2)
                    for t in range(CH):
                        for a in range(FT):
                            mm = eng.matmul(bank[6 + q][:, C * t:C * (t + 1)], hid[q][:, a, P * t:P * (t + 1)],
                                            w3_sb[b][:, a, :], start=(a == 0), stop=(a == FT - 1))
                    mm.then_inc(s["y_ready"], 1)

                def pair(i, first=False, last=False):
                    for n in range(2 * NC):
                        up(i, n, 0)
                        if n + 1 < 2 * NC:
                            turn(i, n + 1)
                        elif not last:
                            turn(i + 1, 0)
                        up(i, n, 1)
                        if n:
                            down(i, n - 1)
                        elif not first:
                            down(i - 1, 2 * NC - 1)
                turn(0, 0)
                pair(0, first=True)
                with eng.Fori(1, E // 2 - 1) as i:
                    pair(i)
                pair(E // 2 - 1, last=True)
                down(E // 2 - 1, 2 * NC - 1)

            with eng.Fori(0, B) as i:
                turn_x(i, 0)
                for q in GROUPS:
                    keys(i, q)
                    if q + 1 < GPB:
                        turn_x(i, q + 1)
                    if q:
                        add_kv(i, q - 1)
                add_kv(i, GPB - 1)
                query(i, 0)
                turn_att(i, 0)
                project_att(i, 0)
                for q in GROUPS:
                    more = q + 1 < GPB
                    if more:
                        query(i, q + 1)
                        turn_att(i, q + 1)
                    turn_rows(i, q, 0)
                    if more:
                        project_att(i, q + 1)
                    router(i, q, 0)
                    count(i, q, 0)
            experts(0)
            eng.wait_ge(s["consts"], 1)

            def turn_z(i, q):
                eng.wait_ge(s["z_ready"], grp(i, q))
                eng.wait_ge(s["ci_ready"], grp(i, q) - 1)
                for j in range(GT):
                    mm = eng.transpose(bank[7][:, P * j:P * (j + 1)], z[q % 2][:, j, :], ident[:, :])
                mm.then_inc(s["zT_ready"], 1)

            def logit(i, q, j):
                if j == 0:
                    eng.wait_ge(s["ci_ready"], grp(i, q))
                eng.wait_ge(s["tanh_ready"], tile(i, q, j) - 2)
                eng.wait_ge(s["gated_ready"], tile(i, q, j) - 2)
                for at, w, part, name in ((0, gate_w, 1, "gate_ready"), (2, dyn_w, 0, "dyn_ready")):
                    bk = bank[at + j % 2][:, :]
                    eng.matmul(bk, ci[q % 2][:, P * j:P * (j + 1)], w[:, :, :].rearrange("p k h -> p (k h)"),
                               start=True, stop=False)
                    eng.matmul(bk, ones[:, 0:P], bpe_parts[:, part, :, :].rearrange("p k h -> p (k h)"),
                               start=False, stop=True).then_inc(s[name], 1)

            def turn_e(i, q, j):
                eng.wait_ge(s["sub_ready"], tile(i, q, j))
                eng.wait_ge(s["exp_ready"], tile(i, q, j) - 1)
                rows = e_sub[j % 2][:, :, :].rearrange("p k h -> p (k h)")
                for g in range(4):
                    mm = eng.transpose(bank[4][:, P * g:P * (g + 1)], rows[:, P * g:P * (g + 1)], ident[:, :])
                mm.then_inc(s["eT_ready"], 1)

            def weigh(i, q):
                eng.wait_ge(s["exp_ready"], tile(i, q, GT - 1))
                eng.wait_ge(s["ci_ready"], grp(i, min(q + 1, GPB - 1)))
                for j in range(GT):
                    for g in range(4):
                        mm = eng.matmul(bank[7][:, H * j:H * (j + 1)], eT[q % 2][:, g, P * j:P * (j + 1)],
                                        mod_head[:, :], start=(g == 0), stop=(g == 3))
                mm.then_inc(s["norm_ready"], 1)

            def spread(i, q):
                eng.wait_ge(s["inv_widened"], grp(i, q))
                for j in range(GT):
                    mm = eng.transpose(bank[7][:, P * j:P * (j + 1)],
                                       inv_wide[:, j, :, :].rearrange("p d h -> p (d h)"), ident[:, :])
                mm.then_inc(s["inv_spread"], 1)

            def add(i, q, o):
                if o == 0:
                    eng.wait_ge(s["conv_ready"], grp(i, q) - 1)
                eng.wait_ge(s["prod_ready"], eighth(i, q, o))
                for n in range(4):
                    mm = eng.matmul(bank[5][32 * n:32 * (n + 1), :], pick[:, o % 2, :], prod[o % 2][:, n, :],
                                    start=(o == 0), stop=(o == 7))
                mm.then_inc(s["prod_added"], 1)

            def project(i, q):
                eng.wait_ge(s["conv_ready"], grp(i, q))
                eng.wait_ge(s["routed"], grp(i, q, 1) - 1)
                for j in range(GT):
                    mm = eng.matmul(bank[6][:, C * j:C * (j + 1)], convT[:, P * j:P * (j + 1)], wfc_sb[:, :],
                                    start=True, stop=True)
                mm.then_inc(s["v_out"], 1)

            with eng.Fori(0, B) as i:
                for q in range(-1, GPB + 1):
                    late, now, next_ = q - 1 in GROUPS, q in GROUPS, q + 1 in GROUPS
                    if late:
                        project(i, q - 1)
                    if now:
                        add(i, q, 0)
                        add(i, q, 1)
                    if next_:
                        turn_z(i, q + 1)
                    if now:
                        add(i, q, 2)
                    if next_:
                        logit(i, q + 1, 0)
                        logit(i, q + 1, 1)
                    if now:
                        weigh(i, q)
                        add(i, q, 3)
                    if late:
                        turn_rows(i, q - 1, 1)
                    if now:
                        add(i, q, 4)
                    if late:
                        router(i, q - 1, 1)
                    if now:
                        spread(i, q)
                    if next_:
                        turn_e(i, q + 1, 0)
                        logit(i, q + 1, 2)
                    if now:
                        add(i, q, 5)
                    if next_:
                        turn_e(i, q + 1, 1)
                        logit(i, q + 1, 3)
                    if now:
                        add(i, q, 6)
                    if next_:
                        turn_e(i, q + 1, 2)
                    if late:
                        count(i, q - 1, 1)
                    if now:
                        add(i, q, 7)
                    if next_:
                        turn_e(i, q + 1, 3)
            experts(1)


def kernel(**inputs):
    import numpy as np
    import concourse.bacc as bacc
    from concourse import mybir as mb
    from concourse.bass_utils import run_bass_kernel_spmd

    a = {n.removeprefix("L0_"): np.asarray(v) for n, v in inputs.items()}
    H, D, K = 16, 8, 31
    E, F2, C = a["ffn_w12"].shape
    rows = lambda v: np.broadcast_to(v.reshape(1, -1), (P, v.size))
    by_head = lambda v: np.repeat(v.reshape(-1, K)[:, :, None], H, axis=2).reshape(-1, K * H)
    bpe = by_head(a["attn_b_b_pe"])
    arrays = {
        "x": a["attn_a_x"],
        "wqkvT": a["attn_a_Wqkv"].T,
        "wprojT": a["attn_a_Wproj"].T,
        "bproj": rows(a["attn_a_bproj"]),
        "wpe": np.tile(a["attn_b_W_pe"], (H, 1)),
        "bpe": np.broadcast_to(bpe[None], (P, 2, K * H)),
        "stt": rows(a["attn_b_stt_energy"].reshape(H, K).T),
        "wfcT": a["attn_b_W_fc"].T.reshape(H, D, C).transpose(1, 0, 2).reshape(C, C),
        "gammaB": rows(a["attn_b_gamma"]),
        "betaB": rows(a["attn_b_beta"]),
        "gammaF": a["ffn_ln_gamma"].reshape(-1, 1),
        "betaF": a["ffn_ln_beta"].reshape(-1, 1),
        "routerT": a["ffn_router_w"].T,
        "w12T": a["ffn_w12"].transpose(0, 2, 1),
        "w3T": a["ffn_w3"].transpose(0, 2, 1).reshape(E, F2 // 2 // P, P, C).transpose(0, 2, 1, 3),
    }
    arrays = {n: np.ascontiguousarray(v) for n, v in arrays.items()}
    nc = bacc.Bacc("TRN2", target_bir_lowering=False, num_devices=1)
    args = [nc.dram_tensor(n, v.shape, mb.dt.from_np(v.dtype), kind="ExternalInput").ap() for n, v in arrays.items()]
    out = nc.dram_tensor("out", a["attn_a_x"].shape, mb.dt.from_np(np.dtype("float32")), kind="ExternalOutput").ap()
    hybrid_block(nc, *args, out)
    r = run_bass_kernel_spmd(nc, [arrays], core_ids=[0])
    return r.results[0]["out"]
```

```python
import concourse.bass as bass
from concourse import mybir
from contextlib import ExitStack

P = 128
SEED = 8


def hybrid_block(nc, x, wqkvT, wprojT, bproj, wpe, bpe, stt, wfcT, gammaB, betaB,
                 gammaF, betaF, routerT, w12T, w3T, out):
    fp32, fp32r, bf16, u32 = mybir.dt.float32, mybir.dt.float32r, mybir.dt.bfloat16, mybir.dt.uint32
    ALU = mybir.AluOpType
    ACT = mybir.ActivationFunctionType
    AX = mybir.AxisListType

    B, T, C = x.shape
    E = w12T.shape[0]
    F = w3T.shape[2] * P
    H, D = 16, 8
    K = 31
    KP = 32
    NT = B * T // P
    GT = 4
    GPB = T // (GT * P)
    NG = B * GPB
    GN = GT * P
    TOPK = 2
    CAP = -(-B * T * TOPK * 5 // (4 * E))
    SLOTS = E * CAP
    CT = CAP // P
    CH = 2
    NC = CT // CH
    FT = F // P
    HALO = K - 1
    PADROW = HALO + T + 2
    GROUPS, ALL = range(GPB), range(NG)
    FAR = 65536.0
    LN_EPS, ATT_EPS, CONV_EPS, CLAMP = 1e-5, 1e-6, 1e-6, 10000.0

    slots_in = nc.dram_tensor("slots_in", (SLOTS, C), fp32, kind="Internal").ap()
    slots_to = nc.dram_tensor("slots_to", (SLOTS, C + 1), fp32, kind="Internal").ap()
    y_sent = nc.dram_tensor("y_sent", (TOPK * NT * P, C), fp32, kind="Internal").ap()
    slots_out = nc.dram_tensor("slots_out", (SLOTS, C), fp32, kind="Internal").ap()
    ci_pad = nc.dram_tensor("ci_pad", (C, B, PADROW), fp32, kind="Internal").ap()

    x_v = x.rearrange("b (t p) c -> p (b t) c", p=P)
    out_v = out.rearrange("b (t p) c -> p (b t) c", p=P)
    slots_in_v = slots_in.rearrange("(e t p) c -> e p t c", p=P, e=E)
    slots_to_v = slots_to.rearrange("(e t p) c -> e p t c", p=P, e=E)
    y_sent_v = y_sent.rearrange("(k t p) c -> p k t c", p=P, k=TOPK)
    slots_out_v = slots_out.rearrange("(e t p) c -> e p t c", p=P, e=E)

    with ExitStack() as ctx:
        def sb(name, shape, dt=fp32):
            return ctx.enter_context(nc.sbuf_tensor(name, shape, dt))

        def sem(name):
            return ctx.enter_context(nc.semaphore(name))

        def two(name, shape, dt=fp32):
            return [sb(f"{name}{n}", shape, dt) for n in range(2)]

        ident = sb("ident", [P, P])
        before = sb("before", [P, P], bf16)
        ones = sb("ones", [P, GN], bf16)
        ones_f = sb("ones_f", [P, GN])
        same_head = sb("same_head", [P, H])
        mod_head = sb("mod_head", [P, H])
        pick = sb("pick", [P, 2, 32])
        inv_count = sb("inv_count", [P, T])
        minus_half = sb("minus_half", [P, GT])
        iota_e = sb("iota_e", [P, E])
        wqkv_sb = sb("wqkv_sb", [P, 3 * C])
        wproj_sb = sb("wproj_sb", [P, C])
        bproj_sb = sb("bproj_sb", [P, C])
        wpe_sb = sb("wpe_sb", [P, 2 * K])
        gate_w = sb("gate_w", [P, KP, H])
        dyn_w = sb("dyn_w", [P, KP, H])
        bpe_sb = sb("bpe_sb", [P, 2, KP, H])
        bpe_hi = sb("bpe_hi", [P, 2, KP, H], bf16)
        bpe_parts = sb("bpe_parts", [P, 2, KP, H], bf16)
        stt_sb = sb("stt_sb", [P, KP, H])
        wfc_sb = sb("wfc_sb", [P, C])
        gammaB_sb, betaB_sb = sb("gammaB_sb", [P, C]), sb("betaB_sb", [P, C])
        gammaF_sb, betaF_sb = sb("gammaF_sb", [P, 1]), sb("betaF_sb", [P, 1])
        router_sb = sb("router_sb", [P, E])

        X = sb("X", [P, NT, C])
        gather_at = sb("gather_at", [P, NT, TOPK], u32)
        route_w = sb("route_w", [P, NT, TOPK])

        stats, mv, var_eps, rstd, neg_mean, shift = (
            {n: sb(f"{name}_{n}", [P, GT, *size]) for n in "arzv"} for name, size in (
                ("stats", [6]), ("mv", [2]), ("var_eps", []), ("rstd", []), ("neg_mean", []), ("shift", [])))

        phase = ExitStack()
        arena = phase.enter_context(nc.sbuf_tensor("arena", [P, 10816], fp32))
        taps = [phase.enter_context(nc.sbuf_tensor(f"taps{n}", [P, D, GN + 24], fp32)) for n in range(2)]
        phase.close()
        w12_parts, xbT_parts = (
            [[sb(f"{name}_{part}{n}", size, fp32r) for part in ("hi", "lo")] for n in range(2)] for name, size in (
                ("w12", [P, 2 * F]), ("xbT", [P, CH * P])))
        xbT = two("xbT", [P, CH * P])
        silu_g = two("silu_g", [P, 2, CH * P])
        hid = two("hid", [P, FT, CH * P])
        rest = sb("rest", [P, 10816 + 2 * D * (GN + 24) - 2 * (4 * F + 5 * CH * P + FT * CH * P)])

        arena_w = sb("arena_w", [P, 4096])

        def carve(arena):
            at = [0]

            def take(name, shape):
                n = 1
                for size in shape[1:]:
                    n *= size
                part = arena[0:shape[0], at[0]:at[0] + n]
                at[0] += n
                if len(shape) == 3:
                    part = part.rearrange("p (a b) -> p a b", a=shape[1])
                if len(shape) == 4:
                    part = part.rearrange("p (a b c) -> p a b c", a=shape[1], b=shape[2])
                return part
            return take, lambda name, shape: [take(name, shape) for _ in range(2)]

        att_sb, att_two = carve(arena)
        conv_sb, conv_two = carve(arena)
        _, prod_two = carve(arena_w)
        zeros = arena_w[:, 0:CT * C]
        unused = arena_w[:, CT * C:CT * (2 * C + 1)].rearrange("p (t c) -> p t c", c=C + 1)
        xn = att_two("xn", [P, GT, C])
        xnT = att_two("xnT", [P, GN])
        q_neg, q_exp = att_sb("q_neg", [P, GN]), att_sb("q_exp", [P, GN])
        k_neg, k_exp = att_sb("k_neg", [P, GN]), att_sb("k_exp", [P, GN])
        q_phi = att_sb("q_phi", [P, GPB, GN])
        k_phi = att_two("k_phi", [P, GN])
        v_one = att_two("v_one", [P, GT, C + 1])
        kv = att_sb("kv", [P, H, D])
        k_sum = att_sb("k_sum", [P, H])
        norm_r = att_two("norm_r", [P, GT, H])
        att = xn
        attT = att_two("attT", [P, GN])

        xf, xf_twin = two("xf", [P, GT, C + 1]), two("xf_twin", [P, GT, C + 1])
        xfT = two("xfT", [P, GN])
        logits = sb("logits", [P, GT, E])
        top = sb("top", [P, GT, 8])
        top_i = sb("top_i", [P, GT, 8], u32)
        expert = sb("expert", [P, GT, TOPK])
        onehot = sb("onehot", [P, GT, TOPK, E])
        hits = two("hits", [P, GT, E], bf16)
        hit_sum = sb("hit_sum", [P, E])
        hits_before = two("hits_before", [P, E], bf16)
        gap = sb("gap", [P, GT])
        e_gap = sb("e_gap", [P, GT])
        masked = sb("masked", [P, GT, TOPK, E])
        pos = sb("pos", [P, GT, TOPK])
        kept = sb("kept", [P, GT, TOPK])
        far = sb("far", [P, GT, TOPK])
        slot = sb("slot", [P, GT, TOPK])
        scatter_at = two("scatter_at", [P, GT * TOPK], u32)
        den = sb("den", [P, GT])
        prob = sb("prob", [P, GT, TOPK])

        w12_sb = two("w12_sb", [P, 2 * F])
        w3_sb = two("w3_sb", [P, FT, C])
        xb = two("xb", [P, CT, C + 1])
        send_at = two("send_at", [P, CT], u32)
        yb = two("yb", [P, CT, C])

        gather_idx = two("gather_idx", [P, GT * TOPK], u32)
        y_got = two("y_got", [P, GT * TOPK, C])
        w_got = sb("w_got", [P, GT, TOPK])

        z = [sb(f"z{n}", [P, GT, C]) for n in range(3)]
        cum = two("cum", [P, GN])
        ci = two("ci", [P, GN])
        th = conv_two("th", [P, KP, H])
        gated = conv_two("gated", [P, KP, H])
        energy = conv_two("energy", [P, KP, H])
        e_max = two("e_max", [P, H])
        e_sub = conv_two("e_sub", [P, KP, H])
        eT = conv_two("eT", [P, 4, GN])
        prod = prod_two("prod", [P, 4, GN])
        w_inv = conv_sb("w_inv", [P, GT, H])
        inv_wide = conv_sb("inv_wide", [P, GT, D, H])
        z_inv = conv_sb("z_inv", [P, GN])
        convT = conv_sb("convT", [P, GN])
        v_hat = conv_sb("v_hat", [P, GT, C])

        bank = [ctx.enter_context(nc.psum_tensor(f"bank{n}", [P, 512], fp32)) for n in range(8)]

        s = {n: sem(n) for n in (
            "zero_rows", "zero_late", "x_in", "w_att", "w_conv", "consts_pool", "consts", "chain", "rooted",
            "var_a", "rstd_a", "xn_ready", "xnT_ready", "xnT_copied", "q_ready", "k_ready", "v_ready",
            "q_negs", "k_negs", "q_exps", "k_exps", "v_copied", "q_done", "k_done", "kv_added",
            "kv_ready", "on_ready", "att_ready", "attT_ready", "attT_copied", "proj_ready", "x_attended",
            "var_r", "rstd_r", "xf_ready", "xf_copied", "ids_ready", "xfT_ready", "xfT_copied", "logits_ready",
            "hits_ready", "gap_ready", "gap_exp", "pos_ready", "scatter_ready", "routed",
            "w_high", "w_split", "xbT_ready", "xbT_copied", "xbT_high", "xbT_low", "g_ready", "u_ready", "silu_ready", "hid_ready",
            "y_ready", "y_copied", "ids_copied",
            "idx_copied", "combined", "stored",
            "var_z", "rstd_z", "z_ready", "zT_ready", "ci_ready",
            "gate_ready", "dyn_ready", "tanh_ready", "gated_ready", "energy_ready", "max_ready",
            "sub_ready", "eT_ready", "exp_ready", "prod_ready", "prod_added", "norm_ready",
            "inv_ready", "inv_widened", "inv_spread", "inv_copied", "conv_ready", "v_out", "var_v", "rstd_v", "v_normed", "x_shifted")}
        scattered = [sem(f"scattered{n}") for n in range(2)]
        gathered = [sem(f"gathered{n}") for n in range(2)]
        sent = [sem(f"sent{n}") for n in range(2)]
        y_back = [sem(f"y_back{n}") for n in range(2)]
        w_loaded = [sem(f"w_loaded{n}") for n in range(2)]
        xb_loaded = [sem(f"xb_loaded{n}") for n in range(2)]
        yb_stored = [sem(f"yb_stored{n}") for n in range(2)]
        ci_stored = [sem(f"ci_stored{n}") for n in range(2)]
        taps_loaded = [sem(f"taps_loaded{n}") for n in range(2)]

        def wait_alone(eng, semaphore, value):
            if not isinstance(value, int):
                value = eng.lower_val(value)
                eng.wait_ge(s["consts_pool"], 1)
            eng.wait_ge(semaphore, value)

        def wait(eng, semaphore, value):
            eng.wait_ge(semaphore, value)

        def seed(eng, *names):
            for n in names:
                eng.sem_inc(s[n], SEED)

        def grp(i, q, r=0):
            return i * GPB + (q + 1 + NG * r + SEED)

        def half(i, q, r, per, start=SEED):
            return i * (16 * per * GPB // 2) + 16 * per * (q // 2 + 1 + NG // 2 * r + start)

        def rows_moved(i, q, r):
            return half(i, q, r, GT * TOPK, 0)

        def tile(i, q, j):
            return i * (GPB * GT) + (GT * q + j + 1 + SEED)

        def eighth(i, q, o):
            return i * (GPB * 8) + (8 * q + o + 1 + SEED)

        def chunk(i, b, c, r):
            return i * (2 * NC) + (b * NC + c + 1 + E * NC * r + SEED)

        def unit(i, b, c, f, r):
            return i * (4 * NC) + (2 * (b * NC + c) + f + 1 + 2 * E * NC * r + SEED)

        def split(i, b, r):
            return i * 2 + (b + 1 + E * r + SEED)

        def sent_by(i):
            return i * (16 * CT)

        def by_pair(i, r, per):
            return i * (16 * per) + 16 * per * (1 + E // 2 * r + SEED)

        def route_bank(r):
            return bank[3] if r == 0 else bank[6]

        def row(g):
            return divmod(g, GPB)

        def tiles_of(t, i, q):
            return t[:, bass.ds(i * (GPB * GT) + GT * q, GT)]

        def tile_of(t, i, q, j):
            return t[:, bass.ds(i * (GPB * GT) + (GT * q + j), 1)].squeeze(1)

        def over(t, axis, n):
            t = t.unsqueeze(axis)
            shape = list(t.shape)
            shape[axis] = n
            return t.to_broadcast(shape)

        block = ctx.enter_context(nc.Block())

        @block.sync
        def _(eng):
            for m in (yb_stored, w_loaded, xb_loaded, ci_stored, taps_loaded):
                for n in range(2):
                    eng.sem_inc(m[n], 16 * SEED * {id(w_loaded): 2, id(taps_loaded): 8}.get(id(m), 1))
            rt = NT // B
            eng.dma_start(X[:, 0:rt, :], x_v[:, 0:rt, :]).then_inc(s["x_in"], 16)
            for dst, src in ((wqkv_sb, wqkvT), (wproj_sb, wprojT), (bproj_sb, bproj),
                             (router_sb, routerT), (gammaF_sb, gammaF), (betaF_sb, betaF)):
                eng.dma_start(dst[:, :], src).then_inc(s["w_att"], 16)
            for b in range(1, B):
                eng.wait_ge(s["x_in"], 16 * b)
                eng.dma_start(X[:, b * rt:(b + 1) * rt, :], x_v[:, b * rt:(b + 1) * rt, :])\
                   .then_inc(s["x_in"], 16)
            eng.wait_ge(s["consts_pool"], 3)
            for e in range(E):
                eng.dma_start(slots_in_v[e], zeros.rearrange("p (t c) -> p t c", c=C))\
                   .then_inc(s["zero_rows"], 16)
            for b in range(B):
                eng.dma_start(ci_pad[:, b, 0:HALO], zeros[:, 0:HALO]).then_inc(s["zero_rows"], 16)
            for e in range(E):
                eng.dma_start(slots_to_v[e], unused).then_inc(s["zero_late"], 16)
            for k in range(TOPK):
                for t in range(0, NT, 8):
                    eng.dma_start(y_sent_v[:, k, t:t + 8, :], zeros[:, 0:8 * C].rearrange("p (t c) -> p t c", c=C))\
                       .then_inc(s["zero_late"], 16)
            for dst, src in ((wpe_sb, wpe), (wfc_sb, wfcT), (gammaB_sb, gammaB), (betaB_sb, betaB)):
                eng.dma_start(dst[:, :], src).then_inc(s["w_conv"], 16)
            for part in range(2):
                eng.dma_start(bpe_sb[:, part, 0:K, :].rearrange("p k h -> p (k h)"), bpe[:, part])\
                   .then_inc(s["w_conv"], 16)
            eng.dma_start(stt_sb[:, 0:K, :].rearrange("p k h -> p (k h)"), stt).then_inc(s["w_conv"], 16)
            eng.wait_ge(s["consts_pool"], 4)

            def expert_io(r):
                if r:
                    eng.wait_ge(s["y_copied"], chunk(E // 2 - 1, 1, NC - 1, 0))
                for b in range(2):
                    load_weights(0, b)
                eng.wait_ge(s["zero_rows"], 16 * (E + B))
                for n in range(2):
                    eng.wait_ge(scattered[n], rows_moved(B - 1, GPB - 2 + n, r))
                for b in range(2):
                    load_rows(0, b, r)
                with eng.Fori(0, E // 2 - 1) as i:
                    for b in range(2):
                        if r == 0:
                            store(i, b)
                        else:
                            wait_alone(eng, s["y_copied"], chunk(i, b, NC - 1, r))
                            wait_alone(eng, s["ids_copied"], split(i, b, 0))
                        wait_alone(eng, s["w_split"], split(i, b, r))
                        load_weights(i + 1, b)
                        load_rows(i + 1, b, r)
                if r == 0:
                    for b in range(2):
                        store(E // 2 - 1, b)

            def load_weights(i, b):
                e = i * 2 + b
                eng.dma_start(w12_sb[b][:, :], w12T[bass.ds(e, 1)].squeeze(0)).then_inc(w_loaded[b], 16)
                eng.dma_start(w3_sb[b][:, :, :], w3T[bass.ds(e, 1)].squeeze(0)).then_inc(w_loaded[b], 16)

            def load_rows(i, b, r):
                to, slots = (xb[b][:, :, 0:C], slots_in_v) if r == 0 else (xb[b][:, :, :], slots_to_v)
                eng.dma_start(to, slots[bass.ds(i * 2 + b, 1)].squeeze(0)).then_inc(xb_loaded[b], 16)

            def store(i, b):
                wait_alone(eng, s["y_copied"], chunk(i, b, NC - 1, 0))
                eng.dma_start(slots_out_v[bass.ds(i * 2 + b, 1)].squeeze(0), yb[b][:, :, :]).then_inc(yb_stored[b], 16)

            expert_io(0)
            eng.wait_ge(s["consts_pool"], 5)

            for g in ALL:
                i, q = row(g)
                p = q % 2
                eng.wait_ge(s["ci_ready"], grp(i, q))
                at = HALO + GN * q
                eng.dma_start(ci_pad[:, i, at:at + GN], ci[p][:, :]).then_inc(ci_stored[p], 16)
                eng.wait_ge(ci_stored[p], half(i, q, 0, 1))
                eng.wait_ge(s["prod_ready"], eighth(i, q, 7) - 16)
                for k in range(8):
                    n = GN + 24 - (k == 7)
                    eng.dma_start(taps[p][H * k:H * (k + 1), :, 0:n],
                                  ci_pad.rearrange("(h d) b t -> h d b t", d=D)[:, :, i, GN * q + k:GN * q + k + n])\
                       .then_inc(taps_loaded[p], 16)

            expert_io(1)
            for n in range(2):
                eng.wait_ge(sent[n], sent_by(E // 2))

            def load_y(i, q):
                for k in range(TOPK):
                    eng.dma_start(y_got[q % 2][:, GT * k:GT * (k + 1), :], tiles_of(y_sent_v[:, k], i, q))\
                       .then_inc(y_back[q % 2], 16)

            with eng.Fori(0, B) as i:
                load_y(i, 0)
                load_y(i, 1)
                for q in range(GPB):
                    wait_alone(eng, s["combined"], grp(i, q, 1))
                    if q + 2 < GPB:
                        load_y(i, q + 2)
                    eng.dma_start(tiles_of(out_v, i, q), tiles_of(X, i, q)).then_inc(s["stored"], 16)
            eng.wait_ge(s["stored"], 16 * NG)

        @block.gpsimd
        def _(eng):
            seed(eng, "rstd_a", "rstd_r", "w_high", "w_split", "idx_copied", "rstd_z", "energy_ready",
                 "ids_ready", "ids_copied", "sub_ready", "rstd_v", "x_shifted", "rooted")
            eng.memset(ident[:, :], 0.0)
            eng.memset(before[:, :], 1.0).then_inc(s["consts_pool"], 1)
            eng.wait_ge(s["consts_pool"], 1)
            eng.affine_select(out=ident[:, :], in_=ident[:, :], compare_op=ALU.not_equal, fill=1.0,
                              base=0, pattern=[[-1, P]], channel_multiplier=1)
            eng.affine_select(out=before[:, :], in_=before[:, :], compare_op=ALU.is_gt, fill=0.0,
                              base=0, pattern=[[1, P]], channel_multiplier=-1)
            eng.memset(ones[:, :], 1.0)
            eng.memset(ones_f[:, :], 1.0)
            eng.memset(minus_half[:, :], -0.5)
            for n in range(2):
                eng.memset(v_one[n][:, :, C:C + 1], 1.0)
            eng.memset(hits_before[0][:, :], 0.0)
            eng.iota(iota_e[:, :], pattern=[[1, E]], base=0, channel_multiplier=0,
                     allow_small_or_imprecise_dtypes=True).then_inc(s["consts_pool"], 1)
            eng.memset(zeros, 0.0)
            eng.memset(unused[:, :, 0:C], 0.0)
            eng.memset(unused[:, :, C:C + 1], FAR).then_inc(s["consts_pool"], 1)
            eng.memset(bpe_sb[:, :, K:KP, :], 0.0)
            eng.memset(stt_sb[:, K:KP, :], -1e30)
            eng.memset(gate_w[:, K:KP, :], 0.0)
            eng.memset(dyn_w[:, K:KP, :], 0.0)
            eng.memset(pick[:, :, :], 0.0)
            eng.memset(bpe_parts[:, :, :, :], 0.0)
            eng.iota(inv_count[:, :], pattern=[[1, T]], base=1, channel_multiplier=0,
                     allow_small_or_imprecise_dtypes=True).then_inc(s["consts_pool"], 1)

            def rsqrt(norm, v):
                eng.wait_ge(s[f"var_{norm}"], v)
                eng.tensor_tensor(rstd[norm][:, :], var_eps[norm][:, :], minus_half[:, :],
                                  ALU.pow).then_inc(s[f"rstd_{norm}"], 1)

            def scale_shift(norm, g, r=0):
                i, q = row(g)
                eng.wait_ge(s[f"var_{norm}"], grp(i, q, r))
                eng.tensor_tensor(rstd[norm][:, :], var_eps[norm][:, :], minus_half[:, :],
                                  ALU.pow).then_inc(s["rooted"], 1)
                roots[0] += 1
                eng.wait_ge(s["rooted"], roots[0] + SEED)
                eng.tensor_tensor(shift[norm][:, :], neg_mean[norm][:, :], rstd[norm][:, :],
                                  ALU.mult).then_inc(s[f"rstd_{norm}"], 1)

            roots = [0]

            def shift_x(i, q):
                eng.wait_ge(s["z_ready"], grp(i, q))
                xg = tiles_of(X, i, q)
                eng.tensor_tensor(xg, xg, over(betaB_sb[:, :], 1, GT), ALU.add).then_inc(s["x_shifted"], 1)

            def scatter(i, q, r, steps=range(GT * TOPK)):
                p = q % 2
                if steps[0] == 0:
                    if q == 0:
                        eng.wait_ge(s["zero_rows"], 16 * (E + B))
                    wait_alone(eng, s["scatter_ready"], grp(i, q, r))
                if r:
                    eng.wait_ge(s["xf_copied"], grp(i, q))
                    eng.wait_ge(s["ids_ready"], grp(i, q))
                for n in steps:
                    if r:
                        rows = (xf, xf_twin)[n % TOPK][p][:, n // TOPK, :]
                        eng.indirect_dma_start(
                            slots_to, bass.IndirectOffsetOnAxis(scatter_at[p][:, n:n + 1], 0), rows, None,
                            bounds_check=SLOTS - 1, oob_is_err=False).then_inc(scattered[p], 16)
                        continue
                    eng.indirect_dma_start(
                        slots_in, bass.IndirectOffsetOnAxis(scatter_at[p][:, n:n + 1], 0),
                        xf[p][:, n // TOPK, 0:C], None, bounds_check=SLOTS - 1,
                        oob_is_err=False).then_inc(scattered[p], 16)

            def number_rows(i, q):
                p = q % 2
                eng.wait_ge(scattered[p], rows_moved(i, q - 2, 1))
                for k, rows in enumerate((xf, xf_twin)):
                    ins = eng.iota(rows[p][:, :, C:C + 1], pattern=[[P, GT], [0, 1]],
                                   base=(k * NT + (i * GPB + q) * GT) * P, channel_multiplier=1,
                                   allow_small_or_imprecise_dtypes=True)
                ins.then_inc(s["ids_ready"], 1)

            def settle(i, r):
                for n in range(2):
                    eng.wait_ge(scattered[n], rows_moved(i, GPB - 2 + n, r))

            def gather(i, q, r, steps=range(GT * TOPK)):
                p = q % 2
                if steps[0] == 0:
                    eng.wait_ge(s["combined"], grp(i, q, r) - 2)
                    eng.wait_ge(s["routed"], grp(i, q, r))
                    eng.tensor_copy(gather_idx[p][:, :].rearrange("p (j k) -> p j k", k=TOPK),
                                    tiles_of(gather_at, i, q)).then_inc(s["idx_copied"], 1)
                    wait_alone(eng, s["idx_copied"], grp(i, q, r))
                for n in steps:
                    eng.indirect_dma_start(
                        y_got[p][:, n, :], None, slots_out,
                        bass.IndirectOffsetOnAxis(gather_idx[p][:, n:n + 1], 0)).then_inc(gathered[p], 16)

            def split_weights(i, b, r):
                wait_alone(eng, s["y_ready"], chunk(i, b, NC - 1, r) - 2 * NC)
                wait_alone(eng, w_loaded[b], by_pair(i, r, 2))
                eng.tensor_copy(w12_parts[b][0][:, :], w12_sb[b][:, :]).then_inc(s["w_high"], 1)
                eng.wait_ge(s["w_high"], split(i, b, r))
                eng.tensor_tensor(w12_parts[b][1][:, :], w12_sb[b][:, :], w12_parts[b][0][:, :],
                                  ALU.subtract).then_inc(s["w_split"], 1)

            def send(i, b, first=False):
                if not first:
                    wait_alone(eng, sent[b], sent_by(i))
                wait_alone(eng, xb_loaded[b], by_pair(i, 1, 1))
                eng.tensor_copy(send_at[b][:, :], xb[b][:, :, C]).then_inc(s["ids_copied"], 1)
                wait_alone(eng, s["ids_copied"], split(i, b, 0))
                for c in range(NC):
                    wait_alone(eng, s["y_copied"], chunk(i, b, c, 1))
                    for t in range(CH * c, CH * (c + 1)):
                        eng.indirect_dma_start(
                            y_sent, bass.IndirectOffsetOnAxis(send_at[b][:, t:t + 1], 0), yb[b][:, t, :], None,
                            bounds_check=TOPK * NT * P - 1, oob_is_err=False).then_inc(sent[b], 16)

            def split_and_send(i, first=False, last=False):
                split_weights(i, 1, 1)
                send(i, 0, first)
                if not last:
                    split_weights(i + 1, 0, 1)
                send(i, 1, first)

            with eng.Fori(0, B) as i:
                for q in range(GPB):
                    rsqrt("a", grp(i, q))
                rsqrt("r", grp(i, 0, 0))
                for q in GROUPS:
                    if q + 1 < GPB:
                        rsqrt("r", grp(i, q + 1, 0))
                    scatter(i, q, 0)
                settle(i, 0)

            with eng.Fori(0, E // 2) as i:
                for b in range(2):
                    split_weights(i, b, 0)

            eng.wait_ge(s["zero_late"], 16 * (E + TOPK * NT // 8))
            for n in range(2):
                eng.wait_ge(yb_stored[n], by_pair(E // 2 - 1, 0, 1))
            for n in range(2):
                ins = eng.memset(taps[n][:, :, GN + 23:GN + 24], 0.0)
            ins.then_inc(s["consts_pool"], 1)

            def add(i, q, j):
                eng.wait_ge(s["gated_ready"], tile(i, q, j))
                eng.wait_ge(s["sub_ready"], tile(i, q, j) - 2)
                eng.tensor_tensor(energy[j % 2][:, :, :], gated[j % 2][:, :, :], stt_sb[:, :, :],
                                  ALU.add).then_inc(s["energy_ready"], 1)

            def sub(i, q, j):
                eng.wait_ge(s["max_ready"], tile(i, q, j))
                eng.wait_ge(s["eT_ready"], tile(i, q, j) - 2)
                eng.tensor_tensor(e_sub[j % 2][:, :, :], energy[j % 2][:, :, :],
                                  over(e_max[j % 2][:, :], 1, KP), ALU.subtract).then_inc(s["sub_ready"], 1)

            for g in (0, 1):
                gather(*row(g), 0)
            for g in range(-1, NG + 2):
                old, late, next_ = g - 2 in ALL, g - 1 in ALL, g + 1 in ALL
                if g == -1:
                    scale_shift("z", 0)
                if g + 1 in ALL:
                    shift_x(*row(g + 1))
                if old:
                    scatter(*row(g - 2), 1)
                if late:
                    scale_shift("v", g - 1)
                if next_:
                    add(*row(g + 1), 0)
                if g + 3 in ALL:
                    gather(*row(g + 3), 0, range(0, 4))
                if late:
                    scale_shift("r", g - 1, 1)
                    number_rows(*row(g - 1))
                if next_:
                    add(*row(g + 1), 1)
                    sub(*row(g + 1), 0)
                    add(*row(g + 1), 2)
                    sub(*row(g + 1), 1)
                    add(*row(g + 1), 3)
                    sub(*row(g + 1), 2)
                if g + 3 in ALL:
                    gather(*row(g + 3), 0, range(4, 6))
                if next_:
                    sub(*row(g + 1), 3)
                if g + 3 in ALL:
                    gather(*row(g + 3), 0, range(6, 8))
                if g + 2 in ALL:
                    scale_shift("z", g + 2)
            settle(B - 1, 1)

            split_weights(0, 0, 1)
            split_and_send(0, first=True)
            with eng.Fori(1, E // 2 - 1) as i:
                split_and_send(i)
            split_and_send(E // 2 - 1, last=True)

        @block.scalar
        def _(eng):
            seed(eng, "xnT_copied", "q_exps", "k_exps", "v_copied", "xfT_copied", "gap_exp",
                 "xbT_copied", "silu_ready", "tanh_ready", "exp_ready",
                 "xbT_high", "xf_copied", "z_ready", "v_normed", "attT_copied", "inv_widened", "inv_copied")

            def copy_rows(i, q):
                eng.wait_ge(s["xnT_ready"], grp(i, q))
                eng.wait_ge(s["v_ready"], grp(i, q) - 2)
                eng.activation(xnT[q % 2][:, :], bank[7][:, :], ACT.Copy).then_inc(s["xnT_copied"], 1)

            def copy_v(i, q):
                eng.wait_ge(s["v_ready"], grp(i, q))
                eng.wait_ge(s["kv_added"], grp(i, q) - 2)
                eng.activation(v_one[q % 2][:, :, 0:C], bank[2 + 4 * (q % 2)][:, :].rearrange("p (j c) -> p j c", c=C),
                               ACT.Copy).then_inc(s["v_copied"], 1)

            def exps(i, q):
                eng.wait_ge(s["q_negs"], grp(i, q))
                eng.wait_ge(s["q_done"], grp(i, q) - 1)
                eng.activation(q_exp[:, :], q_neg[:, :], ACT.Exp).then_inc(s["q_exps"], 1)
                eng.wait_ge(s["k_negs"], grp(i, q))
                eng.wait_ge(s["k_done"], grp(i, q) - 1)
                eng.activation(k_exp[:, :], k_neg[:, :], ACT.Exp).then_inc(s["k_exps"], 1)

            def copy_att(i, q):
                eng.wait_ge(s["attT_ready"], grp(i, q))
                eng.wait_ge(s["proj_ready"], grp(i, q) - 2)
                eng.activation(attT[q % 2][:, :], bank[5 - 4 * (q % 2)][:, :], ACT.Copy).then_inc(s["attT_copied"], 1)

            def turned(i, q, r):
                p, bk = q % 2, route_bank(r)
                eng.wait_ge(s["xfT_ready"], grp(i, q, r))
                eng.wait_ge(s["logits_ready"], grp(i, q, r) - 2)
                eng.activation(xfT[p][:, :], bk[:, :], ACT.Identity, scale=gammaF_sb[:, 0:1],
                               bias=betaF_sb[:, 0:1]).then_inc(s["xfT_copied"], 1)

            def gap_exp(i, q, r):
                eng.wait_ge(s["gap_ready"], grp(i, q, r))
                eng.wait_ge(s["routed"], grp(i, q, r) - 1)
                eng.activation(e_gap[:, :], gap[:, :], ACT.Exp).then_inc(s["gap_exp"], 1)

            def experts(r):
                def copy_rows(i, n):
                    q = n % 2
                    b, c = n // NC, n % NC
                    eng.wait_ge(s["xbT_ready"], chunk(i, b, c, r))
                    eng.wait_ge(s["xbT_low"], chunk(i, b, c, r) - 2)
                    eng.wait_ge(s["u_ready"], unit(i, b, c, 1, r) - 4)
                    eng.activation(xbT[q][:, :], bank[q][:, 0:CH * P], ACT.Identity,
                                   scale=gammaF_sb[:, 0:1], bias=betaF_sb[:, 0:1]).then_inc(s["xbT_copied"], 1)
                    eng.wait_ge(s["xbT_copied"], chunk(i, b, c, r))
                    eng.activation(xbT_parts[q][0][:, :], xbT[q][:, :], ACT.Copy).then_inc(s["xbT_high"], 1)

                def silu(i, n, f):
                    eng.wait_ge(s["g_ready"], unit(i, n // NC, n % NC, f, r))
                    eng.wait_ge(s["hid_ready"], unit(i, n // NC, n % NC, f, r) - 2)
                    eng.activation(silu_g[f][:, :, :], bank[2 + f][:, :].rearrange("p (a n) -> p a n", a=2),
                                   ACT.Silu).then_inc(s["silu_ready"], 1)

                def pair(i, last=False):
                    for n in range(2 * NC):
                        silu(i, n, 0)
                        if n + 1 < 2 * NC:
                            copy_rows(i, n + 1)
                        elif not last:
                            copy_rows(i + 1, 0)
                        silu(i, n, 1)
                copy_rows(0, 0)
                with eng.Fori(0, E // 2 - 1) as i:
                    pair(i)
                pair(E // 2 - 1, last=True)

            eng.wait_ge(s["w_att"], 16 * 6)
            with eng.Fori(0, B) as i:
                copy_rows(i, 0)
                for q in GROUPS:
                    copy_v(i, q)
                    if q + 1 < GPB:
                        copy_rows(i, q + 1)
                    exps(i, q)
                copy_att(i, 0)
                copy_att(i, 1)
                for q in GROUPS:
                    turned(i, q, 0)
                    if q + 2 < GPB:
                        copy_att(i, q + 2)
                    gap_exp(i, q, 0)
            experts(0)

            def tanh(i, q, j):
                eng.wait_ge(s["gate_ready"], tile(i, q, j))
                eng.wait_ge(s["gated_ready"], tile(i, q, j) - 2)
                eng.activation(th[j % 2][:, :, :], bank[j % 2][:, :].rearrange("p (k h) -> p k h", h=H),
                               ACT.Tanh, scale=0.5).then_inc(s["tanh_ready"], 1)

            def exp(i, q, j):
                eng.wait_ge(s["eT_ready"], tile(i, q, j))
                if j == 0:
                    eng.wait_ge(s["prod_ready"], eighth(i, q, 7) - 16)
                    eng.wait_ge(s["norm_ready"], grp(i, q) - 2)
                eng.activation(eT[q % 2][:, :, P * j:P * (j + 1)], bank[4][:, :].rearrange("p (g n) -> p g n", g=4),
                               ACT.Exp).then_inc(s["exp_ready"], 1)

            def widen_inverse(i, q):
                eng.wait_ge(s["inv_ready"], grp(i, q))
                eng.activation(inv_wide[:, :, :, :], over(w_inv[:, :, :], 2, D), ACT.Copy).then_inc(s["inv_widened"], 1)

            def copy_inverse(i, q):
                eng.wait_ge(s["inv_spread"], grp(i, q))
                eng.activation(z_inv[:, :], bank[7][:, :], ACT.Copy).then_inc(s["inv_copied"], 1)

            def normed(norm, to, tile_at, ready):
                for j in range(GT):
                    ins = eng.activation(to[:, j, 0:C], tile_at(j), ACT.Identity, scale=rstd[norm][:, j:j + 1],
                                         bias=shift[norm][:, j:j + 1])
                ins.then_inc(s[ready], 1)

            def z_rows(i, q):
                eng.wait_ge(s["rstd_z"], grp(i, q))
                normed("z", z[(i * GPB + q) % 3], lambda j: tile_of(X, i, q, j), "z_ready")

            def v_rows(i, q):
                eng.wait_ge(s["rstd_v"], grp(i, q))
                normed("v", v_hat, lambda j: bank[6][:, C * j:C * (j + 1)], "v_normed")

            def route_rows(i, q):
                eng.wait_ge(s["rstd_r"], grp(i, q, 1))
                eng.wait_ge(scattered[q % 2], rows_moved(i, q - 2, 1))
                eng.wait_ge(s["xfT_ready"], grp(i, q, 1) - 2)
                normed("r", xf[q % 2], lambda j: tile_of(X, i, q, j), "xf_ready")

            def copy_twin(i, q):
                eng.wait_ge(s["xf_ready"], grp(i, q, 1))
                eng.activation(xf_twin[q % 2][:, :, 0:C], xf[q % 2][:, :, 0:C], ACT.Copy).then_inc(s["xf_copied"], 1)

            for g in range(-2, NG + 1):
                late, now, next_ = g - 1 in ALL, g in ALL, g + 1 in ALL
                if next_:
                    tanh(*row(g + 1), 0)
                if late:
                    v_rows(*row(g - 1))
                if next_:
                    for j in range(1, GT):
                        tanh(*row(g + 1), j)
                if late:
                    route_rows(*row(g - 1))
                if next_:
                    exp(*row(g + 1), 0)
                if late:
                    turned(*row(g - 1), 1)
                    copy_twin(*row(g - 1))
                if next_:
                    for j in range(1, GT):
                        exp(*row(g + 1), j)
                if now:
                    widen_inverse(*row(g))
                    copy_inverse(*row(g))
                if g + 2 in ALL:
                    z_rows(*row(g + 2))
                if late:
                    gap_exp(*row(g - 1), 1)
            experts(1)

        @block.vector
        def _(eng):
            seed(eng, "var_a", "xn_ready", "q_negs", "k_negs", "q_done", "k_done", "kv_ready", "att_ready",
                 "x_attended", "var_r", "xf_ready", "hits_ready", "gap_ready", "scatter_ready", "routed",
                 "xbT_low", "hid_ready", "y_copied", "combined", "var_z", "ci_ready", "gated_ready",
                 "max_ready", "prod_ready", "inv_ready", "conv_ready", "var_v")

            class Chain:

                def __init__(self, base):
                    self.base, self.n = base, 0

                def __call__(self, ins, apart=False):
                    self.n += 1
                    ins.then_inc(s["chain"], 1)
                    (wait_alone if apart else wait)(eng, s["chain"], self.base + self.n)

            def conv_consts(chain, step):
                if step < 4:
                    part = inv_count[:, T // 4 * step:T // 4 * (step + 1)]
                    chain(eng.reciprocal(part, part))
                if step == 4:
                    chain(eng.tensor_reduce(mod_head[:, :], ident[:, :].rearrange("p (k h) -> p h k", h=H),
                                            AX.X, ALU.add))
                    for n in range(2):
                        chain(eng.tensor_copy(pick[:, n, H * n:H * (n + 1)], mod_head[:, :]))
                if step == 5:
                    eng.wait_ge(s["w_conv"], 16 * 7)
                    chain(eng.tensor_tensor(dyn_w[:, 0:K, :], over(wpe_sb[:, 0:K], 2, H),
                                            over(same_head[:, :], 1, K), ALU.mult))
                    chain(eng.tensor_tensor(gate_w[:, 0:K, :], over(wpe_sb[:, K:2 * K], 2, H),
                                            over(same_head[:, :], 1, K), ALU.mult))
                if step == 6:
                    chain(eng.tensor_scalar(dyn_w[:, :, :], dyn_w[:, :, :], 0.5, None, ALU.mult))
                    chain(eng.tensor_scalar(bpe_sb[:, 0, :, :], bpe_sb[:, 0, :, :], 0.5, None, ALU.mult))
                if step > 6:
                    at = 32 * (step - 7)
                    chain(eng.tensor_copy(bpe_hi[:, :, :, :], bpe_sb[:, :, :, :]))
                    chain(eng.tensor_copy(bpe_parts[at:at + 1, :, :, :], bpe_hi[at:at + 1, :, :, :]))
                    chain(eng.tensor_tensor(bpe_sb[:, :, :, :], bpe_sb[:, :, :, :], bpe_hi[:, :, :, :], ALU.subtract))
                if step == 9:
                    eng.memset(hits_before[0][:, :], 0.0).then_inc(s["consts"], 1)
                    eng.wait_ge(s["consts"], 1)

            def moments(chain, norm, tile_at, scale, eps):
                for j in range(GT):
                    ins = eng.bn_stats(stats[norm][:, j, :], tile_at(j))
                chain(ins, apart=True)
                for j in range(GT):
                    ins = eng.bn_aggr(mv[norm][:, j, :], stats[norm][:, j, :])
                chain(ins)
                eng.tensor_scalar(neg_mean[norm][:, :], mv[norm][:, :, 0], -1.0, None, ALU.mult)
                eng.tensor_scalar(var_eps[norm][:, :], mv[norm][:, :, 1], scale, eps, ALU.mult, ALU.add)\
                   .then_inc(s[f"var_{norm}"], 1)

            def center(norm, to, tile_at):
                for j in range(GT):
                    ins = eng.tensor_scalar(to[:, j, 0:C], tile_at(j), mv[norm][:, j, 0:1], rstd[norm][:, j:j + 1],
                                            ALU.subtract, ALU.mult)
                return ins

            def key_moments(chain, i, q):
                if q == 0:
                    wait_alone(eng, s["x_in"], i * 16 + 16)
                moments(chain, "a", lambda j: tile_of(X, i, q, j), 1.0, LN_EPS)

            def key_rows(i, q):
                eng.wait_ge(s["rstd_a"], grp(i, q))
                eng.wait_ge(s["xnT_ready"], grp(i, q) - 2)
                center("a", xn[q % 2], lambda j: tile_of(X, i, q, j)).then_inc(s["xn_ready"], 1)

            def negatives(i, q):
                at = 4 * (q % 2)
                eng.wait_ge(s["q_ready"], grp(i, q))
                eng.wait_ge(s["q_exps"], grp(i, q) - 1)
                eng.tensor_scalar(q_neg[:, :], bank[at][:, :], 0.0, None, ALU.min).then_inc(s["q_negs"], 1)
                eng.wait_ge(s["k_ready"], grp(i, q))
                eng.wait_ge(s["k_exps"], grp(i, q) - 1)
                eng.tensor_scalar(k_neg[:, :], bank[at + 1][:, :], 0.0, None, ALU.min).then_inc(s["k_negs"], 1)

            def phis(i, q):
                at = 4 * (q % 2)
                eng.wait_ge(s["q_exps"], grp(i, q))
                eng.wait_ge(s["on_ready"], grp(i, q) - GPB)
                eng.scalar_tensor_tensor(q_phi[:, q, :], bank[at][:, :], 0.0, q_exp[:, :], ALU.max, ALU.add)\
                   .then_inc(s["q_done"], 1)
                eng.wait_ge(s["k_exps"], grp(i, q))
                eng.wait_ge(s["kv_added"], grp(i, q) - 2)
                eng.scalar_tensor_tensor(k_phi[q % 2][:, :], bank[at + 1][:, :], 0.0, k_exp[:, :], ALU.max, ALU.add)\
                   .then_inc(s["k_done"], 1)

            def states(i):
                eng.wait_ge(s["kv_added"], grp(i, GPB - 1))
                eng.wait_ge(s["on_ready"], grp(i, GPB - 1) - GPB)
                eng.tensor_tensor(kv[:, :, :], bank[3][:, 0:C].rearrange("p (h m) -> p h m", m=D),
                                  over(same_head[:, :], 2, D), ALU.mult)
                eng.tensor_scalar(k_sum[:, :], same_head[:, :], bank[3][:, C:C + 1], None,
                                  ALU.mult).then_inc(s["kv_ready"], 1)

            def normalize(chain, i, q):
                p = q % 2
                eng.wait_ge(s["on_ready"], grp(i, q))
                chain(eng.tensor_scalar(norm_r[p][:, :, :],
                                        bank[5 - 4 * p][:, 0:GT * H].rearrange("p (j h) -> p j h", h=H),
                                        ATT_EPS, None, ALU.add))
                chain(eng.reciprocal(norm_r[p][:, :, :], norm_r[p][:, :, :]))
                eng.wait_ge(s["attT_ready"], grp(i, q) - 2)
                eng.tensor_tensor(att[p][:, :, :].rearrange("p j (h m) -> p (j h) m", m=D),
                                  bank[4 - 4 * p][:, :].rearrange("p (a m) -> p a m", m=D),
                                  over(norm_r[p][:, :, :].rearrange("p j h -> p (j h)"), 2, D),
                                  ALU.mult).then_inc(s["att_ready"], 1)

            def attend(i, q):
                eng.wait_ge(s["proj_ready"], grp(i, q))
                xg = tiles_of(X, i, q)
                eng.tensor_tensor(xg, bank[6 - 4 * (q % 2)][:, :].rearrange("p (j c) -> p j c", c=C), xg,
                                  ALU.add).then_inc(s["x_attended"], 1)
                wait_alone(eng, s["x_attended"], grp(i, q))

            def route_moments(chain, i, q, r):
                moments(chain, "r", lambda j: tile_of(X, i, q, j), 1.0 + LN_EPS, LN_EPS * LN_EPS)

            def route_rows(i, q):
                p, r = q % 2, 0
                eng.wait_ge(s["rstd_r"], grp(i, q, r))
                if q >= 2:
                    eng.wait_ge(scattered[p], rows_moved(i, q - 2, r))
                eng.wait_ge(s["xfT_ready"], grp(i, q, r) - 2)
                center("r", xf[p], lambda j: tile_of(X, i, q, j)).then_inc(s["xf_ready"], 1)

            def choose(chain, i, q, r):
                p, bk = q % 2, route_bank(r)
                eng.wait_ge(s["logits_ready"], grp(i, q, r))
                chain(eng.tensor_scalar(logits[:, :, :], bk[:, 0:GT * E].rearrange("p (j e) -> p j e", e=E),
                                        -CLAMP, CLAMP, ALU.max, ALU.min), apart=True)
                for j in range(GT):
                    ins = eng.max(top[:, j, :], logits[:, j, :])
                chain(ins, apart=True)
                for j in range(GT):
                    ins = eng.max_index(top_i[:, j, :], top[:, j, :], logits[:, j, :])
                eng.wait_ge(s["gap_exp"], grp(i, q, r) - 1)
                chain(ins)
                eng.tensor_tensor(gap[:, :], top[:, :, 1], top[:, :, 0], ALU.subtract).then_inc(s["gap_ready"], 1)
                chain(eng.tensor_copy(expert[:, :, :], top_i[:, :, 0:TOPK]))
                chain(eng.tensor_tensor(onehot[:, :, :, :].rearrange("p j k e -> p (j k) e"),
                                        over(iota_e[:, :], 1, GT * TOPK),
                                        over(expert[:, :, :].rearrange("p j k -> p (j k)"), 2, E), ALU.is_equal))
                eng.wait_ge(s["pos_ready"], grp(i, q, r) - 1)
                eng.tensor_tensor(hits[p][:, :, :], onehot[:, :, 0, :], onehot[:, :, 1, :], ALU.add)\
                   .then_inc(s["hits_ready"], 1)
                eng.wait_ge(s["hits_ready"], grp(i, q, r))
                chain(eng.tensor_reduce(hit_sum[:, :], hits[p][:, :, :].rearrange("p j e -> p e j"), AX.X, ALU.add))
                chain(eng.tensor_tensor(hits_before[1 - p][:, :], hits_before[p][:, :], hit_sum[:, :], ALU.add))

            def place(chain, i, q, r):
                p, bk = q % 2, route_bank(r)
                eng.wait_ge(s["pos_ready"], grp(i, q, r))
                chain(eng.tensor_tensor(masked[:, :, :, :], onehot[:, :, :, :],
                                        over(bk[:, 0:GT * E].rearrange("p (j e) -> p j e", e=E), 2, TOPK), ALU.mult))
                chain(eng.tensor_reduce(pos[:, :, :], masked[:, :, :, :], AX.X, ALU.add))
                eng.tensor_scalar(kept[:, :, :], pos[:, :, :], float(CAP), None, ALU.is_lt)
                eng.tensor_scalar(far[:, :, :], pos[:, :, :], float(CAP), FAR, ALU.is_ge, ALU.mult)
                chain(eng.scalar_tensor_tensor(slot[:, :, :], expert[:, :, :], float(CAP), pos[:, :, :],
                                               ALU.mult, ALU.add))
                chain(eng.tensor_tensor(slot[:, :, :], slot[:, :, :], far[:, :, :], ALU.add))
                eng.tensor_copy(scatter_at[p][:, :].rearrange("p (j k) -> p j k", k=TOPK), slot[:, :, :])\
                   .then_inc(s["scatter_ready"], 1)
                if r == 0:
                    chain(eng.tensor_scalar(tiles_of(gather_at, i, q), slot[:, :, :], float(SLOTS - 1), None, ALU.min))
                eng.wait_ge(s["gap_exp"], grp(i, q, r))
                chain(eng.tensor_scalar(den[:, :], e_gap[:, :], 1.0, 1e-12, ALU.add, ALU.add))
                chain(eng.reciprocal(prob[:, :, 0], den[:, :]))
                chain(eng.tensor_tensor(prob[:, :, 1], e_gap[:, :], prob[:, :, 0], ALU.mult))
                eng.tensor_tensor(tiles_of(route_w, i, q), prob[:, :, :], kept[:, :, :], ALU.mult)\
                   .then_inc(s["routed"], 1)

            def experts(r, once=None):
                def low_rows(i, n):
                    b, c, q = n // NC, n % NC, n % 2
                    eng.wait_ge(s["xbT_high"], chunk(i, b, c, r))
                    eng.wait_ge(s["u_ready"], unit(i, b, c, 1, r) - 4)
                    eng.tensor_tensor(xbT_parts[q][1][:, :], xbT[q][:, :], xbT_parts[q][0][:, :], ALU.subtract)\
                       .then_inc(s["xbT_low"], 1)

                def features(i, n, f):
                    b, c = n // NC, n % NC
                    eng.wait_ge(s["silu_ready"], unit(i, b, c, f, r))
                    eng.wait_ge(s["u_ready"], unit(i, b, c, f, r))
                    if f == 0:
                        eng.wait_ge(s["y_ready"], chunk(i, b, c, r) - 2)
                    eng.tensor_tensor(hid[n % 2][:, 2 * f:2 * f + 2, :], silu_g[f][:, :, :],
                                      bank[4 + f][:, :].rearrange("p (a n) -> p a n", a=2), ALU.mult)\
                       .then_inc(s["hid_ready"], 1)

                def copy_y(i, n, first=False):
                    b, c = n // NC, n % NC
                    eng.wait_ge(s["y_ready"], chunk(i, b, c, r))
                    if c == 0 and r == 0:
                        eng.wait_ge(yb_stored[b], by_pair(i, r, 1) - 16)
                    elif c == 0 and not first:
                        eng.wait_ge(sent[b], sent_by(i))
                    eng.tensor_copy(yb[b][:, CH * c:CH * (c + 1), :],
                                    bank[6 + n % 2][:, 0:CH * C].rearrange("p (t c) -> p t c", c=C))\
                       .then_inc(s["y_copied"], 1)

                def pair(i, first=False, last=False):
                    for n in range(2 * NC):
                        features(i, n, 0)
                        if n + 1 < 2 * NC:
                            low_rows(i, n + 1)
                        elif not last:
                            low_rows(i + 1, 0)
                        features(i, n, 1)
                        if n:
                            copy_y(i, n - 1, first)
                        elif not first:
                            copy_y(i - 1, 2 * NC - 1)
                        if first and r == 0:
                            conv_consts(once, n)
                low_rows(0, 0)
                pair(0, first=True)
                with eng.Fori(1, E // 2 - 1) as i:
                    pair(i)
                pair(E // 2 - 1, last=True)
                copy_y(E // 2 - 1, 2 * NC - 1)

            def combine(chain, i, q, r):
                p = q % 2
                chain(eng.tensor_copy(w_got[:, :, :], tiles_of(route_w, i, q)))
                if r == 0:
                    eng.wait_ge(gathered[p], rows_moved(i, q, r))
                else:
                    eng.wait_ge(y_back[p], half(i, q, 0, TOPK, 0))
                for k in range(TOPK):
                    for j in range(GT):
                        xt = tile_of(X, i, q, j)
                        at = TOPK * j + k if r == 0 else GT * k + j
                        ins = eng.scalar_tensor_tensor(xt, y_got[p][:, at, :], w_got[:, j, k:k + 1], xt,
                                                       ALU.mult, ALU.add)
                    if k == 0:
                        chain(ins)
                ins.then_inc(s["combined"], 1)
                wait_alone(eng, s["combined"], grp(i, q, r))

            once = Chain(0)
            eng.wait_ge(s["consts_pool"], 2)
            once(eng.tensor_reduce(same_head[:, :], ident[:, :].rearrange("p (h d) -> p h d", d=D), AX.X, ALU.add))
            n0 = once.n
            ATT, CMB = GPB * (2 + 2 + 17), GPB * 2
            with eng.Fori(0, B) as i:
                chain = Chain(i * ATT + n0)
                key_moments(chain, i, 0)
                key_rows(i, 0)
                key_moments(chain, i, 1)
                for q in GROUPS:
                    if q + 1 < GPB:
                        key_rows(i, q + 1)
                    negatives(i, q)
                    if q + 2 < GPB:
                        key_moments(chain, i, q + 2)
                    phis(i, q)
                states(i)
                normalize(chain, i, 0)
                normalize(chain, i, 1)
                attend(i, 0)
                route_moments(chain, i, 0, 0)
                for q in GROUPS:
                    route_rows(i, q)
                    if q + 2 < GPB:
                        normalize(chain, i, q + 2)
                    if q + 1 < GPB:
                        attend(i, q + 1)
                        route_moments(chain, i, q + 1, 0)
                    choose(chain, i, q, 0)
                    place(chain, i, q, 0)
                assert chain.n == ATT, chain.n
            n0 += B * ATT
            once = Chain(n0)
            experts(0, once)
            n0 += once.n

            def means(chain, i, q):
                p = q % 2
                eng.wait_ge(s["zT_ready"], grp(i, q))
                chain(eng.tensor_tensor_scan(cum[p][:, :], ones_f[:, :], bank[7][:, :],
                                             0.0 if q == 0 else cum[1 - p][:, GN - 1:GN], ALU.mult, ALU.add))
                eng.wait_ge(s["dyn_ready"], tile(i, q, GT - 1) - 2 * GT)
                eng.wait_ge(ci_stored[p], half(i, q, 0, 1) - 16)
                eng.tensor_tensor(ci[p][:, :], cum[p][:, :], inv_count[:, GN * q:GN * (q + 1)], ALU.mult)\
                   .then_inc(s["ci_ready"], 1)

            def gate(i, q, j):
                eng.wait_ge(s["tanh_ready"], tile(i, q, j))
                eng.wait_ge(s["dyn_ready"], tile(i, q, j))
                eng.wait_ge(s["energy_ready"], tile(i, q, j) - 2)
                eng.scalar_tensor_tensor(gated[j % 2][:, :, :], th[j % 2][:, :, :], 1.0,
                                         bank[2 + j % 2][:, :].rearrange("p (k h) -> p k h", h=H),
                                         ALU.add, ALU.mult).then_inc(s["gated_ready"], 1)

            def biggest(i, q, j):
                eng.wait_ge(s["energy_ready"], tile(i, q, j))
                eng.wait_ge(s["sub_ready"], tile(i, q, j) - 2)
                eng.tensor_reduce(e_max[j % 2][:, :], energy[j % 2][:, 0:K, :].rearrange("p k h -> p h k"),
                                  AX.X, ALU.max).then_inc(s["max_ready"], 1)

            def product(i, q, o):
                p, g, odd = q % 2, o // 2, o % 2
                if o == 0:
                    eng.wait_ge(taps_loaded[p], half(i, q, 0, 8))
                    eng.wait_ge(s["exp_ready"], tile(i, q, GT - 1))
                eng.wait_ge(s["prod_added"], eighth(i, q, o) - 2)
                eng.tensor_tensor(prod[odd][:, :, :], taps[p][:, odd:D:2, 8 * g:8 * g + GN],
                                  over(eT[p][:, g, :], 1, 4), ALU.mult).then_inc(s["prod_ready"], 1)

            def invert(i, q):
                eng.wait_ge(s["norm_ready"], grp(i, q))
                eng.reciprocal(w_inv[:, :, :], bank[7][:, 0:GT * H].rearrange("p (j h) -> p j h", h=H))\
                   .then_inc(s["inv_ready"], 1)

            def divide(i, q):
                eng.wait_ge(s["prod_added"], eighth(i, q, 7))
                eng.wait_ge(s["inv_copied"], grp(i, q))
                eng.wait_ge(s["v_out"], grp(i, q) - 1)
                eng.tensor_tensor(convT[:, :], bank[5][:, :], z_inv[:, :], ALU.mult).then_inc(s["conv_ready"], 1)

            def v_moments(chain, i, q):
                eng.wait_ge(s["v_out"], grp(i, q))
                moments(chain, "v", lambda j: bank[6][:, C * j:C * (j + 1)], 1.0, CONV_EPS)

            def v_rows(chain, i, q):
                eng.wait_ge(s["v_normed"], grp(i, q))
                chain(eng.tensor_tensor(v_hat[:, :, :], v_hat[:, :, :], over(gammaB_sb[:, :], 1, GT), ALU.mult))
                eng.wait_ge(s["x_shifted"], grp(i, q))
                xg = tiles_of(X, i, q)
                chain(eng.tensor_tensor(xg, xg, v_hat[:, :, :], ALU.add), apart=True)

            chain = Chain(n0)
            for g in range(-2, NG + 1):
                late, now, next_, ahead = g - 1 in ALL, g in ALL, g + 1 in ALL, g + 2 in ALL
                at_x = lambda n: (lambda j: tile_of(X, *row(n), j))
                if now:
                    product(*row(g), 0)
                if late:
                    divide(*row(g - 1))
                if next_:
                    means(chain, *row(g + 1))
                if now:
                    product(*row(g), 1)
                if late:
                    v_moments(chain, *row(g - 1))
                if next_:
                    gate(*row(g + 1), 0)
                if now:
                    product(*row(g), 2)
                if late:
                    v_rows(chain, *row(g - 1))
                    route_moments(chain, *row(g - 1), 1)
                if next_:
                    gate(*row(g + 1), 1)
                    biggest(*row(g + 1), 0)
                if now:
                    product(*row(g), 3)
                if next_:
                    gate(*row(g + 1), 2)
                    biggest(*row(g + 1), 1)
                if now:
                    product(*row(g), 4)
                if next_:
                    gate(*row(g + 1), 3)
                    biggest(*row(g + 1), 2)
                if now:
                    product(*row(g), 5)
                if next_:
                    biggest(*row(g + 1), 3)
                if now:
                    invert(*row(g))
                if ahead:
                    combine(chain, *row(g + 2), 0)
                    moments(chain, "z", at_x(g + 2), 1.0, LN_EPS)
                if now:
                    product(*row(g), 6)
                if late:
                    choose(chain, *row(g - 1), 1)
                if now:
                    product(*row(g), 7)
                if late:
                    place(chain, *row(g - 1), 1)
            n0 += chain.n
            experts(1)
            with eng.Fori(0, B) as i:
                chain = Chain(i * CMB + n0)
                for q in range(GPB):
                    combine(chain, i, q, 1)
                assert chain.n == CMB, chain.n

        @block.tensor
        def _(eng):
            seed(eng, "xnT_ready", "q_ready", "k_ready", "v_ready", "kv_added", "on_ready", "proj_ready",
                 "xfT_ready", "logits_ready", "pos_ready", "xbT_ready", "g_ready", "u_ready", "y_ready",
                 "zT_ready", "gate_ready", "dyn_ready", "eT_ready", "prod_added", "norm_ready", "v_out",
                 "attT_ready", "inv_spread")
            eng.wait_ge(s["consts_pool"], 2)
            eng.wait_ge(s["w_att"], 16 * 6)

            def turn_x(i, q):
                eng.wait_ge(s["xn_ready"], grp(i, q))
                eng.wait_ge(s["xnT_copied"], grp(i, q) - 1)
                for j in range(GT):
                    mm = eng.transpose(bank[7][:, P * j:P * (j + 1)], xn[q % 2][:, j, :], ident[:, :])
                mm.then_inc(s["xnT_ready"], 1)

            def keys(i, q):
                p, at = q % 2, 4 * (q % 2)
                if q < 2:
                    eng.wait_ge(s["x_attended"], grp(i, 0) - 1)
                eng.wait_ge(s["xnT_copied"], grp(i, q))
                eng.wait_ge(s["q_done"], grp(i, q) - 2)
                eng.matmul(bank[at][:, :], wqkv_sb[:, 0:C], xnT[p][:, :], start=True, stop=True)\
                   .then_inc(s["q_ready"], 1)
                eng.wait_ge(s["k_done"], grp(i, q) - 2)
                eng.wait_ge(s["v_copied"], grp(i, q) - 2)
                for n, name in ((1, "k_ready"), (2, "v_ready")):
                    for j in range(GT):
                        mm = eng.matmul(bank[at + n][:, C * j:C * (j + 1)], xnT[p][:, P * j:P * (j + 1)],
                                        wqkv_sb[:, C * n:C * (n + 1)], start=True, stop=True)
                    mm.then_inc(s[name], 1)

            def add_kv(i, q):
                p = q % 2
                eng.wait_ge(s["k_done"], grp(i, q))
                eng.wait_ge(s["v_copied"], grp(i, q))
                if q == 0:
                    eng.wait_ge(s["routed"], grp(i, 0) - 1)
                for j in range(GT):
                    mm = eng.matmul(bank[3][:, 0:C + 1], k_phi[p][:, P * j:P * (j + 1)], v_one[p][:, j, :],
                                    start=(q == 0 and j == 0), stop=(q == GPB - 1 and j == GT - 1))
                mm.then_inc(s["kv_added"], 1)

            def query(i, q):
                p = q % 2
                if q == 0:
                    eng.wait_ge(s["kv_ready"], i + (1 + SEED))
                eng.wait_ge(s["att_ready"], grp(i, q) - 2)
                eng.wait_ge(s["attT_copied"], grp(i, q) - 2)
                for j in range(GT):
                    rows = q_phi[:, q, P * j:P * (j + 1)]
                    eng.matmul(bank[4 - 4 * p][:, C * j:C * (j + 1)], rows, kv[:, :, :].rearrange("p h m -> p (h m)"),
                               start=True, stop=True)
                    mm = eng.matmul(bank[5 - 4 * p][:, H * j:H * (j + 1)], rows, k_sum[:, :], start=True, stop=True)
                mm.then_inc(s["on_ready"], 1)

            def turn_att(i, q):
                p = q % 2
                eng.wait_ge(s["att_ready"], grp(i, q))
                for j in range(GT):
                    mm = eng.transpose(bank[5 - 4 * p][:, P * j:P * (j + 1)], att[p][:, j, :], ident[:, :])
                mm.then_inc(s["attT_ready"], 1)

            def project_att(i, q):
                p = q % 2
                eng.wait_ge(s["attT_copied"], grp(i, q))
                eng.wait_ge(s["x_attended"], grp(i, q) - 2)
                for j in range(GT):
                    to = bank[6 - 4 * p][:, C * j:C * (j + 1)]
                    eng.matmul(to, attT[p][:, P * j:P * (j + 1)], wproj_sb[:, :], start=True, stop=False)
                    mm = eng.matmul(to, ones_f[0:1, 0:P], bproj_sb[0:1, :], start=False, stop=True)
                mm.then_inc(s["proj_ready"], 1)

            def turn_rows(i, q, r):
                p, bk = q % 2, route_bank(r)
                eng.wait_ge(s["xf_ready"], grp(i, q, r))
                eng.wait_ge(s["routed"], grp(i, q, r) - 1)
                for j in range(GT):
                    mm = eng.transpose(bk[:, P * j:P * (j + 1)], xf[p][:, j, 0:C], ident[:, :])
                mm.then_inc(s["xfT_ready"], 1)

            def router(i, q, r):
                p, bk = q % 2, route_bank(r)
                eng.wait_ge(s["xfT_copied"], grp(i, q, r))
                for j in range(GT):
                    mm = eng.matmul(bk[:, E * j:E * (j + 1)], xfT[p][:, P * j:P * (j + 1)], router_sb[:, :],
                                    start=True, stop=True)
                mm.then_inc(s["logits_ready"], 1)

            def count(i, q, r):
                p, bk = q % 2, route_bank(r)
                eng.wait_ge(s["hits_ready"], grp(i, q, r))
                rows = hits[p][:, :, :].rearrange("p j e -> p (j e)")
                eng.matmul(bk[:, 0:GT * E], before[:, :], rows, start=True, stop=False, skip_group_check=True)
                for n in range(1, GT):
                    eng.matmul(bk[:, n * E:GT * E], ones[:, 0:P], rows[:, 0:(GT - n) * E],
                               start=False, stop=False, skip_group_check=True)
                eng.matmul(bk[:, 0:GT * E].rearrange("p (j e) -> p j e", e=E), ones[:, 0:P],
                           over(hits_before[p][:, :], 1, GT), start=False, stop=True,
                           skip_group_check=True).then_inc(s["pos_ready"], 1)

            def experts(r):
                def turn(i, n):
                    b, c, q = n // NC, n % NC, n % 2
                    if c == 0:
                        eng.wait_ge(xb_loaded[b], by_pair(i, r, 1))
                    eng.wait_ge(s["xbT_copied"], chunk(i, b, c, r) - 2)
                    for t in range(CH):
                        mm = eng.transpose(bank[q][:, P * t:P * (t + 1)], xb[b][:, CH * c + t, 0:C], ident[:, :])
                    mm.then_inc(s["xbT_ready"], 1)

                def product(to, ws, xs):
                    eng.matmul(to, ws[1], xs[0], start=True, stop=False)
                    eng.matmul(to, ws[0], xs[1], start=False, stop=False)
                    return eng.matmul(to, ws[0], xs[0], start=False, stop=True)

                def up(i, n, f):
                    b, c, q = n // NC, n % NC, n % 2
                    if f == 0:
                        eng.wait_ge(s["xbT_low"], chunk(i, b, c, r))
                        if c == 0:
                            eng.wait_ge(s["w_split"], split(i, b, r))
                    eng.wait_ge(s["hid_ready"], unit(i, b, c, f, r) - 2)
                    for half_of, at, name in ((0, 2, "g_ready"), (1, 4, "u_ready")):
                        for a in range(2):
                            col = F * half_of + P * (2 * f + a)
                            mm = product(bank[at + f][:, CH * P * a:CH * P * (a + 1)],
                                         [t[:, col:col + P] for t in w12_parts[b]], [t[:, :] for t in xbT_parts[q]])
                        mm.then_inc(s[name], 1)

                def down(i, n):
                    b, c, q = n // NC, n % NC, n % 2
                    eng.wait_ge(s["hid_ready"], unit(i, b, c, 1, r))
                    eng.wait_ge(s["y_copied"], chunk(i, b, c, r) - 2)
                    for t in range(CH):
                        for a in range(FT):
                            mm = eng.matmul(bank[6 + q][:, C * t:C * (t + 1)], hid[q][:, a, P * t:P * (t + 1)],
                                            w3_sb[b][:, a, :], start=(a == 0), stop=(a == FT - 1))
                    mm.then_inc(s["y_ready"], 1)

                def pair(i, first=False, last=False):
                    for n in range(2 * NC):
                        up(i, n, 0)
                        if n + 1 < 2 * NC:
                            turn(i, n + 1)
                        elif not last:
                            turn(i + 1, 0)
                        up(i, n, 1)
                        if n:
                            down(i, n - 1)
                        elif not first:
                            down(i - 1, 2 * NC - 1)
                turn(0, 0)
                pair(0, first=True)
                with eng.Fori(1, E // 2 - 1) as i:
                    pair(i)
                pair(E // 2 - 1, last=True)
                down(E // 2 - 1, 2 * NC - 1)

            with eng.Fori(0, B) as i:
                turn_x(i, 0)
                for q in GROUPS:
                    keys(i, q)
                    if q + 1 < GPB:
                        turn_x(i, q + 1)
                    if q:
                        add_kv(i, q - 1)
                add_kv(i, GPB - 1)
                query(i, 0)
                query(i, 1)
                turn_att(i, 0)
                turn_att(i, 1)
                project_att(i, 0)
                for q in GROUPS:
                    if q + 1 < GPB:
                        project_att(i, q + 1)
                    if q + 2 < GPB:
                        query(i, q + 2)
                    turn_rows(i, q, 0)
                    if q + 2 < GPB:
                        turn_att(i, q + 2)
                    router(i, q, 0)
                    count(i, q, 0)
            experts(0)
            eng.wait_ge(s["consts"], 1)

            def turn_z(i, q):
                eng.wait_ge(s["inv_copied"], grp(i, q) - 2)
                eng.wait_ge(s["z_ready"], grp(i, q))
                eng.wait_ge(s["ci_ready"], grp(i, q) - 1)
                for j in range(GT):
                    mm = eng.transpose(bank[7][:, P * j:P * (j + 1)], z[(i * GPB + q) % 3][:, j, :], ident[:, :])
                mm.then_inc(s["zT_ready"], 1)

            def logit(i, q, j):
                if j == 0:
                    eng.wait_ge(s["ci_ready"], grp(i, q))
                eng.wait_ge(s["tanh_ready"], tile(i, q, j) - 2)
                eng.wait_ge(s["gated_ready"], tile(i, q, j) - 2)
                for at, w, part, name in ((0, gate_w, 1, "gate_ready"), (2, dyn_w, 0, "dyn_ready")):
                    bk = bank[at + j % 2][:, :]
                    eng.matmul(bk, ci[q % 2][:, P * j:P * (j + 1)], w[:, :, :].rearrange("p k h -> p (k h)"),
                               start=True, stop=False)
                    eng.matmul(bk, ones[:, 0:P], bpe_parts[:, part, :, :].rearrange("p k h -> p (k h)"),
                               start=False, stop=True).then_inc(s[name], 1)

            def turn_e(i, q, j):
                eng.wait_ge(s["sub_ready"], tile(i, q, j))
                eng.wait_ge(s["exp_ready"], tile(i, q, j) - 1)
                rows = e_sub[j % 2][:, :, :].rearrange("p k h -> p (k h)")
                for g in range(4):
                    mm = eng.transpose(bank[4][:, P * g:P * (g + 1)], rows[:, P * g:P * (g + 1)], ident[:, :])
                mm.then_inc(s["eT_ready"], 1)

            def weigh(i, q):
                eng.wait_ge(s["exp_ready"], tile(i, q, GT - 1))
                eng.wait_ge(s["ci_ready"], min(grp(i, q) + 1, grp(B - 1, GPB - 1)))
                for j in range(GT):
                    for g in range(4):
                        mm = eng.matmul(bank[7][:, H * j:H * (j + 1)], eT[q % 2][:, g, P * j:P * (j + 1)],
                                        mod_head[:, :], start=(g == 0), stop=(g == 3))
                mm.then_inc(s["norm_ready"], 1)

            def spread(i, q):
                eng.wait_ge(s["inv_widened"], grp(i, q))
                for j in range(GT):
                    mm = eng.transpose(bank[7][:, P * j:P * (j + 1)],
                                       inv_wide[:, j, :, :].rearrange("p d h -> p (d h)"), ident[:, :])
                mm.then_inc(s["inv_spread"], 1)

            def add(i, q, o):
                if o == 0:
                    eng.wait_ge(s["conv_ready"], grp(i, q) - 1)
                eng.wait_ge(s["prod_ready"], eighth(i, q, o))
                for n in range(4):
                    mm = eng.matmul(bank[5][32 * n:32 * (n + 1), :], pick[:, o % 2, :], prod[o % 2][:, n, :],
                                    start=(o == 0), stop=(o == 7))
                mm.then_inc(s["prod_added"], 1)

            def project(i, q):
                eng.wait_ge(s["routed"], grp(i, q, 1) - 1)
                eng.matmul(bank[6][:, :], ident[:, :], z[(i * GPB + q) % 3][:, :, :].rearrange("p j c -> p (j c)"),
                           start=True, stop=False, skip_group_check=True)
                eng.wait_ge(s["conv_ready"], grp(i, q))
                for j in range(GT):
                    mm = eng.matmul(bank[6][:, C * j:C * (j + 1)], convT[:, P * j:P * (j + 1)], wfc_sb[:, :],
                                    start=False, stop=True, skip_group_check=True)
                mm.then_inc(s["v_out"], 1)

            for g in range(-2, NG + 1):
                late, now, next_ = g - 1 in ALL, g in ALL, g + 1 in ALL
                if late:
                    project(*row(g - 1))
                if next_:
                    logit(*row(g + 1), 0)
                if now:
                    add(*row(g), 0)
                if next_:
                    logit(*row(g + 1), 1)
                if now:
                    add(*row(g), 1)
                if next_:
                    logit(*row(g + 1), 2)
                if now:
                    add(*row(g), 2)
                if next_:
                    logit(*row(g + 1), 3)
                if now:
                    weigh(*row(g))
                if now:
                    add(*row(g), 3)
                if next_:
                    turn_e(*row(g + 1), 0)
                if late:
                    turn_rows(*row(g - 1), 1)
                if next_:
                    turn_e(*row(g + 1), 1)
                if late:
                    router(*row(g - 1), 1)
                if now:
                    add(*row(g), 4)
                if next_:
                    turn_e(*row(g + 1), 2)
                if now:
                    add(*row(g), 5)
                if next_:
                    turn_e(*row(g + 1), 3)
                if now:
                    spread(*row(g))
                    add(*row(g), 6)
                if g + 2 in ALL:
                    turn_z(*row(g + 2))
                if late:
                    count(*row(g - 1), 1)
                if now:
                    add(*row(g), 7)
            experts(1)


def kernel(**inputs):
    import numpy as np
    import concourse.bacc as bacc
    from concourse import mybir as mb
    from concourse.bass_utils import run_bass_kernel_spmd

    a = {n.removeprefix("L0_"): np.asarray(v) for n, v in inputs.items()}
    H, D, K = 16, 8, 31
    E, F2, C = a["ffn_w12"].shape
    rows = lambda v: np.broadcast_to(v.reshape(1, -1), (P, v.size))
    by_head = lambda v: np.repeat(v.reshape(-1, K)[:, :, None], H, axis=2).reshape(-1, K * H)
    bpe = by_head(a["attn_b_b_pe"])
    arrays = {
        "x": a["attn_a_x"],
        "wqkvT": a["attn_a_Wqkv"].T,
        "wprojT": a["attn_a_Wproj"].T,
        "bproj": rows(a["attn_a_bproj"]),
        "wpe": np.tile(a["attn_b_W_pe"], (H, 1)),
        "bpe": np.broadcast_to(bpe[None], (P, 2, K * H)),
        "stt": rows(a["attn_b_stt_energy"].reshape(H, K).T),
        "wfcT": a["attn_b_W_fc"].T.reshape(H, D, C).transpose(1, 0, 2).reshape(C, C),
        "gammaB": rows(a["attn_b_gamma"]),
        "betaB": rows(a["attn_b_beta"]),
        "gammaF": a["ffn_ln_gamma"].reshape(-1, 1),
        "betaF": a["ffn_ln_beta"].reshape(-1, 1),
        "routerT": a["ffn_router_w"].T,
        "w12T": a["ffn_w12"].transpose(0, 2, 1),
        "w3T": a["ffn_w3"].transpose(0, 2, 1).reshape(E, F2 // 2 // P, P, C).transpose(0, 2, 1, 3),
    }
    arrays = {n: np.ascontiguousarray(v) for n, v in arrays.items()}
    nc = bacc.Bacc("TRN2", target_bir_lowering=False, num_devices=1)
    args = [nc.dram_tensor(n, v.shape, mb.dt.from_np(v.dtype), kind="ExternalInput").ap() for n, v in arrays.items()]
    out = nc.dram_tensor("out", a["attn_a_x"].shape, mb.dt.from_np(np.dtype("float32")), kind="ExternalOutput").ap()
    hybrid_block(nc, *args, out)
    r = run_bass_kernel_spmd(nc, [arrays], core_ids=[0])
    return r.results[0]["out"]
```
